# Optimizing a Trainium2 kernel written in Bass

```python
import numpy as np
import jax
import jax.numpy as jnp

def _softmax(x, axis=-1):
    return jax.nn.softmax(x, axis=axis)

def _gelu(x):
    return jax.nn.gelu(x, approximate=True)

def _silu(x):
    return jax.nn.silu(x)

def _sigmoid(x):
    return jax.nn.sigmoid(x)

def _layernorm(x, axis=-1, eps=1e-05):
    m = jnp.mean(x, axis=axis, keepdims=True)
    v = jnp.var(x, axis=axis, keepdims=True)
    return (x - m) / jnp.sqrt(v + eps)

def _scatter_add(tgt, idx, src, axis=0):
    return tgt.at[idx].add(src)

def _segment_sum(src, seg, n):
    return jax.ops.segment_sum(src, seg, n)
kernel_name = 'mk_decoder_preln_d2_seqx_r8_9b6d20'

def setup_inputs(seed: int=0):
    np.random.seed(seed)
    _w = jnp.asarray

    def _rec_inputs():
        import jax
        import jax.numpy as jnp
        _rk = jax.random.key(seed)
        x = 7.22e-05 + 1 * jax.random.normal(jax.random.fold_in(_rk, 1), (16, 128, 128), jnp.float32)
        _lenS = 128 - jax.random.randint(jax.random.fold_in(_rk, 7), (16,), 0, max(1, 128 // 4) + 1, jnp.int32)
        _lenS2 = 77 - jax.random.randint(jax.random.fold_in(_rk, 8), (16,), 0, max(1, 77 // 4) + 1, jnp.int32)
        _ctx_1024P = jax.random.normal(jax.random.fold_in(_rk, 11), (16, 16, 128), jnp.float32)
        _ctx_1024c = jax.random.dirichlet(jax.random.fold_in(_rk, 511), 0.3 * jnp.ones((16,), jnp.float32), (16, 77))
        _ctx_1024t = jnp.einsum('bsk,bkd->bsd', _ctx_1024c, _ctx_1024P)
        _ctx_1024t = _ctx_1024t * jax.lax.rsqrt(jnp.mean(jnp.square(_ctx_1024t)) + 1e-12) * 0.953939
        ctx_1024 = 4.13588e-05 + 0.999923 * (_ctx_1024t + 0.3 * jax.random.normal(jax.random.fold_in(_rk, 611), (16, 77, 128), jnp.float32))
        _validS = jnp.arange(128)[None, :] < _lenS[:, None]
        _validS2 = jnp.arange(77)[None, :] < _lenS2[:, None]
        _causal = jnp.tril(jnp.ones((128, 128), dtype=bool))
        mask_SxS2_bk1 = jnp.broadcast_to(_validS2[0:1, :], (128, 77))
        return (x, ctx_1024, mask_SxS2_bk1)
    x, ctx_1024, mask_SxS2_bk1 = _rec_inputs()

    def _L0_attn_setup():
        import jax, jax.numpy as jnp
        import numpy as np
        NUM_HEADS = 16
        THETA = 10000.0

        def _rotate_half(x):
            x = x.reshape(x.shape[:-1] + (-1, 2))
            x1, x2 = (x[..., 0], x[..., 1])
            return jnp.stack((-x2, x1), axis=-1).reshape(x.shape[:-2] + (-1,))

        def _rope(x):
            d_k = x.shape[-1]
            seq_len = x.shape[-2]
            inv_freq = 1.0 / THETA ** (jnp.arange(0, d_k, 2, dtype=jnp.float32) / d_k)
            pos = jnp.arange(seq_len, dtype=jnp.float32)
            theta = pos[:, None] * inv_freq[None, :]
            cos = jnp.repeat(jnp.cos(theta), 2, axis=-1)
            sin = jnp.repeat(jnp.sin(theta), 2, axis=-1)
            return x * cos + _rotate_half(x) * sin
        key = jax.random.key(seed)
        kx, kq, kk, kv, ko = jax.random.split(key, 5)
        B, S, D = (2, 256, 128)
        std = 1.0 / (2.0 * (2 * D) ** 0.5)
        return {'x': jax.random.normal(kx, (B, S, D), dtype=jnp.float32), 'Wq': jax.random.normal(kq, (D, D), dtype=jnp.float32) * std, 'Wk': jax.random.normal(kk, (D, D), dtype=jnp.float32) * std, 'Wv': jax.random.normal(kv, (D, D), dtype=jnp.float32) * std, 'Wo': jax.random.normal(ko, (D, D), dtype=jnp.float32) * std}
    _L0_attn_all = _L0_attn_setup()
    _L0_attn_in = {k: v for k, v in _L0_attn_all.items() if k in ('Wq', 'Wk', 'Wv', 'Wo')}
    del _L0_attn_all

    def _L0_xattn_setup():
        import jax, jax.numpy as jnp
        import numpy as np
        D = 128
        H = 16
        HD = 64
        B, S = (4, 256)
        NEG = -1000000000.0
        key = jax.random.key(seed)
        k1, k2, k3, k4, k5, k6, k7 = jax.random.split(key, 7)
        xq = jax.random.normal(k1, (B, S, D), dtype=jnp.float32)
        xk = jax.random.normal(k2, (B, S, D), dtype=jnp.float32)
        xv = jax.random.normal(k3, (B, S, D), dtype=jnp.float32)
        mask = jnp.triu(jnp.ones((S, S), dtype=jnp.bool_), k=1)
        sc = 1.0 / np.sqrt(D)
        W_q = jax.random.normal(k4, (D, H * HD), dtype=jnp.float32) * sc
        W_k = jax.random.normal(k5, (D, H * HD), dtype=jnp.float32) * sc
        W_v = jax.random.normal(k6, (D, H * HD), dtype=jnp.float32) * sc
        W_o = jax.random.normal(k7, (H * HD, D), dtype=jnp.float32) * sc
        return {'xq': xq, 'xk': xk, 'xv': xv, 'mask': mask, 'W_q': W_q, 'W_k': W_k, 'W_v': W_v, 'W_o': W_o}
    _L0_xattn_all = _L0_xattn_setup()
    _L0_xattn_in = {k: v for k, v in _L0_xattn_all.items() if k in ('W_q', 'W_k', 'W_v', 'W_o')}
    del _L0_xattn_all

    def _L0_ffn_setup():
        import jax, jax.numpy as jnp
        import numpy as np
        FP8_MAX = 448.0
        SCALE = 1.0
        _FP8_DTYPE = getattr(jnp, 'float8_e4m3fn', jnp.float16)

        def quantize_e4m3(t, scale):
            return jnp.clip(t / scale, -FP8_MAX, FP8_MAX).astype(_FP8_DTYPE)
        key = jax.random.key(seed)
        kx, kw = jax.random.split(key)
        B, N, C, F = (8, 512, 128, 128)
        x = jax.random.normal(kx, (B, N, C), dtype=jnp.float32)
        weight = jax.random.normal(kw, (F, C), dtype=jnp.float32) * 0.02
        bias = jnp.zeros((F,), dtype=jnp.float32)
        return {'x': x, 'weight': weight, 'bias': bias}
    _L0_ffn_all = _L0_ffn_setup()
    _L0_ffn_in = {k: v for k, v in _L0_ffn_all.items() if k in ('weight', 'bias')}
    del _L0_ffn_all

    def _L1_attn_setup():
        import jax, jax.numpy as jnp
        import numpy as np
        D_MODEL = 128
        B, S = (4, 512)

        def _linear_scan(x_scan, a):

            def combine(l, r):
                al, xl = l
                ar, xr = r
                return (al * ar, ar * xl + xr)
            _, h = jax.lax.associative_scan(combine, (a, x_scan), axis=1)
            return h
        key = jax.random.key(seed)
        ks = jax.random.split(key, 4)
        scale = 1.0 / np.sqrt(D_MODEL)
        return {'x': jax.random.normal(ks[0], (B, S, D_MODEL), dtype=jnp.float32), 'Wg': jax.random.normal(ks[1], (D_MODEL, D_MODEL), dtype=jnp.float32) * scale, 'bg': jnp.zeros((D_MODEL,), dtype=jnp.float32), 'Wv': jax.random.normal(ks[2], (D_MODEL, D_MODEL), dtype=jnp.float32) * scale, 'bv': jnp.zeros((D_MODEL,), dtype=jnp.float32), 'Wd': jax.random.normal(ks[3], (D_MODEL, D_MODEL), dtype=jnp.float32) * scale, 'bd': jnp.ones((D_MODEL,), dtype=jnp.float32)}
    _L1_attn_all = _L1_attn_setup()
    _L1_attn_in = {k: v for k, v in _L1_attn_all.items() if k in ('Wg', 'bg', 'Wv', 'bv', 'Wd', 'bd')}
    del _L1_attn_all

    def _L1_xattn_setup():
        import jax, jax.numpy as jnp
        import numpy as np
        D_MODEL = 128
        N_HEADS = 16
        HEAD_DIM = D_MODEL // N_HEADS
        SCALE = HEAD_DIM ** (-0.5)
        key = jax.random.key(seed)
        ks = jax.random.split(key, 11)
        B, L = (4, 256)
        s = 1.0 / np.sqrt(D_MODEL)
        inp = {'queries': jax.random.normal(ks[0], (B, L, D_MODEL), jnp.float32), 'keys': jax.random.normal(ks[1], (B, L, D_MODEL), jnp.float32), 'values': jax.random.normal(ks[2], (B, L, D_MODEL), jnp.float32), 'Wq': jax.random.normal(ks[3], (D_MODEL, D_MODEL), jnp.float32) * s, 'bq': jnp.zeros((D_MODEL,), jnp.float32), 'Wk': jax.random.normal(ks[4], (D_MODEL, D_MODEL), jnp.float32) * s, 'bk': jnp.zeros((D_MODEL,), jnp.float32), 'Wv': jax.random.normal(ks[5], (D_MODEL, D_MODEL), jnp.float32) * s, 'bv': jnp.zeros((D_MODEL,), jnp.float32), 'Wo': jax.random.normal(ks[6], (D_MODEL, D_MODEL), jnp.float32) * s, 'bo': jnp.zeros((D_MODEL,), jnp.float32)}
        return inp
    _L1_xattn_all = _L1_xattn_setup()
    _L1_xattn_in = {k: v for k, v in _L1_xattn_all.items() if k in ('Wq', 'bq', 'Wk', 'bk', 'Wv', 'bv', 'Wo', 'bo')}
    del _L1_xattn_all

    def _L1_ffn_setup():
        import jax, jax.numpy as jnp
        import numpy as np
        B, SEQ, DIM = (2, 512, 128)
        E, S = (8, 64)
        HID = 4 * DIM
        SCALE = DIM ** 0.5

        def rmsnorm(x, gamma):
            n = jnp.linalg.norm(x, axis=-1, keepdims=True)
            return x / jnp.maximum(n, 1e-12) * SCALE * gamma
        key = jax.random.key(seed)
        ks = jax.random.split(key, 4)
        w_init = lambda k, shape: jax.random.normal(k, shape, dtype=jnp.float32) * 0.02
        return {'x': jax.random.normal(ks[0], (B, SEQ, DIM), dtype=jnp.float32), 'norm_gamma': jnp.ones((DIM,), jnp.float32), 'slot_norm_gamma': jnp.ones((DIM,), jnp.float32), 'slot_embeds': jax.random.normal(ks[1], (E, S, DIM), dtype=jnp.float32), 'w1': w_init(ks[2], (E, DIM, HID)), 'b1': jnp.zeros((E, HID), jnp.float32), 'w2': w_init(ks[3], (E, HID, DIM)), 'b2': jnp.zeros((E, DIM), jnp.float32)}
    _L1_ffn_all = _L1_ffn_setup()
    _L1_ffn_in = {k: v for k, v in _L1_ffn_all.items() if k in ('norm_gamma', 'slot_norm_gamma', 'slot_embeds', 'w1', 'b1', 'w2', 'b2')}
    del _L1_ffn_all
    return {'x': x, 'ctx_1024': ctx_1024, 'mask_SxS2_bk1': mask_SxS2_bk1, 'L0_attn_Wq': _L0_attn_in['Wq'], 'L0_attn_Wk': _L0_attn_in['Wk'], 'L0_attn_Wv': _L0_attn_in['Wv'], 'L0_attn_Wo': _L0_attn_in['Wo'], 'L0_xattn_W_q': _L0_xattn_in['W_q'], 'L0_xattn_W_k': _L0_xattn_in['W_k'], 'L0_xattn_W_v': _L0_xattn_in['W_v'], 'L0_xattn_W_o': _L0_xattn_in['W_o'], 'L0_ffn_weight': _L0_ffn_in['weight'], 'L0_ffn_bias': _L0_ffn_in['bias'], 'L1_attn_Wg': _L1_attn_in['Wg'], 'L1_attn_bg': _L1_attn_in['bg'], 'L1_attn_Wv': _L1_attn_in['Wv'], 'L1_attn_bv': _L1_attn_in['bv'], 'L1_attn_Wd': _L1_attn_in['Wd'], 'L1_attn_bd': _L1_attn_in['bd'], 'L1_xattn_Wq': _L1_xattn_in['Wq'], 'L1_xattn_bq': _L1_xattn_in['bq'], 'L1_xattn_Wk': _L1_xattn_in['Wk'], 'L1_xattn_bk': _L1_xattn_in['bk'], 'L1_xattn_Wv': _L1_xattn_in['Wv'], 'L1_xattn_bv': _L1_xattn_in['bv'], 'L1_xattn_Wo': _L1_xattn_in['Wo'], 'L1_xattn_bo': _L1_xattn_in['bo'], 'L1_ffn_norm_gamma': _L1_ffn_in['norm_gamma'], 'L1_ffn_slot_norm_gamma': _L1_ffn_in['slot_norm_gamma'], 'L1_ffn_slot_embeds': _L1_ffn_in['slot_embeds'], 'L1_ffn_w1': _L1_ffn_in['w1'], 'L1_ffn_b1': _L1_ffn_in['b1'], 'L1_ffn_w2': _L1_ffn_in['w2'], 'L1_ffn_b2': _L1_ffn_in['b2']}

def reference(x, ctx_1024, mask_SxS2_bk1, L0_attn_Wq, L0_attn_Wk, L0_attn_Wv, L0_attn_Wo, L0_xattn_W_q, L0_xattn_W_k, L0_xattn_W_v, L0_xattn_W_o, L0_ffn_weight, L0_ffn_bias, L1_attn_Wg, L1_attn_bg, L1_attn_Wv, L1_attn_bv, L1_attn_Wd, L1_attn_bd, L1_xattn_Wq, L1_xattn_bq, L1_xattn_Wk, L1_xattn_bk, L1_xattn_Wv, L1_xattn_bv, L1_xattn_Wo, L1_xattn_bo, L1_ffn_norm_gamma, L1_ffn_slot_norm_gamma, L1_ffn_slot_embeds, L1_ffn_w1, L1_ffn_b1, L1_ffn_w2, L1_ffn_b2):
    import jax
    import jax.numpy as jnp

    def _L0_attn_ref(x, Wq, Wk, Wv, Wo):
        import jax, jax.numpy as jnp
        import numpy as np
        NUM_HEADS = 16
        THETA = 10000.0

        def _rotate_half(x):
            x = x.reshape(x.shape[:-1] + (-1, 2))
            x1, x2 = (x[..., 0], x[..., 1])
            return jnp.stack((-x2, x1), axis=-1).reshape(x.shape[:-2] + (-1,))

        def _rope(x):
            d_k = x.shape[-1]
            seq_len = x.shape[-2]
            inv_freq = 1.0 / THETA ** (jnp.arange(0, d_k, 2, dtype=jnp.float32) / d_k)
            pos = jnp.arange(seq_len, dtype=jnp.float32)
            theta = pos[:, None] * inv_freq[None, :]
            cos = jnp.repeat(jnp.cos(theta), 2, axis=-1)
            sin = jnp.repeat(jnp.sin(theta), 2, axis=-1)
            return x * cos + _rotate_half(x) * sin
        B, S, D = x.shape
        H = NUM_HEADS
        d_k = D // H

        def split_heads(t):
            return t.reshape(B, S, H, d_k).transpose(0, 2, 1, 3)
        Q = split_heads(x @ Wq)
        K = split_heads(x @ Wk)
        V = split_heads(x @ Wv)
        Q = _rope(Q)
        K = _rope(K)
        scores = jnp.einsum('bhqd,bhkd->bhqk', Q, K) / jnp.sqrt(jnp.float32(d_k))
        causal = jnp.tril(jnp.ones((S, S), dtype=bool))
        scores = jnp.where(causal[None, None], scores, -jnp.inf)
        attn = jax.nn.softmax(scores, axis=-1)
        out = jnp.einsum('bhqk,bhkd->bhqd', attn, V)
        out = out.transpose(0, 2, 1, 3).reshape(B, S, D)
        return out @ Wo

    def _L0_xattn_ref(xq, xk, xv, mask, W_q, W_k, W_v, W_o):
        import jax, jax.numpy as jnp
        import numpy as np
        D = 128
        H = 16
        HD = 64
        B, S = (4, 256)
        NEG = -1000000000.0

        def split_heads(x, W):
            y = jnp.einsum('bsd,df->bsf', x, W)
            return y.reshape(x.shape[0], x.shape[1], H, HD).transpose(0, 2, 1, 3)
        q = split_heads(xq, W_q)
        k = split_heads(xk, W_k)
        v = split_heads(xv, W_v)
        scores = jnp.einsum('bhqd,bhkd->bhqk', q, k) / jnp.sqrt(jnp.float32(HD))
        scores = jnp.where(mask[None, None, :, :], jnp.float32(NEG), scores)
        attn = jax.nn.softmax(scores, axis=-1)
        ctx = jnp.einsum('bhqk,bhkd->bhqd', attn, v)
        ctx = ctx.transpose(0, 2, 1, 3).reshape(xq.shape[0], xq.shape[1], H * HD)
        return jnp.einsum('bsf,fd->bsd', ctx, W_o)

    def _L0_ffn_ref(x, weight, bias):
        import jax, jax.numpy as jnp
        import numpy as np
        FP8_MAX = 448.0
        SCALE = 1.0
        _FP8_DTYPE = getattr(jnp, 'float8_e4m3fn', jnp.float16)

        def quantize_e4m3(t, scale):
            return jnp.clip(t / scale, -FP8_MAX, FP8_MAX).astype(_FP8_DTYPE)
        B, N, C = x.shape
        x2d = x.reshape(B * N, C)
        x_mat = quantize_e4m3(x2d, SCALE).astype(jnp.float16)
        w_mat = quantize_e4m3(weight, SCALE).astype(jnp.float16)
        out2d = (x_mat @ w_mat.T).astype(jnp.float32) * (SCALE * SCALE)
        out2d = out2d + bias
        return out2d.reshape(B, N, -1)

    def _L1_attn_ref(x, Wg, bg, Wv, bv, Wd, bd):
        import jax, jax.numpy as jnp
        import numpy as np
        D_MODEL = 128
        B, S = (4, 512)

        def _linear_scan(x_scan, a):

            def combine(l, r):
                al, xl = l
                ar, xr = r
                return (al * ar, ar * xl + xr)
            _, h = jax.lax.associative_scan(combine, (a, x_scan), axis=1)
            return h
        g = jnp.einsum('bsd,de->bse', x, Wg) + bg
        v = jnp.einsum('bsd,de->bse', x, Wv) + bv
        d = jnp.einsum('bsd,de->bse', x, Wd) + bd
        x_scan = jax.nn.sigmoid(g) * jnp.tanh(v)
        a = 0.001 + 0.998 * jax.nn.sigmoid(d)
        return _linear_scan(x_scan, a)

    def _L1_xattn_ref(queries, keys, values, Wq, bq, Wk, bk, Wv, bv, Wo, bo):
        import jax, jax.numpy as jnp
        import numpy as np
        D_MODEL = 128
        N_HEADS = 16
        HEAD_DIM = D_MODEL // N_HEADS
        SCALE = HEAD_DIM ** (-0.5)
        B, L, _ = queries.shape
        S = keys.shape[1]
        q = (queries @ Wq + bq).reshape(B, L, N_HEADS, HEAD_DIM).transpose(0, 2, 1, 3)
        k = (keys @ Wk + bk).reshape(B, S, N_HEADS, HEAD_DIM).transpose(0, 2, 1, 3)
        v = (values @ Wv + bv).reshape(B, S, N_HEADS, HEAD_DIM).transpose(0, 2, 1, 3)
        scores = jnp.einsum('bhld,bhsd->bhls', q, k) * SCALE
        weights = jax.nn.softmax(scores, axis=-1)
        out = jnp.einsum('bhls,bhsd->bhld', weights, v)
        out = out.transpose(0, 2, 1, 3).reshape(B, L, D_MODEL)
        out = out @ Wo + bo
        return out

    def _L1_ffn_ref(x, norm_gamma, slot_norm_gamma, slot_embeds, w1, b1, w2, b2):
        import jax, jax.numpy as jnp
        import numpy as np
        B, SEQ, DIM = (2, 512, 128)
        E, S = (8, 64)
        HID = 4 * DIM
        SCALE = DIM ** 0.5

        def rmsnorm(x, gamma):
            n = jnp.linalg.norm(x, axis=-1, keepdims=True)
            return x / jnp.maximum(n, 1e-12) * SCALE * gamma
        xn = rmsnorm(x, norm_gamma)
        sn = rmsnorm(slot_embeds, slot_norm_gamma)
        logits = jnp.einsum('bnd,esd->bnes', xn, sn)
        dispatch = jax.nn.softmax(logits, axis=1)
        b, n, e, s = logits.shape
        combine = jax.nn.softmax(logits.reshape(b, n, e * s), axis=-1)
        slots = jnp.einsum('bnd,bnes->besd', xn, dispatch)
        h = jnp.einsum('besd,edh->besh', slots, w1) + b1[None, :, None, :]
        h = jax.nn.gelu(h, approximate=False)
        eo = jnp.einsum('besh,ehd->besd', h, w2) + b2[None, :, None, :]
        eo = eo.reshape(b, e * s, DIM)
        out = jnp.einsum('bmd,bnm->bnd', eo, combine)
        return out
    x = x + _L0_attn_ref(_layernorm(x, axis=-1), L0_attn_Wq, L0_attn_Wk, L0_attn_Wv, L0_attn_Wo)
    x = x + _L0_xattn_ref(_layernorm(x, axis=-1), ctx_1024, ctx_1024, mask_SxS2_bk1, L0_xattn_W_q, L0_xattn_W_k, L0_xattn_W_v, L0_xattn_W_o)
    x = x + _L0_ffn_ref(_layernorm(x, axis=-1), L0_ffn_weight, L0_ffn_bias)
    x = x + _L1_attn_ref(_layernorm(x, axis=-1), L1_attn_Wg, L1_attn_bg, L1_attn_Wv, L1_attn_bv, L1_attn_Wd, L1_attn_bd)
    x = x + _L1_xattn_ref(_layernorm(x, axis=-1), ctx_1024, ctx_1024, L1_xattn_Wq, L1_xattn_bq, L1_xattn_Wk, L1_xattn_bk, L1_xattn_Wv, L1_xattn_bv, L1_xattn_Wo, L1_xattn_bo)
    x = x + _L1_ffn_ref(_layernorm(x, axis=-1), L1_ffn_norm_gamma, L1_ffn_slot_norm_gamma, L1_ffn_slot_embeds, L1_ffn_w1, L1_ffn_b1, L1_ffn_w2, L1_ffn_b2)
    return x

_drawn_inputs = setup_inputs


def setup_inputs(seed=0):
    import zlib

    import numpy as np

    out = dict(_drawn_inputs(seed))
    spreads = {'L0_ffn_bias': (0.0, 0.1),
     'L1_attn_bg': (0.0, 0.371),
     'L1_attn_bv': (0.0, 0.1),
     'L1_attn_bd': (1.0, 0.2),
     'L1_xattn_bq': (0.0, 0.8),
     'L1_xattn_bk': (0.0, 2.0),
     'L1_xattn_bv': (0.0, 0.1),
     'L1_xattn_bo': (0.0, 0.1),
     'L1_ffn_norm_gamma': (1.0, 0.6),
     'L1_ffn_slot_norm_gamma': (1.0, 0.6),
     'L1_ffn_b1': (0.0, 0.8),
     'L1_ffn_b2': (0.0, 0.298)}
    factors = {'L0_attn_Wq': 8.0,
     'L0_attn_Wk': 8.0,
     'L0_attn_Wv': 4.095,
     'L0_attn_Wo': 4.002,
     'L1_ffn_w1': 3.375,
     'L1_ffn_w2': 3.153}
    for name, (base, spread) in spreads.items():
        noise = np.random.default_rng([zlib.crc32(name.encode()), seed]).standard_normal(out[name].shape)
        drawn = base * np.exp(spread * noise) if base else spread * noise
        out[name] = jnp.asarray(drawn.astype(out[name].dtype))
    for name, factor in factors.items():
        out[name] = (out[name] * factor).astype(out[name].dtype)
    return out
```

```python
from collections import namedtuple
from contextlib import ExitStack

import numpy as np
import concourse.bass as bass
from concourse import mybir

F32, BF16, F16, I32, U8 = (mybir.dt.float32, mybir.dt.bfloat16, mybir.dt.float16, mybir.dt.int32, mybir.dt.uint8)
FP8 = mybir.dt.float8e4
ALU = mybir.AluOpType
ACT = mybir.ActivationFunctionType
AX = mybir.AxisListType

B, S, D = 16, 128, 128
H, DK = 16, 8
HD = 64
C2 = 77
NG, HG = 4, 4
NCH = H * HD // 128
E, SL, HID = 8, 64, 512
NHC = HID // 128
ES = E * SL
EPS = 1e-5
MASKED = -float(2.0 ** 100)
RSQRT_MAGIC = 1597463007.0

BG, BV, BD, BQ, GAMMA, SGAMMA, B1 = range(7)
N_ROWS = B1


def wait(eng, sem, value):
    if isinstance(value, int) and value <= 0:
        return
    eng.wait_ge(sem, value)


def valid(b):
    return not isinstance(b, int) or 0 <= b < B


def walk(eng, n, lo, hi, body):
    assert lo % 2 == 0 and (hi - lo) % 2 == 0
    for t in range(lo):
        body(t, t % 2)
    with eng.Fori(lo // 2, hi // 2) as r:
        body(2 * r, 0)
        body(2 * r + 1, 1)
    for t in range(hi, n):
        body(t, t % 2)


def Sems(nc, ctx, prefix, names):
    return namedtuple("Sems", names)(*[ctx.enter_context(nc.semaphore(f"{prefix}_{n}")) for n in names.split()])


class Memory:
    pass


def rsqrt(dve, link, y, v, t):
    link(dve.tensor_scalar(y.bitcast(I32), v.bitcast(I32), 1, None, ALU.logical_shift_right))
    link(dve.tensor_scalar(y.bitcast(I32), y.bitcast(I32), -1.0, RSQRT_MAGIC, ALU.mult, ALU.add))
    for _ in range(4):
        link(dve.tensor_tensor(t, y, y, ALU.mult))
        link(dve.tensor_tensor(t, t, v, ALU.mult))
        link(dve.tensor_scalar(t, t, -0.5, 1.5, ALU.mult, ALU.add))
        link(dve.tensor_tensor(y, y, t, ALU.mult))


def linker(dve, sem, count):
    def link(ins):
        count[0] += 1
        ins.then_inc(sem, 1)
        dve.wait_ge(sem, count[0])
    return link


def row_scale(dve, m):
    link = linker(dve, m.s_link, m.link_count)
    for b in range(B):
        ins = dve.bn_aggr(m.mv[:, b, :], m.bn[:, b, :])
    link(ins)
    link(dve.tensor_scalar(m.veps[:, :], m.mv[:, :, 1], EPS, None, ALU.add))
    rsqrt(dve, link, m.rstd[:, :], m.veps[:, :], m.tmp16[:, :])


def row_stats(dve, m, sem, b):
    dve.bn_stats(m.bn[:, b, :], m.x[:, b, :]).then_inc(sem, 1)


def normalise(dve, m, out, b, **how):
    return dve.tensor_scalar(out, m.x[:, b, :], m.mv[:, b, 0:1], m.rstd[:, bass.ds(b, 1)], ALU.subtract, ALU.mult, **how)


def load_block(nc, ctx, m, d):
    s = Sems(nc, ctx, "ld", "x0 x1 x2 x3 ctx ident small self_w cross_w keys_w prep stats ctx_t ctx_tc vec_t vec_c wt wt_c "
             "kT kTc sn sn_t sn_c bf rot slots mask")
    s_x = (s.x0, s.x1, s.x2, s.x3)
    rows = (d.L1_attn_bg, d.L1_attn_bv, d.L1_attn_bd, d.L1_xattn_bq, d.L1_ffn_norm_gamma, d.L1_ffn_slot_norm_gamma)
    KB = 4
    kraw = B // KB * (NCH + 1)
    with ExitStack() as tmp, nc.Block() as block:
        sb = lambda n, sh, dt: tmp.enter_context(nc.sbuf_tensor(n, sh, dt))
        ps = [tmp.enter_context(nc.psum_tensor(f"ld_ps{i}", [128, 512], F32)) for i in range(4)]
        ctx_raw = sb("ctx_raw", [C2, B, D], F32)
        vec_rows = sb("vec_rows", [N_ROWS + E * NHC, 128], F32)
        w_raw = sb("ffn_w_raw", [128, 128], F32)
        w_clip = sb("ffn_w_clip", [128, 2, 128], F32)
        w8 = sb("ffn_w8", [128, 2, 128], FP8)
        w_val = sb("ffn_w_val", [128, 2, 128], F32)
        w_big = sb("ffn_w_big", [128, 128], F32)
        wk_wide = sb("wk_wide", [128, H * HD], F32)
        wk_narrow = sb("wk_narrow", [128, 128], F32)
        bk_row = sb("bk_row", [1, 128], F32)
        slots = sb("slots", [128, 4, 128], F32)
        slots2 = sb("slots2", [128, 4, 128], F32)
        ss = sb("slot_ss", [128, 4], F32)
        rs = sb("slot_rs", [128, 4], F32)
        t4 = sb("slot_t", [128, 4], F32)
        mask8 = sb("mask8", [128, C2], U8)

        @block.sync
        def _(sp):
            for g in range(4):
                sp.dma_start(m.x[:, 4 * g:4 * g + 4, :], d.x[4 * g:4 * g + 4].rearrange("b t f -> t b f")).then_inc(s_x[g], 16)
            sp.dma_start(ctx_raw[:, :, :], d.ctx_1024.rearrange("b k f -> k b f")).then_inc(s.ctx, 16)
            sp.dma_start(wk_wide[:, :], d.L0_xattn_W_k).then_inc(s.keys_w, 16)
            sp.dma_start(wk_narrow[:, :], d.L1_xattn_Wk).then_inc(s.keys_w, 16)
            sp.dma_start(bk_row[:, :], d.L1_xattn_bk.rearrange("(a n) -> a n", a=1)).then_inc(s.keys_w, 16)
            sp.dma_start(slots[:, :, :], d.L1_ffn_slot_embeds.rearrange("(c e) s f -> (e s) c f", c=4)).then_inc(s.slots, 16)
            sp.dma_start(m.wq_wide[:, :], d.L0_xattn_W_q).then_inc(m.s_weights, 16)
            sp.dma_start(m.wv_wide[:, :], d.L0_xattn_W_v).then_inc(m.s_weights, 16)
            sp.dma_start(m.wo_wide[:, :, :], d.L0_xattn_W_o.rearrange("(c p) f -> p c f", p=128)).then_inc(m.s_weights, 16)
            for dst, src in ((m.wg, d.L1_attn_Wg), (m.wvs, d.L1_attn_Wv), (m.wd, d.L1_attn_Wd), (m.wq1, d.L1_xattn_Wq),
                             (m.wv1, d.L1_xattn_Wv), (m.wo1, d.L1_xattn_Wo)):
                sp.dma_start(dst[:, :], src).then_inc(m.s_weights, 16)

        @block.scalar
        def _(act):
            act.dma_start(m.ident[:, :], d.ident).then_inc(s.ident, 16)
            act.dma_start(m.wqk[:, 0, :], d.L0_attn_Wq).then_inc(s.self_w, 16)
            act.dma_start(m.wqk[:, 1, :], d.L0_attn_Wk).then_inc(s.self_w, 16)
            act.dma_start(m.rope[:, :, :, :], d.rope).then_inc(s.self_w, 16)
            act.dma_start(m.wv0[:, :], d.L0_attn_Wv).then_inc(m.s_weights, 16)
            act.dma_start(m.wo0[:, :], d.L0_attn_Wo).then_inc(m.s_weights, 16)
            act.dma_start(m.headmask[:, :, :], d.headmask).then_inc(m.s_weights, 16)
            act.dma_start(w_raw[:, :], d.L0_ffn_weight).then_inc(s.small, 16)
            act.dma_start(m.ffn_bias[:, :], d.L0_ffn_bias.partition_broadcast(128)).then_inc(m.s_weights, 16)
            act.dma_start(mask8[:, :], d.mask_SxS2_bk1).then_inc(s.mask, 16)
            for i, vec in enumerate(rows):
                act.dma_start(vec_rows[i:i + 1, :], vec.rearrange("(a n) -> a n", a=1)).then_inc(s.cross_w, 16)
            act.dma_start(vec_rows[N_ROWS:, :], d.L1_ffn_b1.rearrange("e (c p) -> (e c) p", p=128)).then_inc(s.cross_w, 16)
            act.dma_start(m.bv1[:, :], d.L1_xattn_bv.rearrange("(a n) -> a n", a=1)).then_inc(m.s_weights, 16)
            act.dma_start(m.bo1[:, :], d.L1_xattn_bo.rearrange("(a n) -> a n", a=1)).then_inc(m.s_weights, 16)
            for g in range(4):
                act.wait_ge(s.ctx_t, g + 1)
                act.activation(m.ctxT[:, 4 * g:4 * g + 4, :], ps[g % 2][:, 0:4 * C2].rearrange("p (b k) -> p b k", b=4),
                               ACT.Copy).then_inc(s.ctx_tc, 1)
            act.wait_ge(s.vec_t, 1)
            act.activation(m.vec[:, :], ps[2][:, 0:N_ROWS + E * NHC], ACT.Copy).then_inc(s.vec_c, 1)
            for i in range(kraw):
                g, c = divmod(i, NCH + 1)
                act.wait_ge(s.kT, i + 1)
                src = ps[i % 2][:, 0:KB * C2].rearrange("p (b k) -> p b k", b=KB)
                dst = m.kT_wide[:, KB * g:KB * g + KB, c, :] if c < NCH else m.kT1[:, KB * g:KB * g + KB, :]
                act.activation(dst, src, ACT.Copy).then_inc(s.kTc, 1)
            act.wait_ge(s.wt, 1)
            act.activation(m.ffn_wT[:, :], ps[2][:, 0:128], ACT.Copy).then_inc(s.wt_c, 1)
            act.wait_ge(s.sn_t, 1)
            act.wait_ge(s.prep, 7)
            act.activation(m.snT[:, :], ps[3][:, :], ACT.Copy, scale=m.gg[:, 0:1]).then_inc(s.sn_c, 1)

        @block.tensor
        def _(pe):
            pe.wait_ge(s.ident, 16)
            pe.wait_ge(s.ctx, 16)
            for g in range(4):
                wait(pe, s.ctx_tc, g - 1)
                for i in range(4):
                    ins = pe.transpose(ps[g % 2][:, i * C2:(i + 1) * C2], ctx_raw[:, 4 * g + i, :], m.ident[0:C2, 0:C2])
                ins.then_inc(s.ctx_t, 1)
            pe.wait_ge(s.cross_w, 16 * (N_ROWS + 1))
            n = N_ROWS + E * NHC
            pe.transpose(ps[2][:, 0:n], vec_rows[:, :], m.ident[0:n, 0:n]).then_inc(s.vec_t, 1)
            pe.wait_ge(s.keys_w, 48)
            pe.wait_ge(s.ctx_tc, 4)
            pe.wait_ge(s.prep, 1)
            for i in range(kraw):
                g, c = divmod(i, NCH + 1)
                wait(pe, s.kTc, i - 1)
                keys = m.ctxT[:, KB * g:KB * g + KB, :]
                w = wk_wide[:, c * 128:(c + 1) * 128] if c < NCH else wk_narrow[:, :]
                ins = pe.matmul(ps[i % 2][:, 0:KB * C2], w, keys, start=True, stop=c < NCH)
                if c == NCH:
                    ins = pe.matmul(ps[i % 2][:, 0:KB * C2], bk_row[0:1, :], m.ones[0:1, 0:KB * C2], start=False, stop=True)
                ins.then_inc(s.kT, 1)
            pe.wait_ge(s.vec_c, 1)
            pe.wait_ge(s.prep, 5)
            pe.transpose(ps[2][:, 0:128], w_val[:, 0, :], m.ident[:, :]).then_inc(s.wt, 1)
            pe.wait_ge(s.prep, 6)
            for c in range(4):
                ins = pe.transpose(ps[3][:, c * 128:(c + 1) * 128], slots2[:, c, :], m.ident[:, :])
            ins.then_inc(s.sn_t, 1)

        @block.gpsimd
        def _(pool):
            pool.memset(m.causal[:, :, :], 0.0).then_inc(s.mask, 1)
            pool.wait_ge(s.mask, 17)
            pool.affine_select(out=m.causal[:, :, :], in_=m.causal[:, :, :], compare_op=ALU.is_ge, fill=MASKED, base=0,
                               pattern=[[0, HG], [-1, 128]], channel_multiplier=1).then_inc(m.s_causal, 1)

        @block.vector
        def _(dve):
            link = linker(dve, m.s_link, m.link_count)
            dve.memset(m.ones[:, :], 1.0).then_inc(s.prep, 1)
            dve.wait_ge(s.ident, 16)
            dve.tensor_copy(m.ident16[:, :], m.ident[:, :]).then_inc(s.bf, 1)
            dve.wait_ge(s.self_w, 48)
            for i in range(2):
                w = m.wqk[:, i, :].rearrange("p (n two) -> p n two", two=2)
                r = m.wqk[:, 2 + i, :].rearrange("p (n two) -> p n two", two=2)
                dve.tensor_scalar(r[:, :, 0], w[:, :, 1], -1.0, None, ALU.mult).then_inc(s.rot, 1)
                dve.tensor_copy(r[:, :, 1], w[:, :, 0]).then_inc(s.rot, 1)
            for b in range(B):
                if b % 4 == 0:
                    dve.wait_ge(s_x[b // 4], 16)
                row_stats(dve, m, s.stats, b)
            dve.wait_ge(s.small, 16)
            link(dve.tensor_scalar(w_clip[:, 0, :], w_raw[:, :], 240.0, -240.0, ALU.min, ALU.max))
            link(dve.tensor_scalar(w_clip[:, 1, :], w_raw[:, :], 448.0, -448.0, ALU.min, ALU.max))
            link(dve.tensor_copy(w8[:, 0, :], w_clip[:, 0, :], saturate=False))
            link(dve.tensor_scalar(w8[:, 1, :], w_clip[:, 1, :], 0.5, None, ALU.mult, saturate=False))
            link(dve.tensor_copy(w_val[:, 0, :], w8[:, 0, :]))
            link(dve.tensor_scalar(w_val[:, 1, :], w8[:, 1, :], 2.0, None, ALU.mult))
            link(dve.tensor_tensor(w_big[:, :], w_raw[:, :], w_raw[:, :], ALU.mult))
            link(dve.tensor_scalar(w_big[:, :], w_big[:, :], 128.0 ** 2, None, ALU.is_gt))
            dve.copy_predicated(w_val[:, 0, :], w_big[:, :].bitcast(I32), w_val[:, 1, :]).then_inc(s.prep, 4)
            dve.wait_ge(s.slots, 16)
            link(dve.tensor_tensor(slots2[:, :, :], slots[:, :, :], slots[:, :, :], ALU.mult))
            link(dve.tensor_reduce(ss[:, :], slots2[:, :, :], AX.X, ALU.add))
            link(dve.tensor_scalar(ss[:, :], ss[:, :], 1e-24, None, ALU.max))
            rsqrt(dve, link, rs[:, :], ss[:, :], t4[:, :])
            link(dve.tensor_scalar(rs[:, :], rs[:, :], float(D) ** 0.5, None, ALU.mult))
            dve.tensor_tensor(slots2[:, :, :], slots[:, :, :], rs[:, :].unsqueeze(2).broadcast_to([128, 4, 128]),
                              ALU.mult).then_inc(s.prep, 1)
            dve.wait_ge(s.vec_c, 1)
            dve.tensor_tensor(m.gg[:, :], m.vec[:, GAMMA:GAMMA + 1], m.vec[:, SGAMMA:SGAMMA + 1], ALU.mult).then_inc(s.prep, 1)
            dve.tensor_scalar(m.half_b[:, 0:1], m.vec[:, BG:BG + 1], 0.5, None, ALU.mult).then_inc(s.bf, 1)
            dve.tensor_scalar(m.half_b[:, 1:2], m.vec[:, BD:BD + 1], 0.5, None, ALU.mult).then_inc(s.bf, 1)
            dve.tensor_scalar(m.half_b[:, 2:3], m.vec[:, BQ:BQ + 1], float(DK) ** -0.5, None, ALU.mult).then_inc(s.bf, 1)
            dve.wait_ge(s.mask, 17)
            for i in range(HG):
                dve.tensor_scalar(m.xmask[:, i, :], mask8[:, :], MASKED, None, ALU.mult).then_inc(s.bf, 1)
            dve.wait_ge(s.stats, B)
            dve.wait_ge(s.bf, 4 + HG)
            dve.wait_ge(s.rot, 4)


def narrow_attention(nc, ctx, m, name, K, cross):
    s = Sems(nc, ctx, name, "xn xt xtc proj rope1 q km vp v sc mx sub ex pt ptc pv rec nrm ot otc y res stats ctxc")
    wv, wo = (m.wv1, m.wo1) if cross else (m.wv0, m.wo0)
    with ExitStack() as tmp, nc.Block() as block:
        sb = lambda n, sh, dt=F32: tmp.enter_context(nc.sbuf_tensor(f"{name}_{n}", sh, dt))
        pb = lambda n, sh, dt=F32: tmp.enter_context(nc.psum_tensor(f"{name}_{n}", sh, dt))
        xn, xnT = sb("xn", [128, 2, 128]), sb("xnT", [128, 2, 128])
        rot = sb("rot", [128, 2, 2, 128])
        qk = sb("qk", [128, 2, 2, 128])
        kmask = sb("kmask", [128, 2, HG, K])
        vx = sb("vx", [K, 2, H, DK + 1])
        cur = sb("cur", [128, 2, C2])
        prob = sb("prob", [128, 2, HG, K])
        probT = sb("probT", [K, 2, HG, 128])
        mx = sb("mx", [128, 2, HG])
        rec = sb("rec", [128, H])
        att, attT = sb("att", [128, 128]), sb("attT", [128, 128])
        pS = [pb(f"pS{i}", [128, HG, 128]) for i in range(2)]
        pT = [pb(f"pT{i}", [128, HG, 128]) for i in range(2)]
        pP, pVX, pO, pY = pb("pP", [128, 4, 128]), pb("pVX", [128, 4, 128]), pb("pO", [128, 512]), pb("pY", [128, 4, 128])
        O = pO[:, 0:H * (DK + 1)].rearrange("p (h w) -> p h w", h=H)
        SC = lambda g: pS[g % 2][:, :, :].rearrange("p a b -> p (a b)")[:, 0:HG * K].rearrange("p (a b) -> p a b", a=HG)

        N = B + 3
        LO, HI = 6, 16

        @block.tensor
        def _(pe):
            if cross:
                pe.wait_ge(m.s_weights, m.all_weights)
            else:
                pe.wait_ge(m.s_weights, m.all_weights)
                pe.wait_ge(m.s_causal, 1)

            def body(t, p):
                for g in range(NG):
                    b, q = t - 1, (p + 1) % 2
                    u = 4 * b + g
                    if valid(b):
                        if g == 0:
                            wait(pe, s.km, b + 1)
                            wait(pe, s.q, b + 1)
                        wait(pe, s.sub, u - 1)
                        rows = slice(32 * g, 32 * g + 32)
                        ins = pe.matmul(SC(g), qk[rows, q, 0, :], kmask[rows, q, :, :], start=True, stop=cross)
                        if not cross:
                            ins = pe.matmul(SC(g), m.ident16[:, :], m.causal[:, :, :], start=False, stop=True)
                        ins.then_inc(s.sc, 1)
                    bt, gt = (b, g - 2) if g >= 2 else (b - 1, g + 2)
                    if valid(bt):
                        v = 4 * bt + gt
                        wait(pe, s.ex, v + 1)
                        wait(pe, s.ptc, v - 1)
                        for i in range(HG):
                            ins = pe.transpose(pT[g % 2][0:K, i, :], prob[:, g % 2, i, :], m.ident[:, :])
                        ins.then_inc(s.pt, 1)
                    bp, gp, qp = (b, 0, q) if g == 3 else (b - 1, g + 1, p)
                    if valid(bp):
                        v = 4 * bp + gp
                        wait(pe, s.ptc, v + 1)
                        if gp == 0:
                            wait(pe, s.v, bp + 1)
                            wait(pe, s.nrm, bp)
                        for i in range(HG):
                            h = HG * gp + i
                            ins = pe.matmul(O[:, h, :], probT[:, gp % 2, i, :], vx[:, qp, h, :], start=True, stop=True)
                        ins.then_inc(s.pv, 1)
                    if g == 0 and valid(t - 3):
                        wait(pe, s.nrm, t - 2)
                        wait(pe, s.res, t - 3)
                        pe.transpose(pY[:, 0, :], att[:, :], m.ident[:, :]).then_inc(s.ot, 1)
                    if g == 2 and valid(t - 3):
                        wait(pe, s.otc, t - 2)
                        ins = pe.matmul(pY[:, 1, :], attT[:, :], wo[:, :], start=True, stop=not cross)
                        if cross:
                            ins = pe.matmul(pY[:, 1, :], m.ones[0:1, 0:128], m.bo1[:, :], start=False, stop=True)
                        ins.then_inc(s.y, 1)
                    if g == 0 and valid(t):
                        wait(pe, s.xn, t + 1)
                        wait(pe, s.v, t)
                        pe.transpose(pVX[:, 0, :], xn[:, p, :], m.ident[:, :]).then_inc(s.xt, 1)
                    if g == 1 and valid(t):
                        wait(pe, s.xtc, t + 1)
                        if cross:
                            wait(pe, s.q, t)
                            pe.matmul(pP[:, 0, :], m.wq1[:, :], xnT[:, p, :], start=True, stop=True).then_inc(s.proj, 1)
                            wait(pe, s.ctxc, t + 1)
                            pe.matmul(pVX[0:K, 1, :], cur[:, p, :], wv[:, :], start=True, stop=False)
                            pe.matmul(pVX[0:K, 1, :], m.ones[0:1, 0:K], m.bv1[:, :], start=False, stop=True).then_inc(s.vp, 1)
                        else:
                            wait(pe, s.rope1, 2 * t)
                            for i in range(4):
                                ins = pe.matmul(pP[:, i, :], m.wqk[:, i, :], xnT[:, p, :], start=True, stop=True)
                            ins.then_inc(s.proj, 1)
                            pe.matmul(pVX[:, 1, :], xnT[:, p, :], wv[:, :], start=True, stop=True).then_inc(s.vp, 1)

            walk(pe, N, LO, HI, body)

        @block.vector
        def _(dve):
            row_scale(dve, m)
            for q in range(2):
                dve.memset(vx[:, q, :, DK:DK + 1], 1.0).then_inc(m.s_ones, 1)

            def body(t, p):
                if valid(t):
                    wait(dve, s.xt, t - 1)
                    normalise(dve, m, xn[:, p, :], t).then_inc(s.xn, 1)
                for g in range(NG):
                    b = t - 1
                    u = 4 * b + g
                    if valid(b):
                        wait(dve, s.sc, u + 1)
                        dve.tensor_reduce(mx[:, g % 2, :], SC(g), AX.X, ALU.max).then_inc(s.mx, 1)
                        wait(dve, s.mx, u + 1)
                        wait(dve, s.pt, u - 1)
                        dve.tensor_tensor(prob[:, g % 2, :, :], SC(g), mx[:, g % 2, :].unsqueeze(2).broadcast_to([128, HG, K]),
                                          ALU.subtract).then_inc(s.sub, 1)
                    if g == 1 and valid(t) and not cross:
                        wait(dve, s.proj, t + 1)
                        wait(dve, s.q, t)
                        dve.tensor_tensor(rot[:, 0, :, :], pP[:, 0:2, :], m.rope[:, 0, :, :], ALU.mult).then_inc(s.rope1, 1)
                        dve.tensor_tensor(rot[:, 1, :, :], pP[:, 2:4, :], m.rope[:, 1, :, :], ALU.mult).then_inc(s.rope1, 1)
                        wait(dve, s.rope1, 2 * t + 2)
                        wait(dve, s.sc, 4 * (t - 1))
                        wait(dve, s.km, t - 1)
                        dve.tensor_tensor(qk[:, p, :, :], rot[:, 0, :, :], rot[:, 1, :, :], ALU.add).then_inc(s.q, 1)
                    if g == 3 and valid(t - 3):
                        b3 = t - 3
                        wait(dve, s.y, b3 + 1)
                        dve.tensor_tensor(m.x[:, b3, :], m.x[:, b3, :], pY[:, 1, :], ALU.add).then_inc(s.res, 1)
                        wait(dve, s.res, b3 + 1)
                        row_stats(dve, m, s.stats, b3)
                    if g == 3 and valid(t - 2):
                        b2 = t - 2
                        wait(dve, s.pv, 4 * b2 + 4)
                        wait(dve, s.ot, b2)
                        dve.reciprocal(rec[:, :], O[:, :, DK]).then_inc(s.rec, 1)
                        wait(dve, s.rec, b2 + 1)
                        dve.tensor_tensor(att[:, :].rearrange("p (h w) -> p h w", h=H), O[:, :, 0:DK],
                                          rec[:, :].unsqueeze(2).broadcast_to([128, H, DK]), ALU.mult).then_inc(s.nrm, 1)

            walk(dve, N, LO, HI, body)
            dve.wait_ge(s.stats, B)

        @block.gpsimd
        def _(pool):
            def body(t, p):
                if not valid(t):
                    return
                if cross:
                    wait(pool, s.vp, t - 1)
                    pool.tensor_copy(cur[:, p, :], m.ctxT[:, t, :]).then_inc(s.ctxc, 1)
                    k = m.kT1[:, t, :]
                else:
                    wait(pool, s.q, t + 1)
                    k = qk[:, p, 1, :]
                wait(pool, s.sc, 4 * (t - 1))
                pool.tensor_tensor(kmask[:, p, :, :], k.unsqueeze(1).broadcast_to([128, HG, K]), m.headmask[:, :, 0:K],
                                   ALU.mult).then_inc(s.km, 1)

            walk(pool, B, LO, HI, body)

        @block.scalar
        def _(act):
            act.wait_ge(m.s_ones, m.ones_base + 2)

            def body(t, p):
                for g in range(NG):
                    b = t - 1
                    u = 4 * b + g
                    bt, gt = (b, g - 2) if g >= 2 else (b - 1, g + 2)
                    if valid(bt):
                        v = 4 * bt + gt
                        wait(act, s.pt, v + 1)
                        wait(act, s.pv, v - 1)
                        act.activation(probT[:, g % 2, :, :], pT[g % 2][0:K, :, :], ACT.Copy).then_inc(s.ptc, 1)
                    if valid(b):
                        wait(act, s.sub, u + 1)
                        act.activation(prob[:, g % 2, :, :], prob[:, g % 2, :, :], ACT.Exp).then_inc(s.ex, 1)
                    if g == 0 and valid(t):
                        wait(act, s.xt, t + 1)
                        wait(act, s.vp, t - 1)
                        wait(act, s.proj, t - 1)
                        act.activation(xnT[:, p, :], pVX[:, 0, :], ACT.Copy).then_inc(s.xtc, 1)
                    if g == 1 and valid(t - 3):
                        wait(act, s.ot, t - 2)
                        wait(act, s.y, t - 3)
                        act.activation(attT[:, :], pY[:, 0, :], ACT.Copy).then_inc(s.otc, 1)
                    if g == 2 and valid(t):
                        wait(act, s.vp, t + 1)
                        wait(act, s.pv, 4 * (t - 1))
                        act.activation(vx[:, p, :, 0:DK], pVX[0:K, 1, :].rearrange("p (h w) -> p h w", h=H),
                                       ACT.Copy).then_inc(s.v, 1)
                        if cross:
                            wait(act, s.proj, t + 1)
                            wait(act, s.sc, 4 * (t - 1))
                            act.activation(qk[:, p, 0, :], pP[:, 0, :], ACT.Identity, bias=m.half_b[:, 2:3],
                                           scale=float(DK) ** -0.5).then_inc(s.q, 1)

            walk(act, N, LO, HI, body)
    m.ones_base += 2


def wide_attention(nc, ctx, m):
    name, K = "wide", C2
    s = Sems(nc, ctx, name, "xn xt xtc qv qve km ctxc sc mx sub ex pt ptc pv rec nrm ot otc y res stats zero")
    with ExitStack() as tmp, nc.Block() as block:
        sb = lambda n, sh, dt=F32: tmp.enter_context(nc.sbuf_tensor(f"{name}_{n}", sh, dt))
        pb = lambda n, sh, dt=F32: tmp.enter_context(nc.psum_tensor(f"{name}_{n}", sh, dt))
        xn, xnT = sb("xn", [128, 2, 128]), sb("xnT", [128, 2, 128])
        qT = sb("qT", [128, 2, NCH, 128])
        kblk = sb("kblk", [128, 2, NCH, 2, K])
        vx = sb("vx", [K, 2, H, HD + 1])
        cur = sb("cur", [128, 2, K])
        prob = sb("prob", [128, 2, HG, K])
        probT = sb("probT", [K, 2, HG, 128])
        mx, rec = sb("mx", [128, 2, HG]), sb("rec", [128, 2, HG])
        att, attT = sb("att", [128, 2, HG, HD]), sb("attT", [128, 2, 2, 128])
        pS = [pb(f"pS{i}", [128, 512]) for i in range(2)]
        pT = [pb(f"pT{i}", [128, HG, 128]) for i in range(2)]
        pQV, pO, pR, pY = pb("pQV", [128, 512]), pb("pO", [128, 512]), pb("pR", [128, 4, 128]), pb("pY", [128, 512])
        O = pO[:, 0:HG * (HD + 1)].rearrange("p (h w) -> p h w", h=HG)
        Y = pY[:, 0:128]
        SC = lambda g: pS[g % 2][:, 0:HG * K].rearrange("p (a b) -> p a b", a=HG)
        N = B + 4
        LO, HI = 6, 16

        def group(t, g, lag):
            back = (g - lag) // NG
            return t - 1 + back, (g - lag) % NG

        @block.tensor
        def _(pe):
            pe.wait_ge(s.zero, 2)

            def body(t, p):
                for g in range(NG):
                    b, q = t - 1, (p + 1) % 2
                    u = 4 * b + g
                    if valid(b):
                        if g == 0:
                            wait(pe, s.km, 2 * b + 2)
                            wait(pe, s.qve, 4 * b + 2)
                        wait(pe, s.sub, u - 1)
                        for i in range(2):
                            c = 2 * g + i
                            pe.matmul(pS[g % 2][:, 2 * K * i:2 * K * (i + 1)], qT[:, q, c, :], kblk[:, q, c, :, :],
                                      start=i == 0, stop=False, skip_group_check=True)
                        pe.matmul(SC(g), m.ident16[:, :], m.xmask[:, :, :], start=False, stop=True,
                                  skip_group_check=True).then_inc(s.sc, 1)
                    if g == 0 and valid(t):
                        wait(pe, s.xn, t + 1)
                        bo, go = group(t, 0, 5)
                        if valid(bo):
                            wait(pe, s.otc, 4 * bo + go + 1)
                        pe.transpose(pR[:, 0, :], xn[:, p, :], m.ident[:, :]).then_inc(s.xt, 1)
                    bt, gt = group(t, g, 2)
                    if valid(bt):
                        v = 4 * bt + gt
                        wait(pe, s.ex, v + 1)
                        wait(pe, s.ptc, v - 1)
                        for i in range(HG):
                            ins = pe.transpose(pT[g % 2][0:K, i, :], prob[:, g % 2, i, :], m.ident[:, :])
                        ins.then_inc(s.pt, 1)
                    bp, gp = group(t, g, 3)
                    if valid(bp):
                        v = 4 * bp + gp
                        wait(pe, s.ptc, v + 1)
                        if gp == 0:
                            wait(pe, s.qve, 4 * bp + 4)
                        wait(pe, s.nrm, v)
                        qp = q if g == 3 else p
                        for i in range(HG):
                            ins = pe.matmul(O[:, i, :], probT[:, gp % 2, i, :], vx[:, qp, HG * gp + i, :], start=True, stop=True)
                        ins.then_inc(s.pv, 1)
                    bo, go = group(t, g, 4)
                    if valid(bo):
                        v = 4 * bo + go
                        wait(pe, s.nrm, v + 1)
                        wait(pe, s.otc, v)
                        if g == 0 and valid(t):
                            wait(pe, s.xtc, t + 1)
                        elif g == 0:
                            wait(pe, s.xtc, B)
                        for i in range(2):
                            ins = pe.transpose(pR[:, 1 + i, :], att[:, go % 2, 2 * i:2 * i + 2, :], m.ident[:, :])
                        ins.then_inc(s.ot, 1)
                    by, gy = group(t, g, 5)
                    if valid(by):
                        v = 4 * by + gy
                        wait(pe, s.otc, v + 1)
                        if gy == 0:
                            wait(pe, s.res, by)
                        for i in range(2):
                            ins = pe.matmul(Y, attT[:, gy % 2, i, :], m.wo_wide[:, 2 * gy + i, :],
                                            start=gy == 0 and i == 0, stop=gy == 3 and i == 1)
                        ins.then_inc(s.y, 1)
                    if g == 0:
                        bv, k, pv = t - 1, 3, (p + 1) % 2
                    else:
                        bv, k, pv = t, g - 1, p
                    if valid(bv):
                        if k == 0:
                            wait(pe, s.xtc, t + 1)
                        if k == 2:
                            wait(pe, s.ctxc, t + 1)
                        wait(pe, s.qve, 4 * bv + k)
                        if k >= 2:
                            half = 512 * (k - 2)
                            ins = pe.matmul(pQV[0:K, :], cur[:, pv, :], m.wv_wide[:, half:half + 512], start=True, stop=True)
                        else:
                            for i in range(4):
                                c = 4 * k + i
                                ins = pe.matmul(pQV[:, 128 * i:128 * i + 128], m.wq_wide[:, 128 * c:128 * c + 128],
                                                xnT[:, p, :], start=True, stop=True)
                        ins.then_inc(s.qv, 1)

            walk(pe, N, LO, HI, body)

        @block.vector
        def _(dve):
            for q in range(2):
                dve.memset(kblk[:, q, :, :, :], 0.0).then_inc(s.zero, 1)
                dve.memset(vx[:, q, :, HD:HD + 1], 1.0).then_inc(s.rec, 1)
            row_scale(dve, m)
            dve.wait_ge(s.rec, 2)

            def body(t, p):
                if valid(t):
                    wait(dve, s.xt, t - 1)
                    normalise(dve, m, xn[:, p, :], t).then_inc(s.xn, 1)
                for g in range(NG):
                    b = t - 1
                    u = 4 * b + g
                    if valid(b):
                        wait(dve, s.sc, u + 1)
                        dve.tensor_reduce(mx[:, g % 2, :], SC(g), AX.X, ALU.max).then_inc(s.mx, 1)
                        wait(dve, s.mx, u + 1)
                        wait(dve, s.pt, u - 1)
                        dve.tensor_tensor(prob[:, g % 2, :, :], SC(g), mx[:, g % 2, :].unsqueeze(2).broadcast_to([128, HG, K]),
                                          ALU.subtract).then_inc(s.sub, 1)
                    bv, k, pv = (t - 1, 3, (p + 1) % 2) if g == 0 else (t, 2, p)
                    if g in (0, 3) and valid(bv):
                        wait(dve, s.qv, 4 * bv + k + 1)
                        if g == 3:
                            wait(dve, s.pv, 4 * (t - 1))
                        dve.tensor_copy(vx[:, pv, 8 * (k - 2):8 * (k - 2) + 8, 0:HD],
                                        pQV[0:K, :].rearrange("p (h w) -> p h w", h=8)).then_inc(s.qve, 1)
                    bp, gp = group(t, g, 3)
                    if valid(bp):
                        v = 4 * bp + gp
                        wait(dve, s.pv, v + 1)
                        dve.reciprocal(rec[:, gp % 2, :], O[:, :, HD]).then_inc(s.rec, 1)
                        wait(dve, s.rec, v + 3)
                        wait(dve, s.ot, v - 1)
                        dve.tensor_tensor(att[:, gp % 2, :, :], O[:, :, 0:HD],
                                          rec[:, gp % 2, :].unsqueeze(2).broadcast_to([128, HG, HD]), ALU.mult).then_inc(s.nrm, 1)
                    if g == 1 and valid(t - 3):
                        b3 = t - 3
                        wait(dve, s.y, 4 * b3 + 4)
                        dve.tensor_tensor(m.x[:, b3, :], m.x[:, b3, :], Y, ALU.add).then_inc(s.res, 1)
                        wait(dve, s.res, b3 + 1)
                        row_stats(dve, m, s.stats, b3)

            walk(dve, N, LO, HI, body)
            dve.wait_ge(s.stats, B)

        @block.gpsimd
        def _(pool):
            pool.wait_ge(s.zero, 2)

            def body(t, p):
                if not valid(t):
                    return
                wait(pool, s.qv, 4 * (t - 1))
                wait(pool, s.km, 2 * t)
                pool.tensor_copy(cur[:, p, :], m.ctxT[:, t, :]).then_inc(s.ctxc, 1)
                wait(pool, s.sc, 4 * (t - 1))
                wait(pool, s.ctxc, t + 1)
                for i in range(2):
                    rows = slice(64 * i, 64 * i + 64)
                    wait(pool, s.km, 2 * t + i)
                    pool.tensor_copy(kblk[rows, p, :, i, :], m.kT_wide[rows, t, :, :]).then_inc(s.km, 1)

            walk(pool, B, LO, HI, body)

        @block.scalar
        def _(act):
            def body(t, p):
                for g in range(NG):
                    b = t - 1
                    u = 4 * b + g
                    if g == 0 and valid(t):
                        wait(act, s.xt, t + 1)
                        wait(act, s.qv, 4 * (t - 2) + 2)
                        act.activation(xnT[:, p, :], pR[:, 0, :], ACT.Copy).then_inc(s.xtc, 1)
                    bt, gt = group(t, g, 2)
                    if valid(bt):
                        v = 4 * bt + gt
                        wait(act, s.pt, v + 1)
                        wait(act, s.pv, v - 1)
                        act.activation(probT[:, g % 2, :, :], pT[g % 2][0:K, :, :], ACT.Copy).then_inc(s.ptc, 1)
                    if valid(b):
                        wait(act, s.sub, u + 1)
                        act.activation(prob[:, g % 2, :, :], prob[:, g % 2, :, :], ACT.Exp).then_inc(s.ex, 1)
                    bo, go = group(t, g, 4)
                    if valid(bo):
                        v = 4 * bo + go
                        wait(act, s.ot, v + 1)
                        wait(act, s.y, v - 1)
                        act.activation(attT[:, go % 2, :, :], pR[:, 1:3, :], ACT.Copy).then_inc(s.otc, 1)
                    if g in (1, 2) and valid(t):
                        wait(act, s.qv, 4 * t + g)
                        wait(act, s.sc, 4 * (t - 1))
                        act.activation(qT[:, p, 4 * (g - 1):4 * g, :], pQV[:, :].rearrange("p (c n) -> p c n", c=4),
                                       ACT.Copy, scale=float(HD) ** -0.5).then_inc(s.qve, 1)

            walk(act, N, LO, HI, body)


def fp8_linear(nc, ctx, m):
    s = Sems(nc, ctx, "lin", "x8 xb xt xtc y yc yb res stats")
    G = 4
    NS = B // G
    with ExitStack() as tmp, nc.Block() as block:
        sb = lambda n, sh, dt=F32: tmp.enter_context(nc.sbuf_tensor(f"lin_{n}", sh, dt))
        x8, xb, xbT = sb("x8", [128, 2, G, 128], FP8), sb("xb", [128, 2, G, 128], BF16), sb("xbT", [128, 2, G, 128], BF16)
        y16, yb = sb("y16", [128, 2, G, 128], F16), sb("yb", [128, 2, G, 128])
        pX = [tmp.enter_context(nc.psum_tensor(f"lin_pX{i}", [128, 2 * G, 128], BF16)) for i in range(2)]
        pY = [tmp.enter_context(nc.psum_tensor(f"lin_pY{i}", [128, G, 128], F32)) for i in range(2)]

        @block.tensor
        def _(pe):
            for t in range(NS + 1):
                if t < NS:
                    wait(pe, s.xb, t + 1)
                    wait(pe, s.xtc, t - 1)
                    for i in range(G):
                        ins = pe.transpose(pX[t % 2][:, i, :], xb[:, t % 2, i, :], m.ident16[:, :])
                    ins.then_inc(s.xt, 1)
                if t >= 1:
                    q = (t - 1) % 2
                    wait(pe, s.xtc, t)
                    wait(pe, s.yc, t - 2)
                    for i in range(G):
                        ins = pe.matmul(pY[q][:, i, :], xbT[:, q, i, :], m.ffn_wT[:, :], start=True, stop=True)
                    ins.then_inc(s.y, 1)

        @block.scalar
        def _(act):
            for t in range(NS + 1):
                if t < NS:
                    wait(act, s.xt, t + 1)
                    wait(act, s.y, t - 1)
                    act.activation(xbT[:, t % 2, :, :], pX[t % 2][:, 0:G, :], ACT.Copy).then_inc(s.xtc, 1)
                if t >= 1:
                    q = (t - 1) % 2
                    wait(act, s.y, t)
                    wait(act, s.yb, t - 2)
                    act.activation(y16[:, q, :, :], pY[q][:, :, :], ACT.Copy).then_inc(s.yc, 1)

        @block.gpsimd
        def _(pool):
            for t in range(NS):
                q = t % 2
                wait(pool, s.yc, t + 1)
                wait(pool, s.res, t - 1)
                pool.tensor_tensor(yb[:, q, :, :], y16[:, q, :, :], m.ffn_bias[:, :].unsqueeze(1).broadcast_to([128, G, 128]),
                                   ALU.add).then_inc(s.yb, 1)

        @block.vector
        def _(dve):
            row_scale(dve, m)
            for t in range(NS + 2):
                if t < NS:
                    for i in range(G):
                        ins = normalise(dve, m, x8[:, t % 2, i, :], G * t + i, saturate=False)
                    ins.then_inc(s.x8, 1)
                    wait(dve, s.x8, t + 1)
                    wait(dve, s.xt, t - 1)
                    dve.tensor_copy(xb[:, t % 2, :, :], x8[:, t % 2, :, :]).then_inc(s.xb, 1)
                if t >= 2:
                    k, rows = t - 2, slice(G * (t - 2), G * (t - 1))
                    wait(dve, s.yb, k + 1)
                    dve.tensor_tensor(m.x[:, rows, :], m.x[:, rows, :], yb[:, k % 2, :, :], ALU.add).then_inc(s.res, 1)
                    wait(dve, s.res, k + 1)
                    for i in range(G):
                        row_stats(dve, m, s.stats, G * k + i)
            dve.wait_ge(s.stats, B)


def gated_scan(nc, ctx, m):
    s = Sems(nc, ctx, "scan", "xn xt xtc pr th in2 h ht res stats")
    with ExitStack() as tmp, nc.Block() as block:
        sb = lambda n, sh, dt=F32: tmp.enter_context(nc.sbuf_tensor(f"scan_{n}", sh, dt))
        pb = lambda n, sh, dt=F32: tmp.enter_context(nc.psum_tensor(f"scan_{n}", sh, dt))
        xn, xnT = sb("xn", [128, 2, 128]), sb("xnT", [128, 2, 128])
        th = sb("th", [128, 2, 3, 128])
        inp, a, h = sb("inp", [128, 2, 128]), sb("a", [128, 2, 128]), sb("h", [128, 2, 128])
        pX, pG = [pb(f"pX{i}", [128, 512]) for i in range(2)], [pb(f"pG{i}", [128, 4, 128]) for i in range(2)]
        pH = [pb(f"pH{i}", [128, 512]) for i in range(2)]
        N, LO, HI = B + 3, 6, 16

        @block.tensor
        def _(pe):
            def body(t, p):
                if valid(t):
                    wait(pe, s.xn, t + 1)
                    wait(pe, s.xtc, t - 1)
                    pe.transpose(pX[p][:, 0:128], xn[:, p, :], m.ident[:, :]).then_inc(s.xt, 1)
                b, q = t - 1, (p + 1) % 2
                if valid(b):
                    wait(pe, s.xtc, b + 1)
                    wait(pe, s.th, b - 1)
                    for i, w in enumerate((m.wg, m.wvs, m.wd)):
                        ins = pe.matmul(pG[q][:, i, :], w[:, :], xnT[:, q, :], start=True, stop=True)
                    ins.then_inc(s.pr, 1)
                b = t - 3
                if valid(b):
                    wait(pe, s.h, b + 1)
                    wait(pe, s.res, b - 1)
                    pe.transpose(pH[q][:, 0:128], h[:, q, :], m.ident[:, :]).then_inc(s.ht, 1)
            walk(pe, N, LO, HI, body)

        @block.scalar
        def _(act):
            def body(t, p):
                if valid(t):
                    wait(act, s.xt, t + 1)
                    wait(act, s.pr, t - 1)
                    act.activation(xnT[:, p, :], pX[p][:, 0:128], ACT.Copy).then_inc(s.xtc, 1)
                b, q = t - 1, (p + 1) % 2
                if valid(b):
                    wait(act, s.pr, b + 1)
                    wait(act, s.in2, 2 * (b - 1))
                    act.activation(th[:, q, 0, :], pG[q][:, 0, :], ACT.Tanh, bias=m.half_b[:, 0:1], scale=0.5)
                    act.activation(th[:, q, 1, :], pG[q][:, 1, :], ACT.Tanh, bias=m.vec[:, BV:BV + 1])
                    act.activation(th[:, q, 2, :], pG[q][:, 2, :], ACT.Tanh, bias=m.half_b[:, 1:2], scale=0.5).then_inc(s.th, 1)
            walk(act, N, LO, HI, body)

        @block.vector
        def _(dve):
            row_scale(dve, m)

            def body(t, p):
                if valid(t):
                    wait(dve, s.xt, t - 1)
                    normalise(dve, m, xn[:, p, :], t).then_inc(s.xn, 1)
                b, q = t - 2, p
                if valid(b):
                    wait(dve, s.th, b + 1)
                    wait(dve, s.h, b - 1)
                    dve.scalar_tensor_tensor(out=inp[:, q, :], in0=th[:, q, 0, :], scalar=1.0, in1=th[:, q, 1, :],
                                             op0=ALU.add, op1=ALU.mult).then_inc(s.in2, 1)
                    dve.tensor_scalar(a[:, q, :], th[:, q, 2, :], 0.499, 0.5, ALU.mult, ALU.add).then_inc(s.in2, 1)
                    wait(dve, s.in2, 2 * b + 2)
                    wait(dve, s.ht, b - 1)
                    dve.tensor_tensor_scan(h[:, q, :], a[:, q, :], inp[:, q, :], 0.0, ALU.mult, ALU.add).then_inc(s.h, 1)
                b, q = t - 3, (p + 1) % 2
                if valid(b):
                    wait(dve, s.ht, b + 1)
                    dve.scalar_tensor_tensor(out=m.x[:, b, :], in0=pH[q][:, 0:128], scalar=0.5, in1=m.x[:, b, :],
                                             op0=ALU.mult, op1=ALU.add).then_inc(s.res, 1)
                    wait(dve, s.res, b + 1)
                    row_stats(dve, m, s.stats, b)
            walk(dve, N, LO, HI, body)
            dve.wait_ge(s.stats, B)


def route(nc, ctx, m):
    s = Sems(nc, ctx, "rt", "xn xt xtc lg lt mc md sub exc exd sd rd dn dt dtc sl slc rs")
    with ExitStack() as tmp, nc.Block() as block:
        sb = lambda n, sh, dt=F32: tmp.enter_context(nc.sbuf_tensor(f"rt_{n}", sh, dt))
        pb = lambda n: tmp.enter_context(nc.psum_tensor(f"rt_{n}", [128, 4, 128], F32))
        xn, xnT = sb("xn", [128, 2, 128]), sb("xnT", [128, 2, 128])
        disp, dispT = sb("disp", [128, 2, ES]), sb("dispT", [128, 2, 4, 128])
        mc, md = sb("mc", [128, 2]), sb("md", [128, 2, 4])
        sd = sb("sd", [128, 2, 4])
        ssq, rn = sb("ssq", [128, B]), sb("rn", [128, B])
        pX, pL, pLT, pD, pSl = pb("pX"), [pb("pL0"), pb("pL1")], [pb("pLT0"), pb("pLT1")], pb("pD"), pb("pSl")
        flat = lambda x: x[:, :, :].rearrange("p a b -> p (a b)")
        N, LO, HI = B + 3, 6, 16

        @block.tensor
        def _(pe):
            def body(t, p):
                if valid(t):
                    wait(pe, s.xn, t + 1)
                    wait(pe, s.xtc, t)
                    pe.transpose(pX[:, 0, :], xn[:, p, :], m.ident[:, :]).then_inc(s.xt, 1)
                b, q = t - 2, p
                if valid(b):
                    wait(pe, s.dn, b + 1)
                    wait(pe, s.dtc, b)
                    for c in range(4):
                        ins = pe.transpose(pD[:, c, :], dispT[:, q, c, :], m.ident[:, :])
                    ins.then_inc(s.dt, 1)
                b, q = t - 1, (p + 1) % 2
                if valid(b):
                    wait(pe, s.xtc, b + 1)
                    wait(pe, s.sub, b - 1)
                    for c in range(4):
                        ins = pe.matmul(pLT[q][:, c, :], m.snT[:, 128 * c:128 * c + 128], xnT[:, q, :], start=True, stop=True)
                    ins.then_inc(s.lt, 1)
                    wait(pe, s.exc, b - 1)
                    pe.matmul(flat(pL[q]), xnT[:, q, :], m.snT[:, :], start=True, stop=True).then_inc(s.lg, 1)
                b, q = t - 2, p
                if valid(b):
                    wait(pe, s.dtc, b + 1)
                    wait(pe, s.slc, b)
                    wait(pe, s.rs, b + 1)
                    pe.matmul(flat(pSl), m.xkeep[:, q, :], disp[:, q, :], start=True, stop=True).then_inc(s.sl, 1)
            walk(pe, N, LO, HI, body)

        @block.vector
        def _(dve):
            row_scale(dve, m)
            link = linker(dve, m.s_link, m.link_count)
            link(dve.tensor_tensor(ssq[:, :], m.rstd[:, :], m.rstd[:, :], ALU.mult))
            link(dve.tensor_tensor(ssq[:, :], ssq[:, :], m.mv[:, :, 1], ALU.mult))
            link(dve.tensor_scalar(ssq[:, :], ssq[:, :], float(D), 1e-24, ALU.mult, ALU.max))
            rsqrt(dve, link, rn[:, :], ssq[:, :], m.tmp16[:, :])
            link(dve.tensor_tensor(m.rstd[:, :], m.rstd[:, :], rn[:, :], ALU.mult))
            link(dve.tensor_scalar(m.rstd[:, :], m.rstd[:, :], float(D) ** 0.5, None, ALU.mult))

            def body(t, p):
                if valid(t):
                    wait(dve, s.xt, t - 1)
                    normalise(dve, m, xn[:, p, :], t).then_inc(s.xn, 1)
                b, q = t - 1, (p + 1) % 2
                if valid(b):
                    wait(dve, s.lt, b + 1)
                    dve.tensor_reduce(md[:, q, :], pLT[q][:, :, :], AX.X, ALU.max).then_inc(s.md, 1)
                    wait(dve, s.lg, b + 1)
                    wait(dve, s.exc, b - 1)
                    dve.tensor_reduce(mc[:, q:q + 1], flat(pL[q]), AX.X, ALU.max, negate=True).then_inc(s.mc, 1)
                    wait(dve, s.md, b + 1)
                    wait(dve, s.dt, b - 1)
                    dve.tensor_tensor(dispT[:, q, :, :], pLT[q][:, :, :], md[:, q, :].unsqueeze(2).broadcast_to([128, 4, 128]),
                                      ALU.subtract).then_inc(s.sub, 1)
                    wait(dve, s.sl, b - 1)
                    dve.tensor_copy(m.xkeep[:, q, :], xn[:, q, :]).then_inc(s.rs, 1)
                    wait(dve, s.exd, b + 1)
                    dve.tensor_reduce(sd[:, q, :], dispT[:, q, :, :], AX.X, ALU.add).then_inc(s.sd, 1)
                    wait(dve, s.sd, b + 1)
                    dve.reciprocal(sd[:, q, :], sd[:, q, :]).then_inc(s.rd, 1)
                    wait(dve, s.rd, b + 1)
                    dve.tensor_tensor(dispT[:, q, :, :], dispT[:, q, :, :], sd[:, q, :].unsqueeze(2).broadcast_to([128, 4, 128]),
                                      ALU.mult).then_inc(s.dn, 1)
                b, q = t - 2, p
                if valid(b):
                    wait(dve, s.sl, b + 1)
                    dve.tensor_scalar(m.slotsT[:, :, b, :], flat(pSl).rearrange("p (e s) -> p e s", e=E),
                                      m.vec[:, GAMMA:GAMMA + 1], None, ALU.mult).then_inc(s.slc, 1)
            walk(dve, N, LO, HI, body)
            dve.wait_ge(s.slc, B)

        @block.scalar
        def _(act):
            def body(t, p):
                if valid(t):
                    wait(act, s.xt, t + 1)
                    wait(act, s.lg, t - 1)
                    act.activation(xnT[:, p, :], pX[:, 0, :], ACT.Copy).then_inc(s.xtc, 1)
                b, q = t - 2, p
                if valid(b):
                    wait(act, s.dt, b + 1)
                    wait(act, s.sl, b - 1)
                    act.activation(disp[:, q, :], flat(pD), ACT.Copy).then_inc(s.dtc, 1)
                b, q = t - 1, (p + 1) % 2
                if valid(b):
                    wait(act, s.mc, b + 1)
                    wait(act, s.sub, b + 1)
                    act.activation(dispT[:, q, :, :], dispT[:, q, :, :], ACT.Exp).then_inc(s.exd, 1)
                    act.activation(m.comb[:, :, b, :], flat(pL[q]).rearrange("p (e s) -> p e s", e=E), ACT.Exp, bias=mc[:, q:q + 1],
                                   accum_out=m.comb_sum[:, bass.ds(b, 1)]).then_inc(s.exc, 1)
            walk(act, N, LO, HI, body)


def experts(nc, ctx, m, d):
    s = Sems(nc, ctx, "ex", "h hc eo eoc b1 w1a w1b w2a w2b b2")
    NS = B * SL
    NQ = B // 2
    with ExitStack() as tmp, nc.Block() as block:
        sb = lambda n, sh, dt=F32: tmp.enter_context(nc.sbuf_tensor(f"ex_{n}", sh, dt))
        w1, w2 = sb("w1", [128, 2, HID]), sb("w2", [128, 2, NHC, 128])
        b2 = sb("b2", [128, E, 128])
        b1 = sb("b1", [128, 2, NHC])
        hT = sb("hT", [128, 2, NHC, NS])
        pH = [tmp.enter_context(nc.psum_tensor(f"ex_pH{i}", [128, 512], F32)) for i in range(4)]
        pE = [tmp.enter_context(nc.psum_tensor(f"ex_pE{i}", [128, 4, 128], F32)) for i in range(2)]
        w1s, w2s = (s.w1a, s.w1b), (s.w2a, s.w2b)

        def run(eng, body):
            body(0, 0)
            body(1, 1)
            with eng.Fori(1, E // 2) as r:
                body(2 * r, 0)
                body(2 * r + 1, 1)
            body(E, 0)

        inside = lambda e: not isinstance(e, int) or 0 <= e < E

        @block.sync
        def _(sp):
            sp.dma_start(b2[:, :, :], d.L1_ffn_b2.partition_broadcast(128)).then_inc(s.b2, 16)

            def body(e, q):
                if inside(e):
                    wait(sp, s.h, 8 * (e - 1))
                    sp.dma_start(w1[:, q, :], d.L1_ffn_w1[e]).then_inc(w1s[q], 16)
                    wait(sp, s.eo, 2 * (e - 1))
                    sp.dma_start(w2[:, q, :, :], d.L1_ffn_w2[e].rearrange("(c p) f -> p c f", p=128)).then_inc(w2s[q], 16)
            run(sp, body)

        @block.tensor
        def _(pe):
            def body(e, q):
                if inside(e):
                    wait(pe, w1s[q], 8 * (e - q) + 16)
                    for c in range(NHC):
                        for k in range(2):
                            n = 2 * c + k
                            wait(pe, s.hc, 8 * e + n - 3)
                            pe.matmul(pH[n % 4][:, :], w1[:, q, 128 * c:128 * c + 128],
                                      m.slotsT[:, e, 8 * k:8 * k + 8, :], start=True, stop=True).then_inc(s.h, 1)
                e1, q1 = e - 1, (q + 1) % 2
                if inside(e1):
                    wait(pe, w2s[q1], 8 * (e1 - q1) + 16)
                    wait(pe, s.hc, 8 * e1 + 8)
                    for r in range(2):
                        wait(pe, s.eoc, 2 * e1 + r - 1)
                        for j in range(4):
                            k = 4 * r + j
                            for c in range(NHC):
                                ins = pe.matmul(pE[r][:, j, :], hT[:, q1, c, 128 * k:128 * k + 128], w2[:, q1, c, :],
                                                start=c == 0, stop=c == NHC - 1)
                        ins.then_inc(s.eo, 1)
            run(pe, body)

        @block.scalar
        def _(act):
            def body(e, q):
                if inside(e):
                    wait(act, s.eo, 2 * (e - 1))
                    wait(act, s.b1, e + 1)
                    for c in range(NHC):
                        for k in range(2):
                            n = 2 * c + k
                            wait(act, s.h, 8 * e + n + 1)
                            act.activation(hT[:, q, c, 512 * k:512 * k + 512], pH[n % 4][:, :], ACT.Gelu,
                                           bias=b1[:, q, c:c + 1]).then_inc(s.hc, 1)
            run(act, body)

        @block.vector
        def _(dve):
            dve.wait_ge(s.b2, 16)

            def body(e, q):
                if inside(e):
                    wait(dve, s.hc, 8 * (e - 1))
                    dve.tensor_copy(b1[:, q, :], m.b1[:, e, :]).then_inc(s.b1, 1)
                e1 = e - 1
                if inside(e1):
                    for r in range(2):
                        wait(dve, s.eo, 2 * e1 + r + 1)
                        dve.tensor_tensor(m.eo[:, e1, 4 * r:4 * r + 4, :], pE[r][:, :, :],
                                          b2[:, e1, :].unsqueeze(1).broadcast_to([128, 4, 128]), ALU.add).then_inc(s.eoc, 1)
            run(dve, body)
            dve.wait_ge(s.eoc, 2 * E)


def combine(nc, ctx, m, out):
    s = Sems(nc, ctx, "cb", "rc ct ctc y res out")
    NQ = B // 2
    with ExitStack() as tmp, nc.Block() as block:
        sb = lambda n, sh, dt=F32: tmp.enter_context(nc.sbuf_tensor(f"cb_{n}", sh, dt))
        pb = lambda n: tmp.enter_context(nc.psum_tensor(f"cb_{n}", [128, 4, 128], F32))
        combT = sb("combT", [128, 2, E, 128])
        rc = sb("rc", [128, B])
        res = sb("res", [128, B, 128])
        pC, pY = [pb(f"pC{i}") for i in range(4)], [pb(f"pY{i}") for i in range(4)]

        @block.tensor
        def _(pe):
            for k in range(NQ + 1):
                if k < NQ:
                    for r in range(2):
                        n = 2 * k + r
                        wait(pe, s.ctc, n - 3)
                        for j in range(4):
                            e = 4 * r + j
                            ins = pe.transpose(pC[n % 4][:, j, :], m.comb[:, e, 2 * k:2 * k + 2, :], m.ident[:, :])
                        ins.then_inc(s.ct, 1)
                if k >= 1:
                    kk = k - 1
                    wait(pe, s.ctc, 2 * kk + 2)
                    for i in range(2):
                        b = 2 * kk + i
                        wait(pe, s.res, b - 3)
                        rows = slice(SL * i, SL * i + SL)
                        for e in range(E):
                            ins = pe.matmul(pY[b % 4][:, 0, :], combT[rows, kk % 2, e, :], m.eo[rows, e, kk, :],
                                            start=e == 0, stop=e == E - 1)
                        ins.then_inc(s.y, 1)

        @block.scalar
        def _(act):
            for n in range(2 * NQ):
                k, r = divmod(n, 2)
                act.wait_ge(s.ct, n + 1)
                wait(act, s.y, 2 * (k - 1))
                act.activation(combT[:, k % 2, 4 * r:4 * r + 4, :], pC[n % 4][:, :, :], ACT.Copy).then_inc(s.ctc, 1)

        @block.vector
        def _(dve):
            dve.reciprocal(rc[:, :], m.comb_sum[:, :]).then_inc(s.rc, 1)
            dve.wait_ge(s.rc, 1)
            for b in range(B):
                dve.wait_ge(s.y, b + 1)
                dve.scalar_tensor_tensor(out=res[:, b, :], in0=pY[b % 4][:, 0, :], scalar=rc[:, b:b + 1], in1=m.x[:, b, :],
                                         op0=ALU.mult, op1=ALU.add).then_inc(s.res, 1)

        @block.sync
        def _(sp):
            for k in range(4):
                sp.wait_ge(s.res, 4 * k + 4)
                sp.dma_start(out[4 * k:4 * k + 4].rearrange("b t f -> t b f"), res[:, 4 * k:4 * k + 4, :]).then_inc(s.out, 16)
            sp.wait_ge(s.out, 64)


def decoder_program(nc, d, out):
    ctx = ExitStack()
    with ctx:
        m = Memory()
        sb = lambda n, sh, dt=F32: ctx.enter_context(nc.sbuf_tensor(n, sh, dt))
        sem = lambda n: ctx.enter_context(nc.semaphore(n))
        m.x = sb("x", [128, B, 128])
        m.mv, m.bn = sb("mv", [128, B, 2]), sb("bn", [128, B, 6])
        m.rstd, m.veps, m.tmp16 = sb("rstd", [128, B]), sb("veps", [128, B]), sb("tmp16", [128, B])
        m.ident, m.ident16, m.ones = sb("ident_s", [128, 128]), sb("ident16", [128, 128], BF16), sb("ones", [128, 4 * C2])
        m.vec = sb("vec", [128, N_ROWS + E * NHC])
        m.b1 = m.vec[:, B1:].rearrange("p (e c) -> p e c", c=NHC)
        m.half_b, m.gg = sb("half_b", [128, 3]), sb("gg", [128, 1])
        m.snT = sb("snT", [128, ES])
        m.ffn_wT, m.ffn_bias = sb("ffn_wT", [128, 128], BF16), sb("ffn_bias", [128, 128])
        m.wg, m.wvs, m.wd = sb("wg", [128, 128]), sb("wvs", [128, 128]), sb("wd", [128, 128])
        m.wq1, m.wv1, m.wo1 = sb("wq1", [128, 128]), sb("wv1", [128, 128]), sb("wo1", [128, 128])
        m.bv1, m.bo1 = sb("bv1", [1, 128]), sb("bo1", [1, 128])
        m.xkeep = sb("xkeep", [128, 2, 128])
        m.s_weights, m.s_causal, m.s_link, m.s_ones = sem("weights"), sem("causal"), sem("link"), sem("ones_set")
        m.all_weights = 16 * 15
        m.link_count, m.ones_base = [0], 0
        with ExitStack() as attn:
            sa = lambda n, sh, dt=F32: attn.enter_context(nc.sbuf_tensor(n, sh, dt))
            m.ctxT = sa("ctxT", [128, B, C2])
            m.kT1 = sa("kT1", [128, B, C2])
            m.headmask = sa("headmask_s", [128, HG, 128])
            with ExitStack() as first:
                sf = lambda n, sh, dt=F32: first.enter_context(nc.sbuf_tensor(n, sh, dt))
                m.wqk, m.rope = sf("wqk", [128, 4, 128]), sf("rope_s", [128, 2, 2, 128])
                m.wv0, m.wo0 = sf("wv0", [128, 128]), sf("wo0", [128, 128])
                m.causal, m.xmask = sf("causal", [128, HG, 128], BF16), sf("xmask", [128, HG, C2], BF16)
                m.kT_wide = sf("kT_wide", [128, B, NCH, C2])
                m.wq_wide, m.wv_wide = sf("wq_wide", [128, H * HD]), sf("wv_wide", [128, H * HD])
                m.wo_wide = sf("wo_wide", [128, NCH, 128])
                load_block(nc, ctx, m, d)
                narrow_attention(nc, ctx, m, "self", S, False)
                wide_attention(nc, ctx, m)
            fp8_linear(nc, ctx, m)
            gated_scan(nc, ctx, m)
            narrow_attention(nc, ctx, m, "cross", C2, True)
        m.comb, m.comb_sum = sb("comb", [128, E, B, SL]), sb("comb_sum", [128, B])
        m.slotsT = sb("slotsT", [128, E, B, SL])
        route(nc, ctx, m)
        m.eo = sb("eo", [128, E, B // 2, 128])
        experts(nc, ctx, m, d)
        combine(nc, ctx, m, out)


def shape_constants():
    inv = (1.0 / np.float32(10000.0) ** (np.arange(0, DK, 2, dtype=np.float32) / np.float32(DK))).astype(np.float32)
    theta = (np.arange(S, dtype=np.float32)[:, None] * inv[None, :]).astype(np.float32)
    cos = np.repeat(np.cos(theta), 2, axis=-1).T
    sin = np.repeat(np.sin(theta), 2, axis=-1).T
    scale = np.float32(1.0) / np.sqrt(np.float32(DK))
    rope = np.empty((D, 2, 2, S), np.float32)
    for i, table in enumerate((cos, sin)):
        rope[:, i, 0] = np.tile(table, (H, 1)) * scale
        rope[:, i, 1] = np.tile(table, (H, 1))
    head = (np.arange(D) // DK) % HG
    headmask = (head[:, None, None] == np.arange(HG)[None, :, None]) * np.ones((1, 1, 128))
    return {"ident": np.eye(128, dtype=np.float32), "rope": rope, "headmask": headmask.astype(np.float32)}


_INS = ["x", "ctx_1024", "mask_SxS2_bk1", "L0_attn_Wq", "L0_attn_Wk", "L0_attn_Wv", "L0_attn_Wo", "L0_xattn_W_q",
        "L0_xattn_W_k", "L0_xattn_W_v", "L0_xattn_W_o", "L0_ffn_weight", "L0_ffn_bias", "L1_attn_Wg", "L1_attn_bg",
        "L1_attn_Wv", "L1_attn_bv", "L1_attn_Wd", "L1_attn_bd", "L1_xattn_Wq", "L1_xattn_bq", "L1_xattn_Wk",
        "L1_xattn_bk", "L1_xattn_Wv", "L1_xattn_bv", "L1_xattn_Wo", "L1_xattn_bo", "L1_ffn_norm_gamma",
        "L1_ffn_slot_norm_gamma", "L1_ffn_slot_embeds", "L1_ffn_w1", "L1_ffn_b1", "L1_ffn_w2", "L1_ffn_b2"]


def kernel(**inputs):
    import concourse.bacc as _bacc
    from concourse.bass_utils import run_bass_kernel_spmd as _run

    nc = _bacc.Bacc("TRN2", target_bir_lowering=False, num_devices=1)
    arrays, aps = {}, {}
    consts = shape_constants()
    for name in _INS + sorted(consts):
        a = np.ascontiguousarray(consts[name] if name in consts else inputs[name])
        arrays[f"in_{name}_dram"] = a
        dtype = U8 if a.dtype == np.bool_ else mybir.dt.from_np(a.dtype)
        aps[name] = nc.dram_tensor(f"in_{name}_dram", a.shape, dtype, kind="ExternalInput").ap()
    out = nc.dram_tensor("out_0_dram", (B, S, D), F32, kind="ExternalOutput").ap()
    decoder_program(nc, namedtuple("Inputs", sorted(aps))(**aps), out)
    r = _run(nc, [arrays], core_ids=[0])
    return r.results[0]["out_0_dram"]
```

```python
from collections import namedtuple
from contextlib import ExitStack

import numpy as np
import concourse.bass as bass
from concourse import mybir

F32, BF16, F16, I32, U8 = (mybir.dt.float32, mybir.dt.bfloat16, mybir.dt.float16, mybir.dt.int32, mybir.dt.uint8)
FP8 = mybir.dt.float8e4
ALU = mybir.AluOpType
ACT = mybir.ActivationFunctionType
AX = mybir.AxisListType

B, S, D = 16, 128, 128
H, DK = 16, 8
HD = 64
C2 = 77
NG, HG = 4, 4
NCH = H * HD // 128
E, SL, HID = 8, 64, 512
NHC = HID // 128
ES = E * SL
EPS = 1e-5
MASKED = -float(2.0 ** 100)
RSQRT_MAGIC = 1597463007.0

BG, BV, BD, BQ, GAMMA, SGAMMA, B1 = range(7)
N_ROWS = B1


def wait(eng, sem, value):
    if isinstance(value, int) and value <= 0:
        return
    eng.wait_ge(sem, value)


def valid(b):
    return not isinstance(b, int) or 0 <= b < B


def walk(eng, n, lo, hi, body):
    assert lo % 2 == 0 and (hi - lo) % 2 == 0
    for t in range(lo):
        body(t, t % 2)
    with eng.Fori(lo // 2, hi // 2) as r:
        body(2 * r, 0)
        body(2 * r + 1, 1)
    for t in range(hi, n):
        body(t, t % 2)


def Sems(nc, ctx, prefix, names):
    return namedtuple("Sems", names)(*[ctx.enter_context(nc.semaphore(f"{prefix}_{n}")) for n in names.split()])


class Memory:
    pass


def rsqrt(dve, link, y, v, t):
    link(dve.tensor_scalar(y.bitcast(I32), v.bitcast(I32), 1, None, ALU.logical_shift_right))
    link(dve.tensor_scalar(y.bitcast(I32), y.bitcast(I32), -1.0, RSQRT_MAGIC, ALU.mult, ALU.add))
    for _ in range(4):
        link(dve.tensor_tensor(t, y, y, ALU.mult))
        link(dve.tensor_tensor(t, t, v, ALU.mult))
        link(dve.tensor_scalar(t, t, -0.5, 1.5, ALU.mult, ALU.add))
        link(dve.tensor_tensor(y, y, t, ALU.mult))


def linker(dve, sem, count):
    def link(ins):
        count[0] += 1
        ins.then_inc(sem, 1)
        dve.wait_ge(sem, count[0])
    return link


def row_scale(dve, m):
    link = linker(dve, m.s_link, m.link_count)
    for b in range(B):
        ins = dve.bn_aggr(m.mv[:, b, :], m.bn[:, b, :])
    link(ins)
    link(dve.tensor_scalar(m.veps[:, :], m.mv[:, :, 1], EPS, None, ALU.add))
    rsqrt(dve, link, m.rstd[:, :], m.veps[:, :], m.tmp16[:, :])


def row_stats(dve, m, sem, b):
    dve.bn_stats(m.bn[:, b, :], m.x[:, b, :]).then_inc(sem, 1)


def normalise(dve, m, out, b, **how):
    return dve.tensor_scalar(out, m.x[:, b, :], m.mv[:, b, 0:1], m.rstd[:, bass.ds(b, 1)], ALU.subtract, ALU.mult, **how)


def load_block(nc, ctx, m, d):
    s = Sems(nc, ctx, "ld", "x0 x1 x2 x3 ctx ident small self_w cross_w keys_w prep stats ctx_t ctx_tc vec_t vec_c wt wt_c "
             "kT kTc sn sn_t sn_c bf rot slots mask")
    s_x = (s.x0, s.x1, s.x2, s.x3)
    rows = (d.L1_attn_bg, d.L1_attn_bv, d.L1_attn_bd, d.L1_xattn_bq, d.L1_ffn_norm_gamma, d.L1_ffn_slot_norm_gamma)
    KB = 4
    kraw = B // KB * (NCH + 1)
    with ExitStack() as tmp, nc.Block() as block:
        sb = lambda n, sh, dt: tmp.enter_context(nc.sbuf_tensor(n, sh, dt))
        ps = [tmp.enter_context(nc.psum_tensor(f"ld_ps{i}", [128, 512], F32)) for i in range(4)]
        ctx_raw = sb("ctx_raw", [C2, B, D], F32)
        vec_rows = sb("vec_rows", [N_ROWS + E * NHC, 128], F32)
        w_raw = sb("ffn_w_raw", [128, 128], F32)
        w_clip = sb("ffn_w_clip", [128, 2, 128], F32)
        w8 = sb("ffn_w8", [128, 2, 128], FP8)
        w_val = sb("ffn_w_val", [128, 2, 128], F32)
        w_big = sb("ffn_w_big", [128, 128], F32)
        wk_wide = sb("wk_wide", [128, H * HD], F32)
        wk_narrow = sb("wk_narrow", [128, 128], F32)
        bk_row = sb("bk_row", [1, 128], F32)
        slots = sb("slots", [128, 4, 128], F32)
        slots2 = sb("slots2", [128, 4, 128], F32)
        ss = sb("slot_ss", [128, 4], F32)
        rs = sb("slot_rs", [128, 4], F32)
        t4 = sb("slot_t", [128, 4], F32)
        mask8 = sb("mask8", [128, C2], U8)

        @block.sync
        def _(sp):
            for g in range(4):
                sp.dma_start(m.x[:, 4 * g:4 * g + 4, :], d.x[4 * g:4 * g + 4].rearrange("b t f -> t b f")).then_inc(s_x[g], 16)
            sp.dma_start(ctx_raw[:, :, :], d.ctx_1024.rearrange("b k f -> k b f")).then_inc(s.ctx, 16)
            sp.dma_start(wk_wide[:, :], d.L0_xattn_W_k).then_inc(s.keys_w, 16)
            sp.dma_start(wk_narrow[:, :], d.L1_xattn_Wk).then_inc(s.keys_w, 16)
            sp.dma_start(bk_row[:, :], d.L1_xattn_bk.rearrange("(a n) -> a n", a=1)).then_inc(s.keys_w, 16)
            sp.dma_start(slots[:, :, :], d.L1_ffn_slot_embeds.rearrange("(c e) s f -> (e s) c f", c=4)).then_inc(s.slots, 16)
            sp.dma_start(m.wq_wide[:, :], d.L0_xattn_W_q).then_inc(m.s_weights, 16)
            sp.dma_start(m.wv_wide[:, :], d.L0_xattn_W_v).then_inc(m.s_weights, 16)
            sp.dma_start(m.wo_wide[:, :, :], d.L0_xattn_W_o.rearrange("(c p) f -> p c f", p=128)).then_inc(m.s_weights, 16)
            for dst, src in ((m.wg, d.L1_attn_Wg), (m.wvs, d.L1_attn_Wv), (m.wd, d.L1_attn_Wd), (m.wq1, d.L1_xattn_Wq),
                             (m.wv1, d.L1_xattn_Wv), (m.wo1, d.L1_xattn_Wo)):
                sp.dma_start(dst[:, :], src).then_inc(m.s_weights, 16)

        @block.scalar
        def _(act):
            act.dma_start(m.ident[:, :], d.ident).then_inc(s.ident, 16)
            act.dma_start(m.wqk[:, 0, :], d.L0_attn_Wq).then_inc(s.self_w, 16)
            act.dma_start(m.wqk[:, 1, :], d.L0_attn_Wk).then_inc(s.self_w, 16)
            act.dma_start(m.rope[:, :, :, :], d.rope).then_inc(s.self_w, 16)
            act.dma_start(m.wv0[:, :], d.L0_attn_Wv).then_inc(m.s_weights, 16)
            act.dma_start(m.wo0[:, :], d.L0_attn_Wo).then_inc(m.s_weights, 16)
            act.dma_start(m.headmask[:, :, :], d.headmask).then_inc(m.s_weights, 16)
            act.dma_start(w_raw[:, :], d.L0_ffn_weight).then_inc(s.small, 16)
            act.dma_start(m.ffn_bias[:, :], d.L0_ffn_bias.partition_broadcast(128)).then_inc(m.s_weights, 16)
            act.dma_start(mask8[:, :], d.mask_SxS2_bk1).then_inc(s.mask, 16)
            for i, vec in enumerate(rows):
                act.dma_start(vec_rows[i:i + 1, :], vec.rearrange("(a n) -> a n", a=1)).then_inc(s.cross_w, 16)
            act.dma_start(vec_rows[N_ROWS:, :], d.L1_ffn_b1.rearrange("e (c p) -> (e c) p", p=128)).then_inc(s.cross_w, 16)
            act.dma_start(m.bv1[:, :], d.L1_xattn_bv.rearrange("(a n) -> a n", a=1)).then_inc(m.s_weights, 16)
            act.dma_start(m.bo1[:, :], d.L1_xattn_bo.rearrange("(a n) -> a n", a=1)).then_inc(m.s_weights, 16)
            for g in range(4):
                act.wait_ge(s.ctx_t, g + 1)
                act.activation(m.ctxT[:, 4 * g:4 * g + 4, :], ps[g % 2][:, 0:4 * C2].rearrange("p (b k) -> p b k", b=4),
                               ACT.Copy).then_inc(s.ctx_tc, 1)
            act.wait_ge(s.vec_t, 1)
            act.activation(m.vec[:, :], ps[2][:, 0:N_ROWS + E * NHC], ACT.Copy).then_inc(s.vec_c, 1)
            for i in range(kraw):
                g, c = divmod(i, NCH + 1)
                act.wait_ge(s.kT, i + 1)
                src = ps[i % 2][:, 0:KB * C2].rearrange("p (b k) -> p b k", b=KB)
                dst = m.kT_wide[:, KB * g:KB * g + KB, c, :] if c < NCH else m.kT1[:, KB * g:KB * g + KB, :]
                act.activation(dst, src, ACT.Copy).then_inc(s.kTc, 1)
            act.wait_ge(s.wt, 1)
            act.activation(m.ffn_wT[:, :], ps[2][:, 0:128], ACT.Copy).then_inc(s.wt_c, 1)
            act.wait_ge(s.sn_t, 1)
            act.wait_ge(s.prep, 7)
            act.activation(m.snT[:, :], ps[3][:, :], ACT.Copy, scale=m.gg[:, 0:1]).then_inc(s.sn_c, 1)

        @block.tensor
        def _(pe):
            pe.wait_ge(s.ident, 16)
            pe.wait_ge(s.ctx, 16)
            for g in range(4):
                wait(pe, s.ctx_tc, g - 1)
                for i in range(4):
                    ins = pe.transpose(ps[g % 2][:, i * C2:(i + 1) * C2], ctx_raw[:, 4 * g + i, :], m.ident[0:C2, 0:C2])
                ins.then_inc(s.ctx_t, 1)
            pe.wait_ge(s.cross_w, 16 * (N_ROWS + 1))
            n = N_ROWS + E * NHC
            pe.transpose(ps[2][:, 0:n], vec_rows[:, :], m.ident[0:n, 0:n]).then_inc(s.vec_t, 1)
            pe.wait_ge(s.keys_w, 48)
            pe.wait_ge(s.ctx_tc, 4)
            pe.wait_ge(s.prep, 1)
            for i in range(kraw):
                g, c = divmod(i, NCH + 1)
                wait(pe, s.kTc, i - 1)
                keys = m.ctxT[:, KB * g:KB * g + KB, :]
                w = wk_wide[:, c * 128:(c + 1) * 128] if c < NCH else wk_narrow[:, :]
                ins = pe.matmul(ps[i % 2][:, 0:KB * C2], w, keys, start=True, stop=c < NCH)
                if c == NCH:
                    ins = pe.matmul(ps[i % 2][:, 0:KB * C2], bk_row[0:1, :], m.ones[0:1, 0:KB * C2], start=False, stop=True)
                ins.then_inc(s.kT, 1)
            pe.wait_ge(s.vec_c, 1)
            pe.wait_ge(s.prep, 5)
            pe.transpose(ps[2][:, 0:128], w_val[:, 0, :], m.ident[:, :]).then_inc(s.wt, 1)
            pe.wait_ge(s.prep, 6)
            for c in range(4):
                ins = pe.transpose(ps[3][:, c * 128:(c + 1) * 128], slots2[:, c, :], m.ident[:, :])
            ins.then_inc(s.sn_t, 1)

        @block.gpsimd
        def _(pool):
            pool.memset(m.causal[:, :, :], 0.0).then_inc(s.mask, 1)
            pool.wait_ge(s.mask, 17)
            pool.affine_select(out=m.causal[:, :, :], in_=m.causal[:, :, :], compare_op=ALU.is_ge, fill=MASKED, base=0,
                               pattern=[[0, HG], [-1, 128]], channel_multiplier=1).then_inc(m.s_causal, 1)

        @block.vector
        def _(dve):
            link = linker(dve, m.s_link, m.link_count)
            dve.memset(m.ones[:, :], 1.0).then_inc(s.prep, 1)
            dve.wait_ge(s.ident, 16)
            dve.tensor_copy(m.ident16[:, :], m.ident[:, :]).then_inc(s.bf, 1)
            dve.wait_ge(s.self_w, 48)
            for i in range(2):
                w = m.wqk[:, i, :].rearrange("p (n two) -> p n two", two=2)
                r = m.wqk[:, 2 + i, :].rearrange("p (n two) -> p n two", two=2)
                dve.tensor_scalar(r[:, :, 0], w[:, :, 1], -1.0, None, ALU.mult).then_inc(s.rot, 1)
                dve.tensor_copy(r[:, :, 1], w[:, :, 0]).then_inc(s.rot, 1)
            for b in range(B):
                if b % 4 == 0:
                    dve.wait_ge(s_x[b // 4], 16)
                row_stats(dve, m, s.stats, b)
            dve.wait_ge(s.small, 16)
            link(dve.tensor_scalar(w_clip[:, 0, :], w_raw[:, :], 240.0, -240.0, ALU.min, ALU.max))
            link(dve.tensor_scalar(w_clip[:, 1, :], w_raw[:, :], 448.0, -448.0, ALU.min, ALU.max))
            link(dve.tensor_copy(w8[:, 0, :], w_clip[:, 0, :], saturate=False))
            link(dve.tensor_scalar(w8[:, 1, :], w_clip[:, 1, :], 0.5, None, ALU.mult, saturate=False))
            link(dve.tensor_copy(w_val[:, 0, :], w8[:, 0, :]))
            link(dve.tensor_scalar(w_val[:, 1, :], w8[:, 1, :], 2.0, None, ALU.mult))
            link(dve.tensor_tensor(w_big[:, :], w_raw[:, :], w_raw[:, :], ALU.mult))
            link(dve.tensor_scalar(w_big[:, :], w_big[:, :], 128.0 ** 2, None, ALU.is_gt))
            dve.copy_predicated(w_val[:, 0, :], w_big[:, :].bitcast(I32), w_val[:, 1, :]).then_inc(s.prep, 4)
            dve.wait_ge(s.slots, 16)
            link(dve.tensor_tensor(slots2[:, :, :], slots[:, :, :], slots[:, :, :], ALU.mult))
            link(dve.tensor_reduce(ss[:, :], slots2[:, :, :], AX.X, ALU.add))
            link(dve.tensor_scalar(ss[:, :], ss[:, :], 1e-24, None, ALU.max))
            rsqrt(dve, link, rs[:, :], ss[:, :], t4[:, :])
            link(dve.tensor_scalar(rs[:, :], rs[:, :], float(D) ** 0.5, None, ALU.mult))
            dve.tensor_tensor(slots2[:, :, :], slots[:, :, :], rs[:, :].unsqueeze(2).broadcast_to([128, 4, 128]),
                              ALU.mult).then_inc(s.prep, 1)
            dve.wait_ge(s.vec_c, 1)
            dve.tensor_tensor(m.gg[:, :], m.vec[:, GAMMA:GAMMA + 1], m.vec[:, SGAMMA:SGAMMA + 1], ALU.mult).then_inc(s.prep, 1)
            dve.tensor_scalar(m.half_b[:, 0:1], m.vec[:, BG:BG + 1], 0.5, None, ALU.mult).then_inc(s.bf, 1)
            dve.tensor_scalar(m.half_b[:, 1:2], m.vec[:, BD:BD + 1], 0.5, None, ALU.mult).then_inc(s.bf, 1)
            dve.tensor_scalar(m.half_b[:, 2:3], m.vec[:, BQ:BQ + 1], float(DK) ** -0.5, None, ALU.mult).then_inc(s.bf, 1)
            dve.wait_ge(s.mask, 17)
            for i in range(HG):
                dve.tensor_scalar(m.xmask[:, i, :], mask8[:, :], MASKED, None, ALU.mult).then_inc(s.bf, 1)
            dve.wait_ge(s.stats, B)
            dve.wait_ge(s.bf, 4 + HG)
            dve.wait_ge(s.rot, 4)


def narrow_attention(nc, ctx, m, name, K, cross):
    s = Sems(nc, ctx, name, "xn xt xtc proj rope1 q km vp v sc mx ex pt ptc pv rec rx rt rtc at y res stats ctxc zero")
    wv, wo = (m.wv1, m.wo1) if cross else (m.wv0, m.wo0)
    with ExitStack() as tmp, nc.Block() as block:
        sb = lambda n, sh, dt=F32: tmp.enter_context(nc.sbuf_tensor(f"{name}_{n}", sh, dt))
        pb = lambda n, sh, dt=F32: tmp.enter_context(nc.psum_tensor(f"{name}_{n}", sh, dt))
        xn, xnT = sb("xn", [128, 2, 128]), sb("xnT", [128, 2, 128])
        rot = sb("rot", [128, 2, 2, 128])
        qk = sb("qk", [128, 2, 2, 128])
        kmask = sb("kmask", [128, 2, HG, K])
        vpad = sb("vpad", [K, 2, NG, (HG + 1) * 32])
        cur = sb("cur", [128, 2, C2])
        prob = sb("prob", [128, 2, HG, K])
        probT = sb("probT", [K, 2, HG, 128])
        mx = sb("mx", [128, 2, HG])
        sums, rec, rec_wide = sb("sums", [128, 2, H]), sb("rec", [128, H]), sb("rec_wide", [128, 128])
        attT = sb("attT", [128, 128])
        pS = [pb(f"pS{i}", [128, HG, 128]) for i in range(2)]
        pT = [pb(f"pT{i}", [128, HG, 128]) for i in range(2)]
        pO = [pb(f"pO{i}", [128, 512]) for i in range(2)]
        pP, pX = pb("pP", [128, 4, 128]), pb("pX", [128, 4, 128])
        XT, V, RT, Y = range(4)
        SC = lambda g: pS[g % 2][:, :, :].rearrange("p a b -> p (a b)")[:, 0:HG * K].rearrange("p (a b) -> p a b", a=HG)

        N = B + 2
        LO, HI = 4, 16

        @block.tensor
        def _(pe):
            pe.wait_ge(m.s_weights, m.all_weights)
            pe.wait_ge(m.s_causal, 1)
            pe.wait_ge(s.zero, 2)

            def body(t, p):
                for g in range(NG):
                    b, q = t - 1, (p + 1) % 2
                    u = 4 * b + g
                    if valid(b):
                        if g == 0:
                            wait(pe, s.km, b + 1)
                            wait(pe, s.q, b + 1)
                        wait(pe, s.ex, u - 1)
                        rows = slice(32 * g, 32 * g + 32)
                        ins = pe.matmul(SC(g), qk[rows, q, 0, :], kmask[rows, q, :, :], start=True, stop=cross)
                        if not cross:
                            ins = pe.matmul(SC(g), m.ident16[:, :], m.causal[:, :, :], start=False, stop=True)
                        ins.then_inc(s.sc, 1)
                    bt, gt = (b, g - 2) if g >= 2 else (b - 1, g + 2)
                    if valid(bt):
                        v = 4 * bt + gt
                        wait(pe, s.ex, v + 1)
                        wait(pe, s.ptc, v - 1)
                        for i in range(HG):
                            ins = pe.transpose(pT[g % 2][0:K, i, :], prob[:, g % 2, i, :], m.ident[:, :])
                        ins.then_inc(s.pt, 1)
                    bp, gp, qp = (b, 0, q) if g == 3 else (b - 1, g + 1, p)
                    if valid(bp):
                        v = 4 * bp + gp
                        wait(pe, s.ptc, v + 1)
                        if gp == 0:
                            wait(pe, s.v, bp + 1)
                            wait(pe, s.at, bp - 1)
                        for i in range(HG):
                            ins = pe.matmul(pO[qp][32 * gp:32 * gp + 32, 0:128], vpad[:, qp, gp, 32 * i:32 * i + 32],
                                            probT[:, gp % 2, i, :], start=i == 0, stop=i == HG - 1)
                        ins.then_inc(s.pv, 1)
                    if g == 0 and valid(t):
                        wait(pe, s.xn, t + 1)
                        wait(pe, s.res, t - 2)
                        wait(pe, s.v, t)
                        pe.transpose(pX[:, XT, :], xn[:, p, :], m.ident[:, :]).then_inc(s.xt, 1)
                    if g == 1 and valid(t):
                        wait(pe, s.xtc, t + 1)
                        if cross:
                            wait(pe, s.q, t)
                            pe.matmul(pP[:, 0, :], m.wq1[:, :], xnT[:, p, :], start=True, stop=True).then_inc(s.proj, 1)
                            wait(pe, s.ctxc, t + 1)
                            pe.matmul(pX[0:K, V, :], cur[:, p, :], wv[:, :], start=True, stop=False)
                            pe.matmul(pX[0:K, V, :], m.ones[0:1, 0:K], m.bv1[:, :], start=False, stop=True).then_inc(s.vp, 1)
                        else:
                            wait(pe, s.rope1, 2 * t)
                            for i in range(4):
                                ins = pe.matmul(pP[:, i, :], m.wqk[:, i, :], xnT[:, p, :], start=True, stop=True)
                            ins.then_inc(s.proj, 1)
                            pe.matmul(pX[:, V, :], xnT[:, p, :], wv[:, :], start=True, stop=True).then_inc(s.vp, 1)
                    if g == 2 and valid(t - 2):
                        wait(pe, s.rx, t - 1)
                        wait(pe, s.v, t + 1 if not isinstance(t, int) or t < B else B)
                        pe.transpose(pX[:, RT, :], rec_wide[:, :], m.ident[:, :]).then_inc(s.rt, 1)
                    if g == 3 and valid(t - 2):
                        wait(pe, s.at, t - 1)
                        ins = pe.matmul(pX[:, Y, :], attT[:, :], wo[:, :], start=True, stop=not cross)
                        if cross:
                            ins = pe.matmul(pX[:, Y, :], m.ones[0:1, 0:128], m.bo1[:, :], start=False, stop=True)
                        ins.then_inc(s.y, 1)

            walk(pe, N, LO, HI, body)

        @block.vector
        def _(dve):
            row_scale(dve, m)

            def body(t, p):
                if valid(t):
                    wait(dve, s.xt, t - 1)
                    normalise(dve, m, xn[:, p, :], t).then_inc(s.xn, 1)
                for g in range(NG):
                    b = t - 1
                    u = 4 * b + g
                    if valid(b):
                        wait(dve, s.sc, u + 1)
                        wait(dve, s.ex, u - 1)
                        dve.tensor_reduce(mx[:, g % 2, :], SC(g), AX.X, ALU.max, negate=True).then_inc(s.mx, 1)
                    if g == 0 and valid(t - 3):
                        wait(dve, s.y, t - 2)
                        dve.tensor_tensor(m.x[:, t - 3, :], m.x[:, t - 3, :], pX[:, Y, :], ALU.add).then_inc(s.res, 1)
                    if g == 1 and valid(t - 3):
                        wait(dve, s.res, t - 2)
                        row_stats(dve, m, s.stats, t - 3)
                    if g == 1 and valid(t - 2):
                        wait(dve, s.ex, 4 * (t - 2) + 4)
                        wait(dve, s.rx, t - 2)
                        dve.reciprocal(rec[:, :], sums[:, p, :]).then_inc(s.rec, 1)
                        wait(dve, s.rec, t - 1)
                        wait(dve, s.rt, t - 2)
                        dve.tensor_copy(rec_wide[:, :].rearrange("p (h w) -> p h w", h=H),
                                        rec[:, :].unsqueeze(2).broadcast_to([128, H, DK])).then_inc(s.rx, 1)
                    if g == 1 and valid(t) and not cross:
                        wait(dve, s.proj, t + 1)
                        wait(dve, s.q, t)
                        dve.tensor_tensor(rot[:, 0, :, :], pP[:, 0:2, :], m.rope[:, 0, :, :], ALU.mult).then_inc(s.rope1, 1)
                        dve.tensor_tensor(rot[:, 1, :, :], pP[:, 2:4, :], m.rope[:, 1, :, :], ALU.mult).then_inc(s.rope1, 1)
                        wait(dve, s.rope1, 2 * t + 2)
                        wait(dve, s.sc, 4 * (t - 1))
                        wait(dve, s.km, t - 1)
                        dve.tensor_tensor(qk[:, p, :, :], rot[:, 0, :, :], rot[:, 1, :, :], ALU.add).then_inc(s.q, 1)
                    if g == 3 and valid(t - 2):
                        wait(dve, s.pv, 4 * (t - 2) + 4)
                        wait(dve, s.rt, t - 1)
                        wait(dve, s.y, t - 2)
                        dve.tensor_copy(attT[:, :], pX[:, RT, :]).then_inc(s.rtc, 1)
                        wait(dve, s.rtc, t - 1)
                        dve.tensor_tensor(attT[:, :], pO[p][:, 0:128], attT[:, :], ALU.mult).then_inc(s.at, 1)

            walk(dve, N, LO, HI, body)
            wait(dve, s.y, B)
            dve.tensor_tensor(m.x[:, B - 1, :], m.x[:, B - 1, :], pX[:, Y, :], ALU.add).then_inc(s.res, 1)
            dve.wait_ge(s.res, B)
            row_stats(dve, m, s.stats, B - 1)
            dve.wait_ge(s.stats, B)

        @block.gpsimd
        def _(pool):
            for q in range(2):
                pool.memset(vpad[:, q, :, :], 0.0).then_inc(s.zero, 1)
            pool.wait_ge(s.zero, 2)

            def body(t, p):
                if not valid(t):
                    return
                if cross:
                    wait(pool, s.vp, t - 1)
                    pool.tensor_copy(cur[:, p, :], m.ctxT[:, t, :]).then_inc(s.ctxc, 1)
                    k = m.kT1[:, t, :]
                else:
                    wait(pool, s.q, t + 1)
                    k = qk[:, p, 1, :]
                wait(pool, s.sc, 4 * (t - 1))
                pool.tensor_tensor(kmask[:, p, :, :], k.unsqueeze(1).broadcast_to([128, HG, K]), m.headmask[:, :, 0:K],
                                   ALU.mult).then_inc(s.km, 1)

            walk(pool, B, LO, HI, body)

        @block.scalar
        def _(act):
            act.wait_ge(s.zero, 2)

            def body(t, p):
                for g in range(NG):
                    b, q = t - 1, (p + 1) % 2
                    u = 4 * b + g
                    bt, gt = (b, g - 2) if g >= 2 else (b - 1, g + 2)
                    if valid(bt):
                        v = 4 * bt + gt
                        wait(act, s.pt, v + 1)
                        wait(act, s.pv, v - 1)
                        act.activation(probT[:, g % 2, :, :], pT[g % 2][0:K, :, :], ACT.Copy).then_inc(s.ptc, 1)
                    if valid(b):
                        wait(act, s.mx, u + 1)
                        wait(act, s.pt, u - 1)
                        if g == 0:
                            wait(act, s.rec, b - 1)
                        for i in range(HG):
                            h = HG * g + i
                            ins = act.activation(prob[:, g % 2, i, :], SC(g)[:, i, :], ACT.Exp, bias=mx[:, g % 2, i:i + 1],
                                                 accum_out=sums[:, q, h:h + 1])
                        ins.then_inc(s.ex, 1)
                    if g == 0 and valid(t):
                        wait(act, s.xt, t + 1)
                        wait(act, s.vp, t - 1)
                        wait(act, s.proj, t - 1)
                        act.activation(xnT[:, p, :], pX[:, XT, :], ACT.Copy).then_inc(s.xtc, 1)
                    if g == 1 and valid(t):
                        wait(act, s.vp, t + 1)
                        wait(act, s.pv, 4 * (t - 1))
                        heads = vpad[:, p, :, :].rearrange("p g (i w) -> p g i w", w=40)[:, :, :, 0:DK]
                        act.activation(heads, pX[0:K, V, :].rearrange("p (g i w) -> p g i w", g=NG, i=HG),
                                       ACT.Copy).then_inc(s.v, 1)
                        if cross:
                            wait(act, s.proj, t + 1)
                            wait(act, s.sc, 4 * (t - 1))
                            act.activation(qk[:, p, 0, :], pP[:, 0, :], ACT.Identity, bias=m.half_b[:, 2:3],
                                           scale=float(DK) ** -0.5).then_inc(s.q, 1)

            walk(act, N, LO, HI, body)


def wide_attention(nc, ctx, m):
    name, K = "wide", C2
    s = Sems(nc, ctx, name, "xn xt xtc qv qve km ctxc sc mx ex rec nrm pt ptc pv otc y res stats zero")
    with ExitStack() as tmp, nc.Block() as block:
        sb = lambda n, sh, dt=F32: tmp.enter_context(nc.sbuf_tensor(f"{name}_{n}", sh, dt))
        pb = lambda n, sh, dt=F32: tmp.enter_context(nc.psum_tensor(f"{name}_{n}", sh, dt))
        xn, xnT = sb("xn", [128, 2, 128]), sb("xnT", [128, 2, 128])
        qT = sb("qT", [128, 2, NCH, 128])
        kblk = sb("kblk", [128, 2, NCH, 2, K])
        vx = sb("vx", [K, 2, H * HD])
        cur = sb("cur", [128, 2, K])
        prob = sb("prob", [128, 2, HG, K])
        probT = sb("probT", [K, 2, HG, 128])
        mx, sums, rec = sb("mx", [128, 2, HG]), sb("sums", [128, 2, HG]), sb("rec", [128, 2, HG])
        attT = sb("attT", [128, 2, 2, 128])
        pS = [pb(f"pS{i}", [128, 512]) for i in range(2)]
        pT = [pb(f"pT{i}", [128, HG, 128]) for i in range(2)]
        pO = [pb(f"pO{i}", [128, 4, 128]) for i in range(2)]
        pQV, pX = pb("pQV", [128, 512]), pb("pX", [128, 4, 128])
        XT, Y = pX[:, 0, :], pX[:, 1, :]
        SC = lambda g: pS[g % 2][:, 0:HG * K].rearrange("p (a b) -> p a b", a=HG)

        N = B + 3
        LO, HI = 4, 16

        def group(t, g, lag):
            back = (g - lag) // NG
            return t - 1 + back, (g - lag) % NG

        def round_of(t, g):
            return (t - 1, 3, 1) if g == 0 else (t, g - 1, 0)

        @block.tensor
        def _(pe):
            pe.wait_ge(s.zero, 2)

            def body(t, p):
                for g in range(NG):
                    b, q = t - 1, (p + 1) % 2
                    u = 4 * b + g
                    if valid(b):
                        if g == 0:
                            wait(pe, s.km, 2 * b + 2)
                            wait(pe, s.qve, 4 * b + 2)
                        wait(pe, s.ex, u - 1)
                        for i in range(2):
                            c = 2 * g + i
                            pe.matmul(pS[g % 2][:, 2 * K * i:2 * K * (i + 1)], qT[:, q, c, :], kblk[:, q, c, :, :],
                                      start=i == 0, stop=False, skip_group_check=True)
                        pe.matmul(SC(g), m.ident16[:, :], m.xmask[:, :, :], start=False, stop=True,
                                  skip_group_check=True).then_inc(s.sc, 1)
                    bt, gt = group(t, g, 2)
                    if valid(bt):
                        v = 4 * bt + gt
                        wait(pe, s.nrm, v + 1)
                        wait(pe, s.ptc, v - 1)
                        for i in range(HG):
                            ins = pe.transpose(pT[g % 2][0:K, i, :], prob[:, g % 2, i, :], m.ident[:, :])
                        ins.then_inc(s.pt, 1)
                    if g == 0 and valid(t):
                        wait(pe, s.xn, t + 1)
                        wait(pe, s.res, t - 2)
                        pe.transpose(XT, xn[:, p, :], m.ident[:, :]).then_inc(s.xt, 1)
                    bp, gp = group(t, g, 3)
                    if valid(bp):
                        v = 4 * bp + gp
                        wait(pe, s.ptc, v + 1)
                        if gp == 0:
                            wait(pe, s.qve, 4 * bp + 4)
                        wait(pe, s.otc, v - 1)
                        qp = q if g == 3 else p
                        for i in range(HG):
                            h = HG * gp + i
                            ins = pe.matmul(pO[gp % 2][64 * (i % 2):64 * (i % 2) + 64, i // 2, :], vx[:, qp, HD * h:HD * h + HD],
                                            probT[:, gp % 2, i, :], start=True, stop=True)
                        ins.then_inc(s.pv, 1)
                    by, gy = group(t, g, 4)
                    if valid(by):
                        v = 4 * by + gy
                        wait(pe, s.otc, v + 1)
                        if gy == 0:
                            wait(pe, s.res, by)
                            wait(pe, s.xtc, t + 1 if not isinstance(t, int) or t < B else B)
                        for i in range(2):
                            ins = pe.matmul(Y, attT[:, gy % 2, i, :], m.wo_wide[:, 2 * gy + i, :],
                                            start=gy == 0 and i == 0, stop=gy == 3 and i == 1)
                        ins.then_inc(s.y, 1)
                    bv, k, late = round_of(t, g)
                    if valid(bv):
                        if k == 0:
                            wait(pe, s.xtc, t + 1)
                        if k == 2:
                            wait(pe, s.ctxc, t + 1)
                        wait(pe, s.qve, 4 * bv + k)
                        if k >= 2:
                            half = 512 * (k - 2)
                            ins = pe.matmul(pQV[0:K, :], cur[:, (p + late) % 2, :], m.wv_wide[:, half:half + 512],
                                            start=True, stop=True)
                        else:
                            for i in range(4):
                                c = 4 * k + i
                                ins = pe.matmul(pQV[:, 128 * i:128 * i + 128], m.wq_wide[:, 128 * c:128 * c + 128],
                                                xnT[:, p, :], start=True, stop=True)
                        ins.then_inc(s.qv, 1)

            walk(pe, N, LO, HI, body)

        @block.vector
        def _(dve):
            row_scale(dve, m)

            def body(t, p):
                if valid(t):
                    wait(dve, s.xt, t - 1)
                    normalise(dve, m, xn[:, p, :], t).then_inc(s.xn, 1)
                for g in range(NG):
                    b = t - 1
                    u = 4 * b + g
                    if valid(b):
                        wait(dve, s.sc, u + 1)
                        wait(dve, s.ex, u - 1)
                        dve.tensor_reduce(mx[:, g % 2, :], SC(g), AX.X, ALU.max, negate=True).then_inc(s.mx, 1)
                    if g == 0 and valid(t - 3):
                        wait(dve, s.y, 4 * (t - 3) + 4)
                        dve.tensor_tensor(m.x[:, t - 3, :], m.x[:, t - 3, :], Y, ALU.add).then_inc(s.res, 1)
                    if g == 1 and valid(t - 3):
                        wait(dve, s.res, t - 2)
                        row_stats(dve, m, s.stats, t - 3)
                    bv, k, late = round_of(t, g)
                    if k >= 2 and valid(bv):
                        wait(dve, s.qv, 4 * bv + k + 1)
                        if k == 2:
                            wait(dve, s.pv, 4 * (t - 1))
                        half = 512 * (k - 2)
                        dve.tensor_copy(vx[:, (p + late) % 2, half:half + 512], pQV[0:K, :]).then_inc(s.qve, 1)
                    bn, gn = group(t, g, 1)
                    if valid(bn):
                        v = 4 * bn + gn
                        wait(dve, s.ex, v + 1)
                        wait(dve, s.nrm, v - 1)
                        dve.reciprocal(rec[:, gn % 2, :], sums[:, gn % 2, :]).then_inc(s.rec, 1)
                        wait(dve, s.rec, v + 1)
                        dve.tensor_tensor(prob[:, gn % 2, :, :], prob[:, gn % 2, :, :],
                                          rec[:, gn % 2, :].unsqueeze(2).broadcast_to([128, HG, K]), ALU.mult).then_inc(s.nrm, 1)

            walk(dve, N, LO, HI, body)
            dve.wait_ge(s.stats, B)

        @block.gpsimd
        def _(pool):
            for q in range(2):
                pool.memset(kblk[:, q, :, :, :], 0.0).then_inc(s.zero, 1)
            pool.wait_ge(s.zero, 2)

            def body(t, p):
                if not valid(t):
                    return
                wait(pool, s.qv, 4 * (t - 1))
                wait(pool, s.km, 2 * t)
                pool.tensor_copy(cur[:, p, :], m.ctxT[:, t, :]).then_inc(s.ctxc, 1)
                wait(pool, s.sc, 4 * (t - 1))
                wait(pool, s.ctxc, t + 1)
                for i in range(2):
                    rows = slice(64 * i, 64 * i + 64)
                    wait(pool, s.km, 2 * t + i)
                    pool.tensor_copy(kblk[rows, p, :, i, :], m.kT_wide[rows, t, :, :]).then_inc(s.km, 1)

            walk(pool, B, LO, HI, body)

        @block.scalar
        def _(act):
            def body(t, p):
                for g in range(NG):
                    b = t - 1
                    u = 4 * b + g
                    bt, gt = group(t, g, 2)
                    if valid(bt):
                        v = 4 * bt + gt
                        wait(act, s.pt, v + 1)
                        wait(act, s.pv, v - 1)
                        act.activation(probT[:, g % 2, :, :], pT[g % 2][0:K, :, :], ACT.Copy).then_inc(s.ptc, 1)
                    if g == 0 and valid(t):
                        wait(act, s.xt, t + 1)
                        wait(act, s.qv, 4 * (t - 2) + 2)
                        act.activation(xnT[:, p, :], XT, ACT.Copy).then_inc(s.xtc, 1)
                    if valid(b):
                        wait(act, s.mx, u + 1)
                        wait(act, s.pt, u - 1)
                        wait(act, s.rec, u - 1)
                        for i in range(HG):
                            ins = act.activation(prob[:, g % 2, i, :], SC(g)[:, i, :], ACT.Exp, bias=mx[:, g % 2, i:i + 1],
                                                 accum_out=sums[:, g % 2, i:i + 1])
                        ins.then_inc(s.ex, 1)
                    bp, gp = group(t, g, 3)
                    if valid(bp):
                        v = 4 * bp + gp
                        wait(act, s.pv, v + 1)
                        wait(act, s.y, v - 1)
                        act.activation(attT[:, gp % 2, :, :], pO[gp % 2][:, 0:2, :], ACT.Copy).then_inc(s.otc, 1)
                    if g in (1, 2) and valid(t):
                        wait(act, s.qv, 4 * t + g)
                        wait(act, s.sc, 4 * (t - 1))
                        act.activation(qT[:, p, 4 * (g - 1):4 * g, :], pQV[:, :].rearrange("p (c n) -> p c n", c=4),
                                       ACT.Copy, scale=float(HD) ** -0.5).then_inc(s.qve, 1)

            walk(act, N, LO, HI, body)


def fp8_linear(nc, ctx, m):
    s = Sems(nc, ctx, "lin", "x8 xb xt xtc y yc yb res stats")
    G = 4
    NS = B // G
    with ExitStack() as tmp, nc.Block() as block:
        sb = lambda n, sh, dt=F32: tmp.enter_context(nc.sbuf_tensor(f"lin_{n}", sh, dt))
        x8, xb, xbT = sb("x8", [128, 2, G, 128], FP8), sb("xb", [128, 2, G, 128], BF16), sb("xbT", [128, 2, G, 128], BF16)
        y16, yb = sb("y16", [128, 2, G, 128], F16), sb("yb", [128, 2, G, 128])
        pX = [tmp.enter_context(nc.psum_tensor(f"lin_pX{i}", [128, 2 * G, 128], BF16)) for i in range(2)]
        pY = [tmp.enter_context(nc.psum_tensor(f"lin_pY{i}", [128, G, 128], F32)) for i in range(2)]

        @block.tensor
        def _(pe):
            for t in range(NS + 1):
                if t < NS:
                    wait(pe, s.xb, t + 1)
                    wait(pe, s.xtc, t - 1)
                    for i in range(G):
                        ins = pe.transpose(pX[t % 2][:, i, :], xb[:, t % 2, i, :], m.ident16[:, :])
                    ins.then_inc(s.xt, 1)
                if t >= 1:
                    q = (t - 1) % 2
                    wait(pe, s.xtc, t)
                    wait(pe, s.yc, t - 2)
                    for i in range(G):
                        ins = pe.matmul(pY[q][:, i, :], xbT[:, q, i, :], m.ffn_wT[:, :], start=True, stop=True)
                    ins.then_inc(s.y, 1)

        @block.scalar
        def _(act):
            for t in range(NS + 1):
                if t < NS:
                    wait(act, s.xt, t + 1)
                    wait(act, s.y, t - 1)
                    act.activation(xbT[:, t % 2, :, :], pX[t % 2][:, 0:G, :], ACT.Copy).then_inc(s.xtc, 1)
                if t >= 1:
                    q = (t - 1) % 2
                    wait(act, s.y, t)
                    wait(act, s.yb, t - 2)
                    act.activation(y16[:, q, :, :], pY[q][:, :, :], ACT.Copy).then_inc(s.yc, 1)

        @block.gpsimd
        def _(pool):
            for t in range(NS):
                q = t % 2
                wait(pool, s.yc, t + 1)
                wait(pool, s.res, t - 1)
                pool.tensor_tensor(yb[:, q, :, :], y16[:, q, :, :], m.ffn_bias[:, :].unsqueeze(1).broadcast_to([128, G, 128]),
                                   ALU.add).then_inc(s.yb, 1)

        @block.vector
        def _(dve):
            row_scale(dve, m)
            for t in range(NS + 2):
                if t < NS:
                    for i in range(G):
                        ins = normalise(dve, m, x8[:, t % 2, i, :], G * t + i, saturate=False)
                    ins.then_inc(s.x8, 1)
                    wait(dve, s.x8, t + 1)
                    wait(dve, s.xt, t - 1)
                    dve.tensor_copy(xb[:, t % 2, :, :], x8[:, t % 2, :, :]).then_inc(s.xb, 1)
                if t >= 2:
                    k, rows = t - 2, slice(G * (t - 2), G * (t - 1))
                    wait(dve, s.yb, k + 1)
                    dve.tensor_tensor(m.x[:, rows, :], m.x[:, rows, :], yb[:, k % 2, :, :], ALU.add).then_inc(s.res, 1)
                    wait(dve, s.res, k + 1)
                    for i in range(G):
                        row_stats(dve, m, s.stats, G * k + i)
            dve.wait_ge(s.stats, B)


def gated_scan(nc, ctx, m):
    s = Sems(nc, ctx, "scan", "xn xt xtc pr th in2 h ht res stats")
    with ExitStack() as tmp, nc.Block() as block:
        sb = lambda n, sh, dt=F32: tmp.enter_context(nc.sbuf_tensor(f"scan_{n}", sh, dt))
        pb = lambda n, sh, dt=F32: tmp.enter_context(nc.psum_tensor(f"scan_{n}", sh, dt))
        xn, xnT = sb("xn", [128, 2, 128]), sb("xnT", [128, 2, 128])
        th = sb("th", [128, 2, 3, 128])
        inp, a, h = sb("inp", [128, 2, 128]), sb("a", [128, 2, 128]), sb("h", [128, 2, 128])
        pX, pG = [pb(f"pX{i}", [128, 512]) for i in range(2)], [pb(f"pG{i}", [128, 4, 128]) for i in range(2)]
        pH = [pb(f"pH{i}", [128, 512]) for i in range(2)]
        N, LO, HI = B + 3, 6, 16

        @block.tensor
        def _(pe):
            def body(t, p):
                if valid(t):
                    wait(pe, s.xn, t + 1)
                    wait(pe, s.xtc, t - 1)
                    pe.transpose(pX[p][:, 0:128], xn[:, p, :], m.ident[:, :]).then_inc(s.xt, 1)
                b, q = t - 1, (p + 1) % 2
                if valid(b):
                    wait(pe, s.xtc, b + 1)
                    wait(pe, s.th, b - 1)
                    for i, w in enumerate((m.wg, m.wvs, m.wd)):
                        ins = pe.matmul(pG[q][:, i, :], w[:, :], xnT[:, q, :], start=True, stop=True)
                    ins.then_inc(s.pr, 1)
                b = t - 3
                if valid(b):
                    wait(pe, s.h, b + 1)
                    wait(pe, s.res, b - 1)
                    pe.transpose(pH[q][:, 0:128], h[:, q, :], m.ident[:, :]).then_inc(s.ht, 1)
            walk(pe, N, LO, HI, body)

        @block.scalar
        def _(act):
            def body(t, p):
                if valid(t):
                    wait(act, s.xt, t + 1)
                    wait(act, s.pr, t - 1)
                    act.activation(xnT[:, p, :], pX[p][:, 0:128], ACT.Copy).then_inc(s.xtc, 1)
                b, q = t - 1, (p + 1) % 2
                if valid(b):
                    wait(act, s.pr, b + 1)
                    wait(act, s.in2, 2 * (b - 1))
                    act.activation(th[:, q, 0, :], pG[q][:, 0, :], ACT.Tanh, bias=m.half_b[:, 0:1], scale=0.5)
                    act.activation(th[:, q, 1, :], pG[q][:, 1, :], ACT.Tanh, bias=m.vec[:, BV:BV + 1])
                    act.activation(th[:, q, 2, :], pG[q][:, 2, :], ACT.Tanh, bias=m.half_b[:, 1:2], scale=0.5).then_inc(s.th, 1)
            walk(act, N, LO, HI, body)

        @block.vector
        def _(dve):
            row_scale(dve, m)

            def body(t, p):
                if valid(t):
                    wait(dve, s.xt, t - 1)
                    normalise(dve, m, xn[:, p, :], t).then_inc(s.xn, 1)
                b, q = t - 2, p
                if valid(b):
                    wait(dve, s.th, b + 1)
                    wait(dve, s.h, b - 1)
                    dve.scalar_tensor_tensor(out=inp[:, q, :], in0=th[:, q, 0, :], scalar=1.0, in1=th[:, q, 1, :],
                                             op0=ALU.add, op1=ALU.mult).then_inc(s.in2, 1)
                    dve.tensor_scalar(a[:, q, :], th[:, q, 2, :], 0.499, 0.5, ALU.mult, ALU.add).then_inc(s.in2, 1)
                    wait(dve, s.in2, 2 * b + 2)
                    wait(dve, s.ht, b - 1)
                    dve.tensor_tensor_scan(h[:, q, :], a[:, q, :], inp[:, q, :], 0.0, ALU.mult, ALU.add).then_inc(s.h, 1)
                b, q = t - 3, (p + 1) % 2
                if valid(b):
                    wait(dve, s.ht, b + 1)
                    dve.scalar_tensor_tensor(out=m.x[:, b, :], in0=pH[q][:, 0:128], scalar=0.5, in1=m.x[:, b, :],
                                             op0=ALU.mult, op1=ALU.add).then_inc(s.res, 1)
                    wait(dve, s.res, b + 1)
                    row_stats(dve, m, s.stats, b)
            walk(dve, N, LO, HI, body)
            dve.wait_ge(s.stats, B)


def route(nc, ctx, m):
    s = Sems(nc, ctx, "rt", "xn xt xtc lg lt mc md sub exc exd sd rd dn dt dtc sl slc rs")
    with ExitStack() as tmp, nc.Block() as block:
        sb = lambda n, sh, dt=F32: tmp.enter_context(nc.sbuf_tensor(f"rt_{n}", sh, dt))
        pb = lambda n: tmp.enter_context(nc.psum_tensor(f"rt_{n}", [128, 4, 128], F32))
        xn, xnT = sb("xn", [128, 2, 128]), sb("xnT", [128, 2, 128])
        disp, dispT = sb("disp", [128, 2, ES]), sb("dispT", [128, 2, 4, 128])
        mc, md = sb("mc", [128, 2]), sb("md", [128, 2, 4])
        sd = sb("sd", [128, 2, 4])
        ssq, rn = sb("ssq", [128, B]), sb("rn", [128, B])
        pX, pL, pLT, pD, pSl = pb("pX"), [pb("pL0"), pb("pL1")], [pb("pLT0"), pb("pLT1")], pb("pD"), pb("pSl")
        flat = lambda x: x[:, :, :].rearrange("p a b -> p (a b)")
        N, LO, HI = B + 3, 6, 16

        @block.tensor
        def _(pe):
            def body(t, p):
                if valid(t):
                    wait(pe, s.xn, t + 1)
                    wait(pe, s.xtc, t)
                    pe.transpose(pX[:, 0, :], xn[:, p, :], m.ident[:, :]).then_inc(s.xt, 1)
                b, q = t - 2, p
                if valid(b):
                    wait(pe, s.dn, b + 1)
                    wait(pe, s.dtc, b)
                    for c in range(4):
                        ins = pe.transpose(pD[:, c, :], dispT[:, q, c, :], m.ident[:, :])
                    ins.then_inc(s.dt, 1)
                b, q = t - 1, (p + 1) % 2
                if valid(b):
                    wait(pe, s.xtc, b + 1)
                    wait(pe, s.sub, b - 1)
                    for c in range(4):
                        ins = pe.matmul(pLT[q][:, c, :], m.snT[:, 128 * c:128 * c + 128], xnT[:, q, :], start=True, stop=True)
                    ins.then_inc(s.lt, 1)
                    wait(pe, s.exc, b - 1)
                    pe.matmul(flat(pL[q]), xnT[:, q, :], m.snT[:, :], start=True, stop=True).then_inc(s.lg, 1)
                b, q = t - 2, p
                if valid(b):
                    wait(pe, s.dtc, b + 1)
                    wait(pe, s.slc, b)
                    wait(pe, s.rs, b + 1)
                    pe.matmul(flat(pSl), m.xkeep[:, q, :], disp[:, q, :], start=True, stop=True).then_inc(s.sl, 1)
            walk(pe, N, LO, HI, body)

        @block.vector
        def _(dve):
            row_scale(dve, m)
            link = linker(dve, m.s_link, m.link_count)
            link(dve.tensor_tensor(ssq[:, :], m.rstd[:, :], m.rstd[:, :], ALU.mult))
            link(dve.tensor_tensor(ssq[:, :], ssq[:, :], m.mv[:, :, 1], ALU.mult))
            link(dve.tensor_scalar(ssq[:, :], ssq[:, :], float(D), 1e-24, ALU.mult, ALU.max))
            rsqrt(dve, link, rn[:, :], ssq[:, :], m.tmp16[:, :])
            link(dve.tensor_tensor(m.rstd[:, :], m.rstd[:, :], rn[:, :], ALU.mult))
            link(dve.tensor_scalar(m.rstd[:, :], m.rstd[:, :], float(D) ** 0.5, None, ALU.mult))

            def body(t, p):
                if valid(t):
                    wait(dve, s.xt, t - 1)
                    normalise(dve, m, xn[:, p, :], t).then_inc(s.xn, 1)
                b, q = t - 1, (p + 1) % 2
                if valid(b):
                    wait(dve, s.lt, b + 1)
                    dve.tensor_reduce(md[:, q, :], pLT[q][:, :, :], AX.X, ALU.max).then_inc(s.md, 1)
                    wait(dve, s.lg, b + 1)
                    wait(dve, s.exc, b - 1)
                    dve.tensor_reduce(mc[:, q:q + 1], flat(pL[q]), AX.X, ALU.max, negate=True).then_inc(s.mc, 1)
                    wait(dve, s.md, b + 1)
                    wait(dve, s.dt, b - 1)
                    dve.tensor_tensor(dispT[:, q, :, :], pLT[q][:, :, :], md[:, q, :].unsqueeze(2).broadcast_to([128, 4, 128]),
                                      ALU.subtract).then_inc(s.sub, 1)
                    wait(dve, s.sl, b - 1)
                    dve.tensor_copy(m.xkeep[:, q, :], xn[:, q, :]).then_inc(s.rs, 1)
                    wait(dve, s.exd, b + 1)
                    dve.tensor_reduce(sd[:, q, :], dispT[:, q, :, :], AX.X, ALU.add).then_inc(s.sd, 1)
                    wait(dve, s.sd, b + 1)
                    dve.reciprocal(sd[:, q, :], sd[:, q, :]).then_inc(s.rd, 1)
                    wait(dve, s.rd, b + 1)
                    dve.tensor_tensor(dispT[:, q, :, :], dispT[:, q, :, :], sd[:, q, :].unsqueeze(2).broadcast_to([128, 4, 128]),
                                      ALU.mult).then_inc(s.dn, 1)
                b, q = t - 2, p
                if valid(b):
                    wait(dve, s.sl, b + 1)
                    dve.tensor_scalar(m.slotsT[:, :, b, :], flat(pSl).rearrange("p (e s) -> p e s", e=E),
                                      m.vec[:, GAMMA:GAMMA + 1], None, ALU.mult).then_inc(s.slc, 1)
            walk(dve, N, LO, HI, body)
            dve.wait_ge(s.slc, B)

        @block.scalar
        def _(act):
            def body(t, p):
                if valid(t):
                    wait(act, s.xt, t + 1)
                    wait(act, s.lg, t - 1)
                    act.activation(xnT[:, p, :], pX[:, 0, :], ACT.Copy).then_inc(s.xtc, 1)
                b, q = t - 2, p
                if valid(b):
                    wait(act, s.dt, b + 1)
                    wait(act, s.sl, b - 1)
                    act.activation(disp[:, q, :], flat(pD), ACT.Copy).then_inc(s.dtc, 1)
                b, q = t - 1, (p + 1) % 2
                if valid(b):
                    wait(act, s.mc, b + 1)
                    wait(act, s.sub, b + 1)
                    act.activation(dispT[:, q, :, :], dispT[:, q, :, :], ACT.Exp).then_inc(s.exd, 1)
                    act.activation(m.comb[:, :, b, :], flat(pL[q]).rearrange("p (e s) -> p e s", e=E), ACT.Exp, bias=mc[:, q:q + 1],
                                   accum_out=m.comb_sum[:, bass.ds(b, 1)]).then_inc(s.exc, 1)
            walk(act, N, LO, HI, body)


def experts(nc, ctx, m, d):
    s = Sems(nc, ctx, "ex", "h hc eo eoc b1 w1a w1b w2a w2b b2")
    NS = B * SL
    NQ = B // 2
    with ExitStack() as tmp, nc.Block() as block:
        sb = lambda n, sh, dt=F32: tmp.enter_context(nc.sbuf_tensor(f"ex_{n}", sh, dt))
        w1, w2 = sb("w1", [128, 2, HID]), sb("w2", [128, 2, NHC, 128])
        b2 = sb("b2", [128, E, 128])
        b1 = sb("b1", [128, 2, NHC])
        hT = sb("hT", [128, 2, NHC, NS])
        pH = [tmp.enter_context(nc.psum_tensor(f"ex_pH{i}", [128, 512], F32)) for i in range(4)]
        pE = [tmp.enter_context(nc.psum_tensor(f"ex_pE{i}", [128, 4, 128], F32)) for i in range(2)]
        w1s, w2s = (s.w1a, s.w1b), (s.w2a, s.w2b)

        def run(eng, body):
            body(0, 0)
            body(1, 1)
            with eng.Fori(1, E // 2) as r:
                body(2 * r, 0)
                body(2 * r + 1, 1)
            body(E, 0)

        inside = lambda e: not isinstance(e, int) or 0 <= e < E

        @block.sync
        def _(sp):
            sp.dma_start(b2[:, :, :], d.L1_ffn_b2.partition_broadcast(128)).then_inc(s.b2, 16)

            def body(e, q):
                if inside(e):
                    wait(sp, s.h, 8 * (e - 1))
                    sp.dma_start(w1[:, q, :], d.L1_ffn_w1[e]).then_inc(w1s[q], 16)
                    wait(sp, s.eo, 2 * (e - 1))
                    sp.dma_start(w2[:, q, :, :], d.L1_ffn_w2[e].rearrange("(c p) f -> p c f", p=128)).then_inc(w2s[q], 16)
            run(sp, body)

        @block.tensor
        def _(pe):
            def body(e, q):
                if inside(e):
                    wait(pe, w1s[q], 8 * (e - q) + 16)
                    for c in range(NHC):
                        for k in range(2):
                            n = 2 * c + k
                            wait(pe, s.hc, 8 * e + n - 3)
                            pe.matmul(pH[n % 4][:, :], w1[:, q, 128 * c:128 * c + 128],
                                      m.slotsT[:, e, 8 * k:8 * k + 8, :], start=True, stop=True).then_inc(s.h, 1)
                e1, q1 = e - 1, (q + 1) % 2
                if inside(e1):
                    wait(pe, w2s[q1], 8 * (e1 - q1) + 16)
                    wait(pe, s.hc, 8 * e1 + 8)
                    for r in range(2):
                        wait(pe, s.eoc, 2 * e1 + r - 1)
                        for j in range(4):
                            k = 4 * r + j
                            for c in range(NHC):
                                ins = pe.matmul(pE[r][:, j, :], hT[:, q1, c, 128 * k:128 * k + 128], w2[:, q1, c, :],
                                                start=c == 0, stop=c == NHC - 1)
                        ins.then_inc(s.eo, 1)
            run(pe, body)

        @block.scalar
        def _(act):
            def body(e, q):
                if inside(e):
                    wait(act, s.eo, 2 * (e - 1))
                    wait(act, s.b1, e + 1)
                    for c in range(NHC):
                        for k in range(2):
                            n = 2 * c + k
                            wait(act, s.h, 8 * e + n + 1)
                            act.activation(hT[:, q, c, 512 * k:512 * k + 512], pH[n % 4][:, :], ACT.Gelu,
                                           bias=b1[:, q, c:c + 1]).then_inc(s.hc, 1)
            run(act, body)

        @block.vector
        def _(dve):
            dve.wait_ge(s.b2, 16)

            def body(e, q):
                if inside(e):
                    wait(dve, s.hc, 8 * (e - 1))
                    dve.tensor_copy(b1[:, q, :], m.b1[:, e, :]).then_inc(s.b1, 1)
                e1 = e - 1
                if inside(e1):
                    for r in range(2):
                        wait(dve, s.eo, 2 * e1 + r + 1)
                        dve.tensor_tensor(m.eo[:, e1, 4 * r:4 * r + 4, :], pE[r][:, :, :],
                                          b2[:, e1, :].unsqueeze(1).broadcast_to([128, 4, 128]), ALU.add).then_inc(s.eoc, 1)
            run(dve, body)
            dve.wait_ge(s.eoc, 2 * E)


def combine(nc, ctx, m, out):
    s = Sems(nc, ctx, "cb", "rc ct ctc y res out")
    NQ = B // 2
    with ExitStack() as tmp, nc.Block() as block:
        sb = lambda n, sh, dt=F32: tmp.enter_context(nc.sbuf_tensor(f"cb_{n}", sh, dt))
        pb = lambda n: tmp.enter_context(nc.psum_tensor(f"cb_{n}", [128, 4, 128], F32))
        combT = sb("combT", [128, 2, E, 128])
        rc = sb("rc", [128, B])
        res = sb("res", [128, B, 128])
        pC, pY = [pb(f"pC{i}") for i in range(4)], [pb(f"pY{i}") for i in range(4)]

        @block.tensor
        def _(pe):
            for k in range(NQ + 1):
                if k < NQ:
                    for r in range(2):
                        n = 2 * k + r
                        wait(pe, s.ctc, n - 3)
                        for j in range(4):
                            e = 4 * r + j
                            ins = pe.transpose(pC[n % 4][:, j, :], m.comb[:, e, 2 * k:2 * k + 2, :], m.ident[:, :])
                        ins.then_inc(s.ct, 1)
                if k >= 1:
                    kk = k - 1
                    wait(pe, s.ctc, 2 * kk + 2)
                    for i in range(2):
                        b = 2 * kk + i
                        wait(pe, s.res, b - 3)
                        rows = slice(SL * i, SL * i + SL)
                        for e in range(E):
                            ins = pe.matmul(pY[b % 4][:, 0, :], combT[rows, kk % 2, e, :], m.eo[rows, e, kk, :],
                                            start=e == 0, stop=e == E - 1)
                        ins.then_inc(s.y, 1)

        @block.scalar
        def _(act):
            for n in range(2 * NQ):
                k, r = divmod(n, 2)
                act.wait_ge(s.ct, n + 1)
                wait(act, s.y, 2 * (k - 1))
                act.activation(combT[:, k % 2, 4 * r:4 * r + 4, :], pC[n % 4][:, :, :], ACT.Copy).then_inc(s.ctc, 1)

        @block.vector
        def _(dve):
            dve.reciprocal(rc[:, :], m.comb_sum[:, :]).then_inc(s.rc, 1)
            dve.wait_ge(s.rc, 1)
            for b in range(B):
                dve.wait_ge(s.y, b + 1)
                dve.scalar_tensor_tensor(out=res[:, b, :], in0=pY[b % 4][:, 0, :], scalar=rc[:, b:b + 1], in1=m.x[:, b, :],
                                         op0=ALU.mult, op1=ALU.add).then_inc(s.res, 1)

        @block.sync
        def _(sp):
            for k in range(4):
                sp.wait_ge(s.res, 4 * k + 4)
                sp.dma_start(out[4 * k:4 * k + 4].rearrange("b t f -> t b f"), res[:, 4 * k:4 * k + 4, :]).then_inc(s.out, 16)
            sp.wait_ge(s.out, 64)


def decoder_program(nc, d, out):
    ctx = ExitStack()
    with ctx:
        m = Memory()
        sb = lambda n, sh, dt=F32: ctx.enter_context(nc.sbuf_tensor(n, sh, dt))
        sem = lambda n: ctx.enter_context(nc.semaphore(n))
        m.x = sb("x", [128, B, 128])
        m.mv, m.bn = sb("mv", [128, B, 2]), sb("bn", [128, B, 6])
        m.rstd, m.veps, m.tmp16 = sb("rstd", [128, B]), sb("veps", [128, B]), sb("tmp16", [128, B])
        m.ident, m.ident16, m.ones = sb("ident_s", [128, 128]), sb("ident16", [128, 128], BF16), sb("ones", [128, 4 * C2])
        m.vec = sb("vec", [128, N_ROWS + E * NHC])
        m.b1 = m.vec[:, B1:].rearrange("p (e c) -> p e c", c=NHC)
        m.half_b, m.gg = sb("half_b", [128, 3]), sb("gg", [128, 1])
        m.snT = sb("snT", [128, ES])
        m.ffn_wT, m.ffn_bias = sb("ffn_wT", [128, 128], BF16), sb("ffn_bias", [128, 128])
        m.wg, m.wvs, m.wd = sb("wg", [128, 128]), sb("wvs", [128, 128]), sb("wd", [128, 128])
        m.wq1, m.wv1, m.wo1 = sb("wq1", [128, 128]), sb("wv1", [128, 128]), sb("wo1", [128, 128])
        m.bv1, m.bo1 = sb("bv1", [1, 128]), sb("bo1", [1, 128])
        m.xkeep = sb("xkeep", [128, 2, 128])
        m.s_weights, m.s_causal, m.s_link, m.s_ones = sem("weights"), sem("causal"), sem("link"), sem("ones_set")
        m.all_weights = 16 * 15
        m.link_count, m.ones_base = [0], 0
        with ExitStack() as attn:
            sa = lambda n, sh, dt=F32: attn.enter_context(nc.sbuf_tensor(n, sh, dt))
            m.ctxT = sa("ctxT", [128, B, C2])
            m.kT1 = sa("kT1", [128, B, C2])
            m.headmask = sa("headmask_s", [128, HG, 128])
            with ExitStack() as first:
                sf = lambda n, sh, dt=F32: first.enter_context(nc.sbuf_tensor(n, sh, dt))
                m.wqk, m.rope = sf("wqk", [128, 4, 128]), sf("rope_s", [128, 2, 2, 128])
                m.wv0, m.wo0 = sf("wv0", [128, 128]), sf("wo0", [128, 128])
                m.causal, m.xmask = sf("causal", [128, HG, 128], BF16), sf("xmask", [128, HG, C2], BF16)
                m.kT_wide = sf("kT_wide", [128, B, NCH, C2])
                m.wq_wide, m.wv_wide = sf("wq_wide", [128, H * HD]), sf("wv_wide", [128, H * HD])
                m.wo_wide = sf("wo_wide", [128, NCH, 128])
                load_block(nc, ctx, m, d)
                narrow_attention(nc, ctx, m, "self", S, False)
                wide_attention(nc, ctx, m)
            fp8_linear(nc, ctx, m)
            gated_scan(nc, ctx, m)
            narrow_attention(nc, ctx, m, "cross", C2, True)
        m.comb, m.comb_sum = sb("comb", [128, E, B, SL]), sb("comb_sum", [128, B])
        m.slotsT = sb("slotsT", [128, E, B, SL])
        route(nc, ctx, m)
        m.eo = sb("eo", [128, E, B // 2, 128])
        experts(nc, ctx, m, d)
        combine(nc, ctx, m, out)


def shape_constants():
    inv = (1.0 / np.float32(10000.0) ** (np.arange(0, DK, 2, dtype=np.float32) / np.float32(DK))).astype(np.float32)
    theta = (np.arange(S, dtype=np.float32)[:, None] * inv[None, :]).astype(np.float32)
    cos = np.repeat(np.cos(theta), 2, axis=-1).T
    sin = np.repeat(np.sin(theta), 2, axis=-1).T
    scale = np.float32(1.0) / np.sqrt(np.float32(DK))
    rope = np.empty((D, 2, 2, S), np.float32)
    for i, table in enumerate((cos, sin)):
        rope[:, i, 0] = np.tile(table, (H, 1)) * scale
        rope[:, i, 1] = np.tile(table, (H, 1))
    head = (np.arange(D) // DK) % HG
    headmask = (head[:, None, None] == np.arange(HG)[None, :, None]) * np.ones((1, 1, 128))
    return {"ident": np.eye(128, dtype=np.float32), "rope": rope, "headmask": headmask.astype(np.float32)}


_INS = ["x", "ctx_1024", "mask_SxS2_bk1", "L0_attn_Wq", "L0_attn_Wk", "L0_attn_Wv", "L0_attn_Wo", "L0_xattn_W_q",
        "L0_xattn_W_k", "L0_xattn_W_v", "L0_xattn_W_o", "L0_ffn_weight", "L0_ffn_bias", "L1_attn_Wg", "L1_attn_bg",
        "L1_attn_Wv", "L1_attn_bv", "L1_attn_Wd", "L1_attn_bd", "L1_xattn_Wq", "L1_xattn_bq", "L1_xattn_Wk",
        "L1_xattn_bk", "L1_xattn_Wv", "L1_xattn_bv", "L1_xattn_Wo", "L1_xattn_bo", "L1_ffn_norm_gamma",
        "L1_ffn_slot_norm_gamma", "L1_ffn_slot_embeds", "L1_ffn_w1", "L1_ffn_b1", "L1_ffn_w2", "L1_ffn_b2"]


def kernel(**inputs):
    import concourse.bacc as _bacc
    from concourse.bass_utils import run_bass_kernel_spmd as _run

    nc = _bacc.Bacc("TRN2", target_bir_lowering=False, num_devices=1)
    arrays, aps = {}, {}
    consts = shape_constants()
    for name in _INS + sorted(consts):
        a = np.ascontiguousarray(consts[name] if name in consts else inputs[name])
        arrays[f"in_{name}_dram"] = a
        dtype = U8 if a.dtype == np.bool_ else mybir.dt.from_np(a.dtype)
        aps[name] = nc.dram_tensor(f"in_{name}_dram", a.shape, dtype, kind="ExternalInput").ap()
    out = nc.dram_tensor("out_0_dram", (B, S, D), F32, kind="ExternalOutput").ap()
    decoder_program(nc, namedtuple("Inputs", sorted(aps))(**aps), out)
    r = _run(nc, [arrays], core_ids=[0])
    return r.results[0]["out_0_dram"]
```

```python
from collections import namedtuple
from contextlib import ExitStack

import numpy as np
import concourse.bass as bass
from concourse import mybir

F32, BF16, F16, I32, U8 = (mybir.dt.float32, mybir.dt.bfloat16, mybir.dt.float16, mybir.dt.int32, mybir.dt.uint8)
FP8 = mybir.dt.float8e4
ALU = mybir.AluOpType
ACT = mybir.ActivationFunctionType
AX = mybir.AxisListType

B, S, D = 16, 128, 128
H, DK = 16, 8
HD = 64
C2 = 77
NG, HG = 4, 4
NCH = H * HD // 128
E, SL, HID = 8, 64, 512
NHC = HID // 128
ES = E * SL
EPS = 1e-5
MASKED = -float(2.0 ** 100)
RSQRT_MAGIC = 1597463007.0
AHEAD = 12

BG, BV, BD, BQ, GAMMA, SGAMMA, B1 = range(7)
N_ROWS = B1


def wait(eng, sem, value):
    if isinstance(value, int) and value <= 0:
        return
    eng.wait_ge(sem, value)


def inside(k, n):
    return not isinstance(k, int) or 0 <= k < n


def valid(b):
    return inside(b, B)


def walk(eng, n, lo, hi, body):
    assert lo % 2 == 0 and (hi - lo) % 2 == 0
    for t in range(lo):
        body(t, t % 2)
    with eng.Fori(lo // 2, hi // 2) as r:
        body(2 * r, 0)
        body(2 * r + 1, 1)
    for t in range(hi, n):
        body(t, t % 2)


def Sems(nc, ctx, prefix, names):
    return namedtuple("Sems", names)(*[ctx.enter_context(nc.semaphore(f"{prefix}_{n}")) for n in names.split()])


class Memory:
    pass


def rsqrt_seed(dve, link, y, v):
    link(dve.tensor_scalar(y.bitcast(I32), v.bitcast(I32), -0.5, RSQRT_MAGIC, ALU.mult, ALU.add))


def rsqrt_newton(dve, link, y, v, t):
    link(dve.tensor_tensor(t, y, y, ALU.mult))
    link(dve.scalar_tensor_tensor(out=t, in0=t, scalar=-0.5, in1=v, op0=ALU.mult, op1=ALU.mult))
    link(dve.scalar_tensor_tensor(out=y, in0=t, scalar=1.5, in1=y, op0=ALU.add, op1=ALU.mult))


def linker(dve, sem, count):
    def link(ins):
        count[0] += 1
        ins.then_inc(sem, 1)
        dve.wait_ge(sem, count[0])
    return link


SCALE_STEPS, RMS_STEPS = 4, 8


def scale_step(dve, m, first, last, step, rms=False):
    if step >= (RMS_STEPS if rms else SCALE_STEPS):
        return
    link = linker(dve, m.s_link, m.link_count)
    cut = slice(first, last)
    var, veps, rstd, tmp, ssq = m.mv[:, cut, 1], m.veps[:, cut], m.rstd[:, cut], m.tmp16[:, cut], m.ssq[:, cut]
    if step == 0:
        for b in range(first, last):
            ins = dve.bn_aggr(m.mv[:, b, :], m.bn[:, b, :])
        link(ins)
        link(dve.tensor_scalar(veps, var, EPS, None, ALU.add))
        rsqrt_seed(dve, link, rstd, veps)
    elif step < 4:
        rsqrt_newton(dve, link, rstd, veps, tmp)
    elif step == 4:
        link(dve.tensor_tensor(ssq, rstd, rstd, ALU.mult))
        link(dve.tensor_tensor(ssq, ssq, var, ALU.mult))
        link(dve.tensor_scalar(ssq, ssq, float(D), 1e-24, ALU.mult, ALU.max))
        rsqrt_seed(dve, link, veps, ssq)
    else:
        rsqrt_newton(dve, link, veps, ssq, tmp)
        if step == 7:
            link(dve.scalar_tensor_tensor(out=rstd, in0=rstd, scalar=float(D) ** 0.5, in1=veps, op0=ALU.mult, op1=ALU.mult))


def row_scale(dve, m, first, last, rms=False):
    for step in range(RMS_STEPS):
        scale_step(dve, m, first, last, step, rms)


def row_stats(dve, m, sem, b):
    dve.bn_stats(m.bn[:, b, :], m.x[:, b, :]).then_inc(sem, 1)


def normalise(dve, m, out, b, **how):
    return dve.tensor_scalar(out, m.x[:, b, :], m.mv[:, b, 0:1], m.rstd[:, bass.ds(b, 1)], ALU.subtract, ALU.mult, **how)


def first_stats(dve, m, first, last):
    for b in range(first, last):
        if b % 4 == 0:
            dve.wait_ge(m.s_x[b // 4], 16)
        row_stats(dve, m, m.s_first_stats, b)
    dve.wait_ge(m.s_first_stats, last)


def load_block(nc, ctx, m, d):
    s = Sems(nc, ctx, "ld", "ident self_w rot ones")
    rows = (d.L1_attn_bg, d.L1_attn_bv, d.L1_attn_bd, d.L1_xattn_bq, d.L1_ffn_norm_gamma, d.L1_ffn_slot_norm_gamma)
    with nc.Block() as block:
        @block.sync
        def _(sp):
            for g in range(4):
                sp.dma_start(m.x[:, 4 * g:4 * g + 4, :], d.x[4 * g:4 * g + 4].rearrange("b t f -> t b f")).then_inc(m.s_x[g], 16)
            sp.dma_start(m.headmask[:, :], d.headmask).then_inc(m.s_first, 16)
            sp.dma_start(m.wo0[:, :], d.L0_attn_Wo).then_inc(m.s_first, 16)

        @block.scalar
        def _(act):
            act.dma_start(m.ident[:, :], d.ident).then_inc(s.ident, 16)
            act.dma_start(m.wqk[:, 0, :], d.L0_attn_Wq).then_inc(s.self_w, 16)
            act.dma_start(m.wqk[:, 1, :], d.L0_attn_Wk).then_inc(s.self_w, 16)
            act.dma_start(m.wv0[:, :], d.L0_attn_Wv).then_inc(m.s_first, 16)
            act.dma_start(m.rope[:, :, :, :], d.rope).then_inc(m.s_first, 16)
            act.wait_ge(s.ones, 1)
            act.activation(m.scrap[:, :], m.ones[:, 0:1], ACT.Exp).then_inc(s.ones, 1)

        @block.gpsimd
        def _(pool):
            pool.memset(m.causal[:, :, :], 0.0).then_inc(m.s_causal, 1)
            pool.wait_ge(m.s_causal, 1)
            pool.affine_select(out=m.causal[:, :, :], in_=m.causal[:, :, :], compare_op=ALU.is_ge, fill=MASKED, base=0,
                               pattern=[[0, HG], [-1, 128]], channel_multiplier=1).then_inc(m.s_causal, 1)

        @block.vector
        def _(dve):
            dve.memset(m.ones[:, :], 1.0).then_inc(s.ones, 1)
            first_stats(dve, m, 0, 4)
            row_scale(dve, m, 0, 4)
            dve.wait_ge(s.ident, 16)
            dve.tensor_copy(m.ident16[:, :], m.ident[:, :]).then_inc(s.ones, 1)
            dve.wait_ge(s.self_w, 32)
            for i in range(2):
                w = m.wqk[:, i, :].rearrange("p (n two) -> p n two", two=2)
                r = m.wqk[:, 2 + i, :].rearrange("p (n two) -> p n two", two=2)
                dve.tensor_scalar(r[:, :, 0], w[:, :, 1], -1.0, None, ALU.mult).then_inc(s.rot, 1)
                dve.tensor_copy(r[:, :, 1], w[:, :, 0]).then_inc(s.rot, 1)
            dve.wait_ge(s.ones, 3)
            dve.wait_ge(s.rot, 4)
            dve.wait_ge(m.s_first, 64)

    def loads(sp):
        row = lambda v: v.rearrange("(a n) -> a n", a=1)
        for dst, src in [(m.ctx_raw[:, :, :], d.ctx_1024.rearrange("b k f -> k b f")), (m.wk_wide[:, :], d.L0_xattn_W_k),
                         (m.wk_narrow[:, :], d.L1_xattn_Wk), (m.bk_row[:, :], row(d.L1_xattn_bk)),
                         (m.slots[:, :, :], d.L1_ffn_slot_embeds.rearrange("(c e) s f -> (e s) c f", c=4)),
                         (m.w_raw[:, :], d.L0_ffn_weight), (m.mask8[:, :], d.mask_SxS2_bk1),
                         (m.vec_rows[N_ROWS:, :], d.L1_ffn_b1.rearrange("e (c p) -> (e c) p", p=128)),
                         (m.wq_wide[:, :], d.L0_xattn_W_q), (m.wv_wide[:, :], d.L0_xattn_W_v),
                         (m.wo_wide[:, :, :], d.L0_xattn_W_o.rearrange("(c p) f -> p c f", p=128)),
                         (m.ffn_bias[:, :], d.L0_ffn_bias.partition_broadcast(128)),
                         (m.wg[:, :], d.L1_attn_Wg), (m.wvs[:, :], d.L1_attn_Wv), (m.wd[:, :], d.L1_attn_Wd),
                         (m.wq1[:, :], d.L1_xattn_Wq), (m.wv1[:, :], d.L1_xattn_Wv), (m.wo1[:, :], d.L1_xattn_Wo),
                         (m.bv1[:, :], row(d.L1_xattn_bv)), (m.bo1[:, :], row(d.L1_xattn_bo))]:
            sp.dma_start(dst, src).then_inc(m.s_rest, 16)
            m.all_rest += 16
        for i, vec in enumerate(rows):
            sp.dma_start(m.vec_rows[i:i + 1, :], row(vec)).then_inc(m.s_rest, 16)
            m.all_rest += 16

    return loads


def keys_block(nc, ctx, m):
    s = Sems(nc, ctx, "kb", "prep ctx_t ctx_tc vec_t vec_c wt kT kTc sn_t bf zero")
    KB = 4
    kraw = B // KB * (NCH + 1)
    NV = N_ROWS + E * NHC
    with ExitStack() as tmp, nc.Block() as block:
        sb = lambda n, sh, dt: tmp.enter_context(nc.sbuf_tensor(n, sh, dt))
        ps = [tmp.enter_context(nc.psum_tensor(f"kb_ps{i}", [128, 512], F32)) for i in range(4)]
        pW, pSn = [tmp.enter_context(nc.psum_tensor(f"kb_{n}", [128, 512], F32)) for n in ("pW", "pSn")]
        w_clip = sb("ffn_w_clip", [128, 2, 128], F32)
        w8 = sb("ffn_w8", [128, 2, 128], FP8)
        w_val = sb("ffn_w_val", [128, 2, 128], F32)
        w_big = sb("ffn_w_big", [128, 128], F32)
        slots2 = sb("slots2", [128, 4, 128], F32)
        ss = sb("slot_ss", [128, 4], F32)
        rs = sb("slot_rs", [128, 4], F32)
        t4 = sb("slot_t", [128, 4], F32)

        @block.tensor
        def _(pe):
            pe.wait_ge(m.s_rest, m.all_rest)
            for g in range(4):
                for i in range(4):
                    ins = pe.transpose(ps[g][:, i * C2:(i + 1) * C2], m.ctx_raw[:, 4 * g + i, :], m.ident[0:C2, 0:C2])
                ins.then_inc(s.ctx_t, 1)
            pe.transpose(pW[:, 0:NV], m.vec_rows[:, :], m.ident[0:NV, 0:NV]).then_inc(s.vec_t, 1)
            for i in range(kraw):
                g, c = divmod(i, NCH + 1)
                pe.wait_ge(s.ctx_tc, 4)
                wait(pe, s.kTc, i - 3)
                keys = m.ck[:, KB * g:KB * g + KB, 0, :]
                w = m.wk_wide[:, c * 128:(c + 1) * 128] if c < NCH else m.wk_narrow[:, :]
                ins = pe.matmul(ps[i % 4][:, 0:KB * C2], w, keys, start=True, stop=c < NCH)
                if c == NCH:
                    ins = pe.matmul(ps[i % 4][:, 0:KB * C2], m.bk_row[0:1, :], m.ones[0:1, 0:KB * C2], start=False, stop=True)
                ins.then_inc(s.kT, 1)
            pe.wait_ge(s.vec_c, 1)
            pe.wait_ge(s.prep, 1)
            pe.transpose(pW[:, 0:128], w_val[:, 0, :], m.ident[:, :]).then_inc(s.wt, 1)
            pe.wait_ge(s.prep, 2)
            for c in range(4):
                ins = pe.transpose(pSn[:, c * 128:(c + 1) * 128], slots2[:, c, :], m.ident[:, :])
            ins.then_inc(s.sn_t, 1)

        @block.gpsimd
        def _(pool):
            for buffer in (m.kblk[:, :, :, :, :], m.prob_wide[:, :, :, :], m.vx_wide[:, :, :]):
                pool.memset(buffer, 0.0).then_inc(s.zero, 1)
            pool.wait_ge(s.zero, 3)

        @block.scalar
        def _(act):
            for g in range(4):
                act.wait_ge(s.ctx_t, g + 1)
                act.activation(m.ck[:, 4 * g:4 * g + 4, 0, :], ps[g][:, 0:4 * C2].rearrange("p (b k) -> p b k", b=4),
                               ACT.Copy).then_inc(s.ctx_tc, 1)
            act.wait_ge(s.vec_t, 1)
            act.activation(m.vec[:, :], pW[:, 0:NV], ACT.Copy).then_inc(s.vec_c, 1)
            for i in range(kraw):
                g, c = divmod(i, NCH + 1)
                act.wait_ge(s.kT, i + 1)
                src = ps[i % 4][:, 0:KB * C2].rearrange("p (b k) -> p b k", b=KB)
                dst = m.kT_wide[:, KB * g:KB * g + KB, c, :] if c < NCH else m.ck[:, KB * g:KB * g + KB, 1, :]
                act.activation(dst, src, ACT.Copy).then_inc(s.kTc, 1)
            act.wait_ge(s.wt, 1)
            act.activation(m.ffn_wT[:, :], pW[:, 0:128], ACT.Copy).then_inc(s.vec_c, 1)
            act.wait_ge(s.sn_t, 1)
            act.wait_ge(s.prep, 3)
            act.activation(m.snT[:, :], pSn[:, :], ACT.Copy, scale=m.gg[:, 0:1]).then_inc(s.vec_c, 1)
            act.wait_ge(s.vec_c, 3)

        @block.vector
        def _(dve):
            link = linker(dve, m.s_link, m.link_count)
            dve.wait_ge(m.s_rest, m.all_rest)
            link(dve.tensor_scalar(w_clip[:, 0, :], m.w_raw[:, :], 240.0, -240.0, ALU.min, ALU.max))
            link(dve.tensor_scalar(w_clip[:, 1, :], m.w_raw[:, :], 448.0, -448.0, ALU.min, ALU.max))
            link(dve.tensor_copy(w8[:, 0, :], w_clip[:, 0, :], saturate=False))
            link(dve.tensor_scalar(w8[:, 1, :], w_clip[:, 1, :], 0.5, None, ALU.mult, saturate=False))
            link(dve.tensor_copy(w_val[:, 0, :], w8[:, 0, :]))
            link(dve.tensor_scalar(w_val[:, 1, :], w8[:, 1, :], 2.0, None, ALU.mult))
            link(dve.tensor_tensor(w_big[:, :], m.w_raw[:, :], m.w_raw[:, :], ALU.mult))
            link(dve.tensor_scalar(w_big[:, :], w_big[:, :], 128.0 ** 2, None, ALU.is_gt))
            dve.copy_predicated(w_val[:, 0, :], w_big[:, :].bitcast(I32), w_val[:, 1, :]).then_inc(s.prep, 1)
            link(dve.tensor_tensor(slots2[:, :, :], m.slots[:, :, :], m.slots[:, :, :], ALU.mult))
            link(dve.tensor_reduce(ss[:, :], slots2[:, :, :], AX.X, ALU.add))
            link(dve.tensor_scalar(ss[:, :], ss[:, :], 1e-24, None, ALU.max))
            rsqrt_seed(dve, link, rs[:, :], ss[:, :])
            for _ in range(3):
                rsqrt_newton(dve, link, rs[:, :], ss[:, :], t4[:, :])
            link(dve.tensor_scalar(rs[:, :], rs[:, :], float(D) ** 0.5, None, ALU.mult))
            dve.tensor_tensor(slots2[:, :, :], m.slots[:, :, :], rs[:, :].unsqueeze(2).broadcast_to([128, 4, 128]),
                              ALU.mult).then_inc(s.prep, 1)
            dve.wait_ge(s.vec_c, 1)
            dve.tensor_tensor(m.gg[:, :], m.vec[:, GAMMA:GAMMA + 1], m.vec[:, SGAMMA:SGAMMA + 1], ALU.mult).then_inc(s.prep, 1)
            dve.tensor_scalar(m.half_b[:, 0:1], m.vec[:, BG:BG + 1], 0.5, None, ALU.mult).then_inc(s.bf, 1)
            dve.tensor_scalar(m.half_b[:, 1:2], m.vec[:, BD:BD + 1], 0.5, None, ALU.mult).then_inc(s.bf, 1)
            dve.tensor_scalar(m.half_b[:, 2:3], m.vec[:, BQ:BQ + 1], float(DK) ** -0.5, None, ALU.mult).then_inc(s.bf, 1)
            for i in range(HG):
                dve.tensor_scalar(m.xmask[:, i, :], m.mask8[:, :], MASKED, None, ALU.mult).then_inc(s.bf, 1)
            dve.wait_ge(s.bf, 3 + HG)
            row_scale(dve, m, AHEAD, B)


def narrow_attention(nc, ctx, m, name, K, cross, loads=None):
    s = Sems(nc, ctx, name, "xn xt xtc proj q km vp v1 v vx sc mx ex pt pt1 ptc pv red nrm ot otc y res stats zero "
             + ("ctxc" if cross else "rope1"))
    wv, wo = (m.wv1, m.wo1) if cross else (m.wv0, m.wo0)
    PSCALE = 2048.0
    W = 3 * DK + 1
    with ExitStack() as tmp, nc.Block() as block:
        sb = lambda n, sh, dt=F32: tmp.enter_context(nc.sbuf_tensor(f"{name}_{n}", sh, dt))
        pb = lambda n, sh, dt=F32: tmp.enter_context(nc.psum_tensor(f"{name}_{n}", sh, dt))
        xn, xnT = sb("xn", [128, 2, 128]), sb("xnT", [128, 2, 128])
        rot = sb("rot", [128, 2, 2, 128])
        qk = sb("qk", [128, 2, 2, 128])
        kmask = sb("kmask", [128, 2, H, K])
        vx = sb("vx", [128, 2, H, W], BF16)
        vr = sb("vr", [128, H, DK])
        cur = sb("cur", [128, 2, 2, C2])
        prob = sb("prob", [128, 2, HG, 128])
        p1, p2 = sb("p1", [128, 2, HG, 128], F16), sb("p2", [128, 2, HG, 128], F16)
        mx = sb("mx", [128, 2, HG])
        rec = sb("rec", [128, H])
        att, attT = sb("att", [128, 128]), sb("attT", [128, 128])
        pS = [pb(f"pS{i}", [128, HG, 128]) for i in range(2)]
        pT = [pb(f"pT{i}", [128, HG, 128]) for i in range(2)]
        pO = [pb(f"pO{i}", [128, 512]) for i in range(2)]
        pP, pX = pb("pP", [128, 4, 128]), pb("pX", [128, 4, 128])
        XT, Y, V, AT = range(4)
        SC = lambda g: pS[g % 2][:, :, :].rearrange("p a b -> p (a b)")[:, 0:HG * K].rearrange("p (a b) -> p a b", a=HG)
        O = [po[:, 0:H * W].rearrange("p (h w) -> p h w", h=H) for po in pO]
        heads = lambda x: x.rearrange("p (h w) -> p h w", h=H)

        N = B + 3
        LO, HI = 4, 14

        @block.tensor
        def _(pe):
            pe.wait_ge(m.s_causal, 2)

            def body(t, p):
                for g in range(NG):
                    b, q = t - 1, (p + 1) % 2
                    u = 4 * b + g
                    if valid(b):
                        if g == 0:
                            wait(pe, s.q, b + 1)
                        wait(pe, s.km, u + 1)
                        wait(pe, s.ex, u - 1)
                        ins = pe.matmul(SC(g), qk[:, q, 0, :], kmask[:, q, HG * g:HG * g + HG, :], start=True, stop=cross)
                        if not cross:
                            ins = pe.matmul(SC(g), m.ident16[:, :], m.causal[:, :, :], start=False, stop=True)
                        ins.then_inc(s.sc, 1)
                    bt, gt = (b, g - 2) if g >= 2 else (b - 1, g + 2)
                    if valid(bt):
                        v = 4 * bt + gt
                        wait(pe, s.ex, v + 1)
                        wait(pe, s.ptc, v - 1)
                        for i in range(HG):
                            ins = pe.transpose(pT[g % 2][:, i, :], prob[:, g % 2, i, :], m.ident[:, :])
                        ins.then_inc(s.pt, 1)
                    bp, gp, qp = (b, 0, q) if g == 3 else (b - 1, g + 1, p)
                    if valid(bp):
                        v = 4 * bp + gp
                        wait(pe, s.ptc, v + 1)
                        if gp == 0:
                            wait(pe, s.vx, bp + 1)
                            wait(pe, s.red, 2 * (bp - 1))
                        for i in range(HG):
                            h = HG * gp + i
                            pe.matmul(O[qp][:, h, :], p1[:, gp % 2, i, :], vx[:, qp, h, :], start=True, stop=False)
                            ins = pe.matmul(O[qp][:, h, :], p2[:, gp % 2, i, :], vx[:, qp, h, :], start=False, stop=True)
                        ins.then_inc(s.pv, 1)
                    if g == 0 and valid(t - 3):
                        wait(pe, s.nrm, t - 2)
                        wait(pe, s.v, 2 * t - 1 if not isinstance(t, int) or t < B else 2 * B - 1)
                        pe.transpose(pX[:, AT, :], att[:, :], m.ident[:, :]).then_inc(s.ot, 1)
                    if g == 0 and valid(t):
                        wait(pe, s.xn, t + 1)
                        wait(pe, s.v, 2 * t - 1)
                        pe.transpose(pX[:, XT, :], xn[:, p, :], m.ident[:, :]).then_inc(s.xt, 1)
                    if g == 1 and valid(t):
                        wait(pe, s.xtc, t + 1)
                        if cross:
                            wait(pe, s.q, t)
                            pe.matmul(pP[:, 0, :], m.wq1[:, :], xnT[:, p, :], start=True, stop=True).then_inc(s.proj, 1)
                        else:
                            wait(pe, s.rope1, 2 * t)
                            for i in range(4):
                                ins = pe.matmul(pP[:, i, :], m.wqk[:, i, :], xnT[:, p, :], start=True, stop=True)
                            ins.then_inc(s.proj, 1)
                    if g == 1 and valid(t - 3):
                        wait(pe, s.otc, t - 2)
                        wait(pe, s.xtc, t + 1 if not isinstance(t, int) or t < B else B)
                        ins = pe.matmul(pX[:, Y, :], attT[:, :], wo[:, :], start=True, stop=not cross)
                        if cross:
                            ins = pe.matmul(pX[:, Y, :], m.ones[0:1, 0:128], m.bo1[:, :], start=False, stop=True)
                        ins.then_inc(s.y, 1)
                    if g == 2 and valid(t):
                        wait(pe, s.res, t - 2)
                        wait(pe, s.xtc, t + 1)
                        if cross:
                            wait(pe, s.ctxc, t + 1)
                            pe.matmul(pX[0:K, V, :], cur[:, p, 0, :], wv[:, :], start=True, stop=False)
                            pe.matmul(pX[0:K, V, :], m.ones[0:1, 0:K], m.bv1[:, :], start=False, stop=True).then_inc(s.vp, 1)
                        else:
                            pe.matmul(pX[:, V, :], xnT[:, p, :], wv[:, :], start=True, stop=True).then_inc(s.vp, 1)

            walk(pe, N, LO, HI, body)

        @block.vector
        def _(dve):
            normalise(dve, m, xn[:, 0, :], 0).then_inc(s.xn, 1)
            for q in range(2):
                dve.memset(vx[:, q, :, 0:W - 1], 0.0).then_inc(s.zero, 1)
                dve.memset(vx[:, q, :, W - 1:W], 1.0).then_inc(s.zero, 1)

            def body(t, p):
                if isinstance(t, int) and t == B - cross:
                    dve.wait_ge(s.stats, AHEAD)
                if isinstance(t, int) and t == 0 and not cross:
                    first_stats(dve, m, 4, B)
                for g in range(NG):
                    b = t - 1
                    u = 4 * b + g
                    if g == 2 and valid(t - 3):
                        wait(dve, s.y, t - 2)
                        dve.tensor_tensor(m.x[:, t - 3, :], m.x[:, t - 3, :], pX[:, Y, :], ALU.add).then_inc(s.res, 1)
                    if g == 3 and valid(t - 2):
                        wait(dve, s.pv, 4 * (t - 2) + 4)
                        dve.reciprocal(rec[:, :], O[p][:, :, W - 1]).then_inc(s.red, 1)
                        wait(dve, s.ot, t - 2)
                        parts = O[p][:, :, 0:3 * DK].rearrange("p h (j w) -> p h w j", j=3)
                        dve.tensor_reduce(heads(att[:, :]), parts, AX.X, ALU.add).then_inc(s.red, 1)
                        wait(dve, s.red, 2 * (t - 1))
                        dve.tensor_tensor(heads(att[:, :]), heads(att[:, :]), rec[:, :].unsqueeze(2).broadcast_to([128, H, DK]),
                                          ALU.mult).then_inc(s.nrm, 1)
                    if g == 2 and valid(t) and not cross:
                        wait(dve, s.proj, t + 1)
                        wait(dve, s.q, t)
                        dve.tensor_tensor(rot[:, 0, :, :], pP[:, 0:2, :], m.rope[:, 0, :, :], ALU.mult).then_inc(s.rope1, 1)
                        dve.tensor_tensor(rot[:, 1, :, :], pP[:, 2:4, :], m.rope[:, 1, :, :], ALU.mult).then_inc(s.rope1, 1)
                        wait(dve, s.rope1, 2 * t + 2)
                        wait(dve, s.sc, 4 * (t - 1))
                        wait(dve, s.km, 4 * (t - 1))
                        dve.tensor_tensor(qk[:, p, :, :], rot[:, 0, :, :], rot[:, 1, :, :], ALU.add).then_inc(s.q, 1)
                    if valid(b):
                        wait(dve, s.sc, u + 1)
                        wait(dve, s.ex, u - 1)
                        dve.tensor_reduce(mx[:, g % 2, :], SC(g), AX.X, ALU.max, negate=True).then_inc(s.mx, 1)
                    if g == 3 and valid(t):
                        wait(dve, s.v1, t + 1)
                        wait(dve, s.vx, t)
                        dve.tensor_tensor(vr[0:K, :, :], heads(pX[0:K, V, :]), vx[0:K, p, :, 0:DK], ALU.subtract).then_inc(s.v, 1)
                        wait(dve, s.v, 2 * t + 1)
                        dve.tensor_copy(vx[0:K, p, :, DK:2 * DK], vr[0:K, :, :]).then_inc(s.v, 1)
                    bt, gt = (b, g - 2) if g >= 2 else (b - 1, g + 2)
                    if valid(bt):
                        v = 4 * bt + gt
                        wait(dve, s.pt1, v + 1)
                        wait(dve, s.pv, v - 1)
                        dve.scalar_tensor_tensor(out=p2[:, g % 2, :, :], in0=pT[g % 2][:, :, :], scalar=PSCALE,
                                                 in1=p1[:, g % 2, :, :], op0=ALU.mult, op1=ALU.subtract).then_inc(s.ptc, 1)
                    if g == 3 and valid(t - 3):
                        wait(dve, s.res, t - 2)
                        row_stats(dve, m, s.stats, t - 3)
                    if g == 1 and valid(t + 1):
                        wait(dve, s.xt, t)
                        normalise(dve, m, xn[:, (p + 1) % 2, :], t + 1).then_inc(s.xn, 1)
                    if isinstance(t, int) and t == 1:
                        scale_step(dve, m, B // 2 if cross else 4, B, g)
                    if isinstance(t, int) and t >= B - cross:
                        scale_step(dve, m, 0, AHEAD, NG * (t - B + cross) + g, rms=cross)

            walk(dve, N, LO, HI, body)
            dve.wait_ge(s.stats, B)

        if loads is not None:
            @block.sync
            def _(sp):
                loads(sp)

        @block.gpsimd
        def _(pool):
            pool.memset(prob[:, :, :, :], 0.0).then_inc(s.zero, 1)

            def body(t, p):
                if not valid(t):
                    return
                if cross:
                    wait(pool, s.vp, t - 1)
                    wait(pool, s.km, 4 * t)
                    pool.tensor_copy(cur[:, p, :, :], m.ck[:, t, :, :]).then_inc(s.ctxc, 1)
                    wait(pool, s.ctxc, t + 1)
                    k = cur[:, p, 1, :]
                else:
                    wait(pool, s.q, t + 1)
                    k = qk[:, p, 1, :]
                for g in range(NG):
                    wait(pool, s.sc, 4 * (t - 2) + g + 1)
                    own = slice(HG * g, HG * g + HG)
                    pool.tensor_tensor(kmask[:, p, own, :], k.unsqueeze(1).broadcast_to([128, HG, K]),
                                       m.headmask[:, own].unsqueeze(2).broadcast_to([128, HG, K]), ALU.mult).then_inc(s.km, 1)
                wait(pool, s.v, 2 * t + 2)
                pool.tensor_tensor(vx[0:K, p, :, 2 * DK:3 * DK], vr[0:K, :, :], vx[0:K, p, :, DK:2 * DK],
                                   ALU.subtract).then_inc(s.vx, 1)

            walk(pool, B, LO, HI, body)

        @block.scalar
        def _(act):
            g_turned = 1

            def body(t, p):
                for g in range(NG):
                    b, q = t - 1, (p + 1) % 2
                    u = 4 * b + g
                    if g == g_turned and valid(t):
                        wait(act, s.xt, t + 1)
                        wait(act, s.vp, t - 1)
                        wait(act, s.proj, t - 1)
                        act.activation(xnT[:, p, :], pX[:, XT, :], ACT.Copy).then_inc(s.xtc, 1)
                    if g == g_turned and valid(t - 3):
                        wait(act, s.ot, t - 2)
                        wait(act, s.y, t - 3)
                        act.activation(attT[:, :], pX[:, AT, :], ACT.Copy).then_inc(s.otc, 1)
                    if g == 3 and valid(t):
                        if isinstance(t, int) and t == 0:
                            act.wait_ge(s.zero, 5)
                        wait(act, s.vp, t + 1)
                        wait(act, s.pv, 4 * (t - 1))
                        act.activation(vx[0:K, p, :, 0:DK], heads(pX[0:K, V, :]), ACT.Copy).then_inc(s.v1, 1)
                    bt, gt = (b, g - 2) if g >= 2 else (b - 1, g + 2)
                    if valid(bt):
                        v = 4 * bt + gt
                        wait(act, s.pt, v + 1)
                        wait(act, s.pv, v - 1)
                        act.activation(p1[:, g % 2, :, :], pT[g % 2][:, :, :], ACT.Copy, scale=PSCALE).then_inc(s.pt1, 1)
                    if g == 2 and valid(t) and cross:
                        wait(act, s.proj, t + 1)
                        wait(act, s.sc, 4 * (t - 1))
                        act.activation(qk[:, p, 0, :], pP[:, 0, :], ACT.Identity, bias=m.half_b[:, 2:3],
                                       scale=float(DK) ** -0.5).then_inc(s.q, 1)
                    if valid(b):
                        wait(act, s.mx, u + 1)
                        wait(act, s.pt, u - 1)
                        for i in range(HG):
                            ins = act.activation(prob[:, g % 2, i, 0:K], SC(g)[:, i, :], ACT.Exp, bias=mx[:, g % 2, i:i + 1])
                        ins.then_inc(s.ex, 1)

            walk(act, N, LO, HI, body)


def wide_attention(nc, ctx, m):
    name, K = "wide", C2
    s = Sems(nc, ctx, name, "xn xt xtc qv qve km ctxc sc mx ex rec nrm pt ptc pv otc y res stats")
    with ExitStack() as tmp, nc.Block() as block:
        sb = lambda n, sh, dt=F32: tmp.enter_context(nc.sbuf_tensor(f"{name}_{n}", sh, dt))
        pb = lambda n, sh, dt=F32: tmp.enter_context(nc.psum_tensor(f"{name}_{n}", sh, dt))
        xn, xnT = sb("xn", [128, 2, 128]), sb("xnT", [128, 2, 128])
        qT = sb("qT", [128, 2, NCH, 128])
        cur = sb("cur", [128, 2, K])
        kblk, vx, prob = m.kblk, m.vx_wide, m.prob_wide
        probT = sb("probT", [128, 2, HG, 128])
        mx, sums, rec = sb("mx", [128, 2, HG]), sb("sums", [128, 2, HG]), sb("rec", [128, 2, HG])
        attT = sb("attT", [128, 2, 2, 128])
        pS = [pb(f"pS{i}", [128, 512]) for i in range(2)]
        pT = [pb(f"pT{i}", [128, HG, 128]) for i in range(2)]
        pO = [pb(f"pO{i}", [128, 4, 128]) for i in range(2)]
        pQV, pX = pb("pQV", [128, 512]), pb("pX", [128, 4, 128])
        XT, Y = pX[:, 0, :], pX[:, 1, :]
        SC = lambda g: pS[g % 2][:, 0:HG * K].rearrange("p (a b) -> p a b", a=HG)

        N = B + 3
        LO, HI = 4, 16

        def group(t, g, lag):
            back = (g - lag) // NG
            return t - 1 + back, (g - lag) % NG

        def round_of(t, g):
            return (t - 1, 3, 1) if g == 0 else (t, g - 1, 0)

        @block.tensor
        def _(pe):
            def body(t, p):
                for g in range(NG):
                    b, q = t - 1, (p + 1) % 2
                    u = 4 * b + g
                    if valid(b):
                        if g == 0:
                            wait(pe, s.km, 2 * b + 2)
                            wait(pe, s.qve, 4 * b + 2)
                        wait(pe, s.ex, u - 1)
                        for i in range(2):
                            c = 2 * g + i
                            pe.matmul(pS[g % 2][:, 2 * K * i:2 * K * (i + 1)], qT[:, q, c, :], kblk[:, q, c, :, :],
                                      start=i == 0, stop=False, skip_group_check=True)
                        pe.matmul(SC(g), m.ident16[:, :], m.xmask[:, :, :], start=False, stop=True,
                                  skip_group_check=True).then_inc(s.sc, 1)
                    bt, gt = group(t, g, 2)
                    if valid(bt):
                        v = 4 * bt + gt
                        wait(pe, s.nrm, v + 1)
                        wait(pe, s.ptc, v - 1)
                        for i in range(HG):
                            ins = pe.transpose(pT[g % 2][:, i, :], prob[:, g % 2, i, :], m.ident[:, :])
                        ins.then_inc(s.pt, 1)
                    if g == 0 and valid(t):
                        wait(pe, s.xn, t + 1)
                        wait(pe, s.res, t - 2)
                        pe.transpose(XT, xn[:, p, :], m.ident[:, :]).then_inc(s.xt, 1)
                    bp, gp = group(t, g, 3)
                    if valid(bp):
                        v = 4 * bp + gp
                        wait(pe, s.ptc, v + 1)
                        if gp == 0:
                            wait(pe, s.qve, 4 * bp + 4)
                        wait(pe, s.otc, v - 1)
                        qp = q if g == 3 else p
                        for i in range(HG):
                            h = HG * gp + i
                            ins = pe.matmul(pO[gp % 2][64 * (i % 2):64 * (i % 2) + 64, i // 2, :], vx[:, qp, HD * h:HD * h + HD],
                                            probT[:, gp % 2, i, :], start=True, stop=True)
                        ins.then_inc(s.pv, 1)
                    by, gy = group(t, g, 4)
                    if valid(by):
                        v = 4 * by + gy
                        wait(pe, s.otc, v + 1)
                        if gy == 0:
                            wait(pe, s.res, by)
                            wait(pe, s.xtc, t + 1 if not isinstance(t, int) or t < B else B)
                        for i in range(2):
                            ins = pe.matmul(Y, attT[:, gy % 2, i, :], m.wo_wide[:, 2 * gy + i, :],
                                            start=gy == 0 and i == 0, stop=gy == 3 and i == 1)
                        ins.then_inc(s.y, 1)
                    bv, k, late = round_of(t, g)
                    if valid(bv):
                        if k == 0:
                            wait(pe, s.xtc, t + 1)
                        if k == 2:
                            wait(pe, s.ctxc, t + 1)
                        wait(pe, s.qve, 4 * bv + k)
                        if k >= 2:
                            half = 512 * (k - 2)
                            ins = pe.matmul(pQV[0:K, :], cur[:, (p + late) % 2, :], m.wv_wide[:, half:half + 512],
                                            start=True, stop=True)
                        else:
                            for i in range(4):
                                c = 4 * k + i
                                ins = pe.matmul(pQV[:, 128 * i:128 * i + 128], m.wq_wide[:, 128 * c:128 * c + 128],
                                                xnT[:, p, :], start=True, stop=True)
                        ins.then_inc(s.qv, 1)

            walk(pe, N, LO, HI, body)

        @block.vector
        def _(dve):
            def body(t, p):
                if isinstance(t, int) and t == B:
                    dve.wait_ge(s.stats, AHEAD)
                if valid(t):
                    wait(dve, s.xt, t - 1)
                    normalise(dve, m, xn[:, p, :], t).then_inc(s.xn, 1)
                for g in range(NG):
                    b = t - 1
                    u = 4 * b + g
                    if g == 0 and valid(t - 3):
                        wait(dve, s.y, 4 * (t - 3) + 4)
                        dve.tensor_tensor(m.x[:, t - 3, :], m.x[:, t - 3, :], Y, ALU.add).then_inc(s.res, 1)
                    if g <= 1 and valid(t - 1):
                        k, q = g + 2, (p + 1) % 2
                        wait(dve, s.qv, 4 * (t - 1) + k + 1)
                        if k == 2:
                            wait(dve, s.pv, 4 * (t - 2))
                        half = 512 * (k - 2)
                        dve.tensor_copy(vx[0:K, q, half:half + 512], pQV[0:K, :]).then_inc(s.qve, 1)
                    if valid(b):
                        wait(dve, s.sc, u + 1)
                        wait(dve, s.ex, u - 1)
                        dve.tensor_reduce(mx[:, g % 2, :], SC(g), AX.X, ALU.max, negate=True).then_inc(s.mx, 1)
                    if g == 1 and valid(t - 3):
                        wait(dve, s.res, t - 2)
                        row_stats(dve, m, s.stats, t - 3)
                    if isinstance(t, int) and t >= B:
                        scale_step(dve, m, 0, AHEAD, NG * (t - B) + g)
                    bn, gn = group(t, g, 1)
                    if valid(bn):
                        v = 4 * bn + gn
                        wait(dve, s.ex, v + 1)
                        wait(dve, s.nrm, v - 1)
                        dve.reciprocal(rec[:, gn % 2, :], sums[:, gn % 2, :]).then_inc(s.rec, 1)
                        wait(dve, s.rec, v + 1)
                        dve.tensor_tensor(prob[:, gn % 2, :, 0:K], prob[:, gn % 2, :, 0:K],
                                          rec[:, gn % 2, :].unsqueeze(2).broadcast_to([128, HG, K]), ALU.mult).then_inc(s.nrm, 1)

            walk(dve, N, LO, HI, body)
            dve.wait_ge(s.stats, B)

        @block.gpsimd
        def _(pool):
            def body(t, p):
                if not valid(t):
                    return
                wait(pool, s.qv, 4 * (t - 1))
                wait(pool, s.km, 2 * t)
                pool.tensor_copy(cur[:, p, :], m.ck[:, t, 0, :]).then_inc(s.ctxc, 1)
                wait(pool, s.sc, 4 * (t - 1))
                wait(pool, s.ctxc, t + 1)
                for i in range(2):
                    rows = slice(64 * i, 64 * i + 64)
                    wait(pool, s.km, 2 * t + i)
                    pool.tensor_copy(kblk[rows, p, :, i, :], m.kT_wide[rows, t, :, :]).then_inc(s.km, 1)

            walk(pool, B, LO, HI, body)

        @block.scalar
        def _(act):
            def body(t, p):
                for g in range(NG):
                    b = t - 1
                    u = 4 * b + g
                    bt, gt = group(t, g, 2)
                    if valid(bt):
                        v = 4 * bt + gt
                        wait(act, s.pt, v + 1)
                        wait(act, s.pv, v - 1)
                        act.activation(probT[:, g % 2, :, :], pT[g % 2][:, :, :], ACT.Copy).then_inc(s.ptc, 1)
                    if g == 0 and valid(t):
                        wait(act, s.xt, t + 1)
                        wait(act, s.qv, 4 * (t - 2) + 2)
                        act.activation(xnT[:, p, :], XT, ACT.Copy).then_inc(s.xtc, 1)
                    if g >= 2 and valid(t):
                        wait(act, s.qv, 4 * t + g - 1)
                        wait(act, s.sc, 4 * (t - 1))
                        act.activation(qT[:, p, 4 * (g - 2):4 * (g - 1), :], pQV[:, :].rearrange("p (c n) -> p c n", c=4),
                                       ACT.Copy, scale=float(HD) ** -0.5).then_inc(s.qve, 1)
                    if valid(b):
                        wait(act, s.mx, u + 1)
                        wait(act, s.pt, u - 1)
                        wait(act, s.rec, u - 1)
                        for i in range(HG):
                            ins = act.activation(prob[:, g % 2, i, 0:K], SC(g)[:, i, :], ACT.Exp, bias=mx[:, g % 2, i:i + 1],
                                                 accum_out=sums[:, g % 2, i:i + 1])
                        ins.then_inc(s.ex, 1)
                    bp, gp = group(t, g, 3)
                    if valid(bp):
                        v = 4 * bp + gp
                        wait(act, s.pv, v + 1)
                        wait(act, s.y, v - 1)
                        act.activation(attT[:, gp % 2, :, :], pO[gp % 2][:, 0:2, :], ACT.Copy).then_inc(s.otc, 1)

            walk(act, N, LO, HI, body)


def linear_and_scan(nc, ctx, m):
    l = Sems(nc, ctx, "lin", "x8 xb xt xtc y yc yb res stats")
    s = Sems(nc, ctx, "scan", "xn xt xtc pr thd th inp a h ht res stats")
    LG, G = 4, 2
    LS, NS = B // LG, B // G
    with ExitStack() as tmp, nc.Block() as block:
        sb = lambda n, sh, dt=F32: tmp.enter_context(nc.sbuf_tensor(f"ls_{n}", sh, dt))
        pb = lambda n, sh: tmp.enter_context(nc.psum_tensor(f"ls_{n}", sh, F32))
        x8, xb, xbT = sb("x8", [128, 2, LG, 128], FP8), sb("xb", [128, 2, LG, 128], BF16), sb("xbT", [128, 2, LG, 128], BF16)
        y16, yb = sb("y16", [128, 2, LG, 128], F16), sb("yb", [128, 2, LG, 128])
        xn, xnT = sb("xn", [128, 2, G, 128]), sb("xnT", [128, 2, G, 128])
        th = sb("th", [128, 2, 3, G, 128])
        inp, a, h = sb("inp", [128, 2, G, 128]), sb("a", [128, 2, G, 128]), sb("h", [128, 2, G, 128])
        pX, pH = [pb(f"pX{i}", [128, 4, 128]) for i in range(2)], [pb(f"pH{i}", [128, 4, 128]) for i in range(2)]
        pG = [pb(f"pG{i}", [128, 4, G, 128]) for i in range(2)]
        pXb = [pG[i][:, 3, :, :].bitcast(BF16).rearrange("p g (h c) -> p (g h) c", h=2) for i in range(2)]
        pY = pH

        @block.tensor
        def _(pe):
            for t in range(LS + 1):
                if t < LS:
                    wait(pe, l.xb, t + 1)
                    wait(pe, l.xtc, t - 1)
                    for i in range(LG):
                        ins = pe.transpose(pXb[t % 2][:, i, :], xb[:, t % 2, i, :], m.ident16[:, :])
                    ins.then_inc(l.xt, 1)
                if t >= 1:
                    q = (t - 1) % 2
                    wait(pe, l.xtc, t)
                    wait(pe, l.yc, t - 2)
                    for i in range(LG):
                        ins = pe.matmul(pY[q][:, i, :], xbT[:, q, i, :], m.ffn_wT[:, :], start=True, stop=True)
                    ins.then_inc(l.y, 1)

            for t in range(NS + 3):
                k = t - 3
                if inside(k, NS):
                    if k == 0:
                        pe.wait_ge(l.yc, LS)
                    wait(pe, s.h, k + 1)
                    wait(pe, s.res, k - 1)
                    for i in range(G):
                        ins = pe.transpose(pH[k % 2][:, i, :], h[:, k % 2, i, :], m.ident[:, :])
                    ins.then_inc(s.ht, 1)
                if t < NS:
                    wait(pe, s.xn, t + 1)
                    wait(pe, s.xtc, t - 1)
                    for i in range(G):
                        ins = pe.transpose(pX[t % 2][:, i, :], xn[:, t % 2, i, :], m.ident[:, :])
                    ins.then_inc(s.xt, 1)
                k = t - 1
                if inside(k, NS):
                    wait(pe, s.xtc, k + 1)
                    wait(pe, s.th, k - 1)
                    for i, w in enumerate((m.wg, m.wvs, m.wd)):
                        ins = pe.matmul(pG[k % 2][:, i, :, :], w[:, :], xnT[:, k % 2, :, :], start=True, stop=True)
                    ins.then_inc(s.pr, 1)

        @block.scalar
        def _(act):
            for t in range(LS + 1):
                if t < LS:
                    wait(act, l.x8, t + 1)
                    act.activation(xb[:, t % 2, :, :], x8[:, t % 2, :, :], ACT.Copy).then_inc(l.xb, 1)
                    wait(act, l.xt, t + 1)
                    wait(act, l.y, t - 1)
                    act.activation(xbT[:, t % 2, :, :], pXb[t % 2], ACT.Copy).then_inc(l.xtc, 1)
                if t >= 1:
                    q = (t - 1) % 2
                    wait(act, l.y, t)
                    wait(act, l.yb, t - 2)
                    act.activation(y16[:, q, :, :], pY[q][:, :, :], ACT.Copy).then_inc(l.yc, 1)

            for t in range(NS + 1):
                if t < NS:
                    wait(act, s.xt, t + 1)
                    wait(act, s.pr, t - 1)
                    act.activation(xnT[:, t % 2, :, :], pX[t % 2][:, 0:G, :], ACT.Copy).then_inc(s.xtc, 1)
                k, q = t - 1, (t - 1) % 2
                if inside(k, NS):
                    wait(act, s.pr, k + 1)
                    wait(act, s.inp, k - 1)
                    wait(act, s.a, k - 1)
                    act.activation(th[:, q, 2, :, :], pG[q][:, 2, :, :], ACT.Tanh, bias=m.half_b[:, 1:2], scale=0.5).then_inc(s.thd, 1)
                    act.activation(th[:, q, 0, :, :], pG[q][:, 0, :, :], ACT.Tanh, bias=m.half_b[:, 0:1], scale=0.5)
                    act.activation(th[:, q, 1, :, :], pG[q][:, 1, :, :], ACT.Tanh, bias=m.vec[:, BV:BV + 1]).then_inc(s.th, 1)

        @block.gpsimd
        def _(pool):
            for t in range(LS):
                q = t % 2
                wait(pool, l.yc, t + 1)
                wait(pool, l.res, t - 1)
                pool.tensor_tensor(yb[:, q, :, :], y16[:, q, :, :], m.ffn_bias[:, :].unsqueeze(1).broadcast_to([128, LG, 128]),
                                   ALU.add).then_inc(l.yb, 1)

            for k in range(NS):
                wait(pool, s.thd, k + 1)
                wait(pool, s.h, k - 1)
                pool.tensor_scalar(a[:, k % 2, :, :], th[:, k % 2, 2, :, :], 0.499, 0.5, ALU.mult, ALU.add).then_inc(s.a, 1)

        @block.vector
        def _(dve):
            def scan_rows(t):
                wait(dve, s.xt, t - 1)
                for i in range(G):
                    ins = normalise(dve, m, xn[:, t % 2, i, :], G * t + i)
                ins.then_inc(s.xn, 1)

            for t in range(LS + 2):
                if t == LS:
                    dve.wait_ge(l.stats, B // 2)
                    row_scale(dve, m, 0, B // 2)
                    scan_rows(0)
                    scan_rows(1)
                if t < LS:
                    wait(dve, l.xb, t - 1)
                    for i in range(LG):
                        ins = normalise(dve, m, x8[:, t % 2, i, :], LG * t + i, saturate=False)
                    ins.then_inc(l.x8, 1)
                if t == 2:
                    row_scale(dve, m, AHEAD, B)
                if t >= 2:
                    k, rows = t - 2, slice(LG * (t - 2), LG * (t - 1))
                    wait(dve, l.yb, k + 1)
                    dve.tensor_tensor(m.x[:, rows, :], m.x[:, rows, :], yb[:, k % 2, :, :], ALU.add).then_inc(l.res, 1)
                    wait(dve, l.res, k + 1)
                    for i in range(LG):
                        row_stats(dve, m, l.stats, LG * k + i)

            for t in range(2, NS + 3):
                if t == NS:
                    dve.wait_ge(s.stats, B // 2)
                    row_scale(dve, m, 0, B // 2)
                if t < NS:
                    scan_rows(t)
                if t == 2:
                    dve.wait_ge(l.stats, B)
                    row_scale(dve, m, B // 2, B)
                k, q = t - 2, t % 2
                if inside(k, NS):
                    wait(dve, s.th, k + 1)
                    wait(dve, s.h, k - 1)
                    dve.scalar_tensor_tensor(out=inp[:, q, :, :], in0=th[:, q, 0, :, :], scalar=1.0, in1=th[:, q, 1, :, :],
                                             op0=ALU.add, op1=ALU.mult).then_inc(s.inp, 1)
                    wait(dve, s.inp, k + 1)
                    wait(dve, s.a, k + 1)
                    wait(dve, s.ht, k - 1)
                    for i in range(G):
                        ins = dve.tensor_tensor_scan(h[:, q, i, :], a[:, q, i, :], inp[:, q, i, :], 0.0, ALU.mult, ALU.add)
                    ins.then_inc(s.h, 1)
                k = t - 3
                if inside(k, NS):
                    wait(dve, s.ht, k + 1)
                    rows = slice(G * k, G * k + G)
                    dve.scalar_tensor_tensor(out=m.x[:, rows, :], in0=pH[k % 2][:, 0:G, :], scalar=0.5, in1=m.x[:, rows, :],
                                             op0=ALU.mult, op1=ALU.add).then_inc(s.res, 1)
                    wait(dve, s.res, k + 1)
                    for i in range(G):
                        row_stats(dve, m, s.stats, G * k + i)
            dve.wait_ge(s.stats, B)


def route(nc, ctx, m, d):
    s = Sems(nc, ctx, "rt", "xn xt xtc lg lt mc md exc exd rd dn dt dtc sl slc rs")
    with ExitStack() as tmp, nc.Block() as block:
        sb = lambda n, sh, dt=F32: tmp.enter_context(nc.sbuf_tensor(f"rt_{n}", sh, dt))
        pb = lambda n: tmp.enter_context(nc.psum_tensor(f"rt_{n}", [128, 4, 128], F32))
        xn, xnT, xkeep = sb("xn", [128, 2, 128]), sb("xnT", [128, 2, 128]), sb("xkeep", [128, 2, 128])
        disp, dispT = sb("disp", [128, 2, ES]), sb("dispT", [128, 2, 4, 128])
        mc, md = sb("mc", [128, 2]), sb("md", [128, 2, 4])
        sd, rd = sb("sd", [128, 2, 4]), sb("rd", [128, 2, 4])
        pX, pL, pLT, pD, pSl = pb("pX"), [pb("pL0"), pb("pL1")], [pb("pLT0"), pb("pLT1")], pb("pD"), pb("pSl")
        flat = lambda x: x[:, :, :].rearrange("p a b -> p (a b)")
        N, LO, HI = B + 3, 6, 16

        @block.sync
        def _(sp):
            sp.dma_start(m.b2[:, :, :], d.L1_ffn_b2.partition_broadcast(128)).then_inc(m.s_b2, 16)
            for e in range(2):
                load_expert(sp, m, d, e, e)

        @block.tensor
        def _(pe):
            def body(t, p):
                b, q = t - 1, (p + 1) % 2
                if valid(t - 3):
                    wait(pe, s.dn, t - 2)
                    wait(pe, s.dtc, t - 3)
                    for c in range(4):
                        ins = pe.transpose(pD[:, c, :], dispT[:, q, c, :], m.ident[:, :])
                    ins.then_inc(s.dt, 1)
                if valid(b):
                    wait(pe, s.xtc, b + 1)
                    wait(pe, s.exd, b - 1)
                    for c in range(4):
                        ins = pe.matmul(pLT[q][:, c, :], m.snT[:, 128 * c:128 * c + 128], xnT[:, q, :], start=True, stop=True)
                    ins.then_inc(s.lt, 1)
                if valid(t):
                    wait(pe, s.xn, t + 1)
                    pe.transpose(pX[:, 0, :], xn[:, p, :], m.ident[:, :]).then_inc(s.xt, 1)
                if valid(b):
                    wait(pe, s.exc, b - 1)
                    pe.matmul(flat(pL[q]), xnT[:, q, :], m.snT[:, :], start=True, stop=True).then_inc(s.lg, 1)
                if valid(t - 3):
                    wait(pe, s.dtc, t - 2)
                    wait(pe, s.rs, t - 2)
                    wait(pe, s.slc, t - 3)
                    pe.matmul(flat(pSl), xkeep[:, q, :], disp[:, q, :], start=True, stop=True).then_inc(s.sl, 1)
            walk(pe, N, LO, HI, body)

        @block.vector
        def _(dve):
            def body(t, p):
                b, q = t - 1, (p + 1) % 2
                if valid(t):
                    wait(dve, s.xt, t - 1)
                    wait(dve, s.rs, t - 1)
                    normalise(dve, m, xn[:, p, :], t).then_inc(s.xn, 1)
                if valid(b):
                    wait(dve, s.lt, b + 1)
                    wait(dve, s.exd, b - 1)
                    dve.tensor_reduce(md[:, q, :], pLT[q][:, :, :], AX.X, ALU.max, negate=True).then_inc(s.md, 1)
                    wait(dve, s.lg, b + 1)
                    wait(dve, s.exc, b - 1)
                    dve.tensor_reduce(mc[:, q:q + 1], flat(pL[q]), AX.X, ALU.max, negate=True).then_inc(s.mc, 1)
                    if isinstance(t, int) and t < LO:
                        for step in range(max(0, 2 * t - 3), min(RMS_STEPS, 2 * t - 1)):
                            scale_step(dve, m, AHEAD, B, step, rms=True)
                    wait(dve, s.exd, b + 1)
                    wait(dve, s.dn, b - 1)
                    dve.reciprocal(rd[:, q, :], sd[:, q, :]).then_inc(s.rd, 1)
                if valid(t - 3):
                    wait(dve, s.sl, t - 2)
                    dve.tensor_scalar(m.slotsT[:, :, t - 3, :], flat(pSl).rearrange("p (e s) -> p e s", e=E),
                                      m.vec[:, GAMMA:GAMMA + 1], None, ALU.mult).then_inc(s.slc, 1)
                if valid(b):
                    wait(dve, s.xn, b + 1)
                    dve.tensor_copy(xkeep[:, q, :], xn[:, q, :]).then_inc(s.rs, 1)
            walk(dve, N, LO, HI, body)
            dve.wait_ge(s.slc, B)

        @block.gpsimd
        def _(pool):
            def body(t, p):
                q = p
                if valid(t):
                    wait(pool, s.rd, t + 1)
                    pool.tensor_tensor(dispT[:, q, :, :], dispT[:, q, :, :], rd[:, q, :].unsqueeze(2).broadcast_to([128, 4, 128]),
                                       ALU.mult).then_inc(s.dn, 1)
            walk(pool, B, LO, HI, body)

        @block.scalar
        def _(act):
            def body(t, p):
                b, q = t - 1, (p + 1) % 2
                if valid(t - 3):
                    wait(act, s.dt, t - 2)
                    wait(act, s.sl, t - 4)
                    act.activation(disp[:, q, :], flat(pD), ACT.Copy).then_inc(s.dtc, 1)
                if valid(b):
                    wait(act, s.mc, b)
                    wait(act, s.md, b + 1)
                    wait(act, s.dt, b - 1)
                    for c in range(4):
                        ins = act.activation(dispT[:, q, c, :], pLT[q][:, c, :], ACT.Exp, bias=md[:, q, c:c + 1],
                                             accum_out=sd[:, q, c:c + 1])
                    ins.then_inc(s.exd, 1)
                elif valid(t - 2):
                    act.wait_ge(s.mc, B)
                if valid(t):
                    wait(act, s.xt, t + 1)
                    wait(act, s.lg, t - 1)
                    act.activation(xnT[:, p, :], pX[:, 0, :], ACT.Copy).then_inc(s.xtc, 1)
                if valid(t - 2):
                    act.activation(m.comb[:, t - 2, :], flat(pL[p]), ACT.Exp, bias=mc[:, p:p + 1],
                                   accum_out=m.comb_sum[:, bass.ds(t - 2, 1)]).then_inc(s.exc, 1)
            walk(act, N, LO, HI, body)
            act.wait_ge(s.exc, B)


def load_expert(sp, m, d, e, q, first=True, second=True):
    if first:
        sp.dma_start(m.w1[:, q, :], d.L1_ffn_w1[e]).then_inc(m.s_w1[q], 16)
    if second:
        sp.dma_start(m.w2[:, q, :, :], d.L1_ffn_w2[e].rearrange("(c p) f -> p c f", p=128)).then_inc(m.s_w2[q], 16)


def experts(nc, ctx, m, d):
    s = Sems(nc, ctx, "ex", "h hc eo eoc b1")
    NS = B * SL
    NQ = B // 2
    with ExitStack() as tmp, nc.Block() as block:
        sb = lambda n, sh, dt=F32: tmp.enter_context(nc.sbuf_tensor(f"ex_{n}", sh, dt))
        w1, w2, b2 = m.w1, m.w2, m.b2
        b1 = sb("b1", [128, 2, NHC])
        hT = sb("hT", [128, 2, NHC, NS])
        pH = [tmp.enter_context(nc.psum_tensor(f"ex_pH{i}", [128, 512], F32)) for i in range(4)]
        pE = [tmp.enter_context(nc.psum_tensor(f"ex_pE{i}", [128, 4, 128], F32)) for i in range(2)]
        w1s, w2s = m.s_w1, m.s_w2

        def run(eng, body):
            body(0, 0, None)
            body(1, 1, 0)
            with eng.Fori(1, E // 2) as r:
                body(2 * r, 0, r - 1)
                body(2 * r + 1, 1, r)
            body(E, 0, E // 2 - 1)


        @block.sync
        def _(sp):
            with sp.Fori(1, E // 2) as r:
                for q in range(2):
                    e = 2 * r + q
                    sp.wait_ge(s.h, 8 * (e - 1))
                    load_expert(sp, m, d, e, q, second=False)
                    sp.wait_ge(s.eo, 2 * (e - 1))
                    load_expert(sp, m, d, e, q, first=False)

        @block.tensor
        def _(pe):
            def body(e, q, pair):
                if inside(e, E):
                    wait(pe, w1s[q], 8 * (e - q) + 16)
                    for c in range(NHC):
                        for k in range(2):
                            n = 2 * c + k
                            wait(pe, s.hc, 8 * e + n - 3)
                            pe.matmul(pH[n % 4][:, :], w1[:, q, 128 * c:128 * c + 128],
                                      m.slotsT[:, e, 8 * k:8 * k + 8, :], start=True, stop=True).then_inc(s.h, 1)
                e1, q1 = e - 1, (q + 1) % 2
                if inside(e1, E):
                    wait(pe, w2s[q1], 8 * (e1 - q1) + 16)
                    wait(pe, s.hc, 8 * e1 + 8)
                    for r in range(2):
                        wait(pe, s.eoc, 2 * e1 + r - 1)
                        for j in range(4):
                            k = 4 * r + j
                            for c in range(NHC):
                                ins = pe.matmul(pE[r][:, j, :], hT[:, q1, c, 128 * k:128 * k + 128], w2[:, q1, c, :],
                                                start=c == 0, stop=c == NHC - 1)
                        ins.then_inc(s.eo, 1)
            run(pe, body)

        @block.scalar
        def _(act):
            def body(e, q, pair):
                if inside(e, E):
                    wait(act, s.eo, 2 * (e - 1))
                    wait(act, s.b1, e + 1)
                    for c in range(NHC):
                        for k in range(2):
                            n = 2 * c + k
                            wait(act, s.h, 8 * e + n + 1)
                            act.activation(hT[:, q, c, 512 * k:512 * k + 512], pH[n % 4][:, :], ACT.Gelu,
                                           bias=b1[:, q, c:c + 1]).then_inc(s.hc, 1)
            run(act, body)

        @block.vector
        def _(dve):
            dve.wait_ge(m.s_b2, 16)

            def body(e, q, pair):
                if inside(e, E):
                    wait(dve, s.hc, 8 * (e - 1))
                    dve.tensor_copy(b1[:, q, :], m.b1[:, e, :]).then_inc(s.b1, 1)
                e1, q1 = e - 1, (q + 1) % 2
                if inside(e1, E):
                    for r in range(2):
                        wait(dve, s.eo, 2 * e1 + r + 1)
                        for i in range(2):
                            rows, own = slice(SL * i, SL * i + SL), slice(SL * q1, SL * q1 + SL)
                            ins = dve.tensor_tensor(m.eo[own, pair, r, :, i, :], pE[r][rows, :, :],
                                                    b2[rows, e1, :].unsqueeze(1).broadcast_to([SL, 4, 128]), ALU.add)
                        ins.then_inc(s.eoc, 1)
            run(dve, body)
            dve.wait_ge(s.eoc, 2 * E)


def combine(nc, ctx, m, out):
    s = Sems(nc, ctx, "cb", "rc ct ctc y res out")
    NC = ES // 128
    with ExitStack() as tmp, nc.Block() as block:
        sb = lambda n, sh, dt=F32: tmp.enter_context(nc.sbuf_tensor(f"cb_{n}", sh, dt))
        pb = lambda n: tmp.enter_context(nc.psum_tensor(f"cb_{n}", [128, 4, 128], F32))
        combT = sb("combT", [128, 2, NC, 128])
        rc = sb("rc", [128, B])
        res = sb("res", [128, B, 128])
        pC, pY = [pb(f"pC{i}") for i in range(4)], [pb(f"pY{i}") for i in range(4)]

        @block.tensor
        def _(pe):
            for t in range(B + 2):
                if t < B:
                    wait(pe, s.ctc, t - 3)
                    for c in range(NC):
                        ins = pe.transpose(pC[t % 4][:, c, :], m.comb[:, t, 128 * c:128 * c + 128], m.ident[:, :])
                    ins.then_inc(s.ct, 1)
                b = t - 2
                if b >= 0:
                    wait(pe, s.ctc, b + 1)
                    wait(pe, s.res, b - 3)
                    for c in range(NC):
                        ins = pe.matmul(pY[b % 4][:, 0, :], combT[:, b % 2, c, :], m.eo[:, c, b // 8, b // 2 % 4, b % 2, :],
                                        start=c == 0, stop=c == NC - 1)
                    ins.then_inc(s.y, 1)

        @block.scalar
        def _(act):
            for b in range(B):
                act.wait_ge(s.ct, b + 1)
                wait(act, s.y, b - 1)
                act.activation(combT[:, b % 2, :, :], pC[b % 4][:, :, :], ACT.Copy).then_inc(s.ctc, 1)

        @block.vector
        def _(dve):
            dve.reciprocal(rc[:, :], m.comb_sum[:, :]).then_inc(s.rc, 1)
            dve.wait_ge(s.rc, 1)
            for b in range(B):
                dve.wait_ge(s.y, b + 1)
                dve.scalar_tensor_tensor(out=res[:, b, :], in0=pY[b % 4][:, 0, :], scalar=rc[:, b:b + 1], in1=m.x[:, b, :],
                                         op0=ALU.mult, op1=ALU.add).then_inc(s.res, 1)

        @block.sync
        def _(sp):
            for k in range(4):
                sp.wait_ge(s.res, 4 * k + 4)
                sp.dma_start(out[4 * k:4 * k + 4].rearrange("b t f -> t b f"), res[:, 4 * k:4 * k + 4, :]).then_inc(s.out, 16)
            sp.wait_ge(s.out, 64)


def decoder_program(nc, d, out):
    ctx = ExitStack()
    with ctx:
        m = Memory()
        sb = lambda n, sh, dt=F32: ctx.enter_context(nc.sbuf_tensor(n, sh, dt))
        sem = lambda n: ctx.enter_context(nc.semaphore(n))
        m.x = sb("x", [128, B, 128])
        m.mv, m.bn = sb("mv", [128, B, 2]), sb("bn", [128, B, 6])
        m.rstd, m.veps, m.tmp16, m.ssq = sb("rstd", [128, B]), sb("veps", [128, B]), sb("tmp16", [128, B]), sb("ssq", [128, B])
        m.ident, m.ident16, m.ones = sb("ident_s", [128, 128]), sb("ident16", [128, 128], BF16), sb("ones", [128, 4 * C2])
        m.vec = sb("vec", [128, N_ROWS + E * NHC])
        m.b1 = m.vec[:, B1:].rearrange("p (e c) -> p e c", c=NHC)
        m.scrap = sb("scrap", [128, 1])
        m.half_b, m.gg = sb("half_b", [128, 3]), sb("gg", [128, 1])
        m.snT = sb("snT", [128, ES])
        m.ffn_wT, m.ffn_bias = sb("ffn_wT", [128, 128], BF16), sb("ffn_bias", [128, 128])
        m.wg, m.wvs, m.wd = sb("wg", [128, 128]), sb("wvs", [128, 128]), sb("wd", [128, 128])
        m.wq1, m.wv1, m.wo1 = sb("wq1", [128, 128]), sb("wv1", [128, 128]), sb("wo1", [128, 128])
        m.bv1, m.bo1 = sb("bv1", [1, 128]), sb("bo1", [1, 128])
        m.s_first, m.s_rest, m.s_causal, m.s_link = sem("first_weights"), sem("rest"), sem("causal"), sem("link")
        m.s_x, m.s_first_stats = [sem(f"x{g}") for g in range(4)], sem("first_stats")
        m.link_count, m.all_rest = [0], 0
        with ExitStack() as attn:
            sa = lambda n, sh, dt=F32: attn.enter_context(nc.sbuf_tensor(n, sh, dt))
            m.ck = sa("ck", [128, B, 2, C2])
            m.headmask = sa("headmask_s", [128, H])
            with ExitStack() as first:
                sf = lambda n, sh, dt=F32: first.enter_context(nc.sbuf_tensor(n, sh, dt))
                m.wqk, m.rope = sf("wqk", [128, 4, 128]), sf("rope_s", [128, 2, 2, 128])
                m.wv0, m.wo0 = sf("wv0", [128, 128]), sf("wo0", [128, 128])
                m.causal, m.xmask = sf("causal", [128, HG, 128], BF16), sf("xmask", [128, HG, C2], BF16)
                m.kT_wide = sf("kT_wide", [128, B, NCH, C2])
                m.wq_wide, m.wv_wide = sf("wq_wide", [128, H * HD]), sf("wv_wide", [128, H * HD])
                m.wo_wide = sf("wo_wide", [128, NCH, 128])
                m.kblk = sf("kblk", [128, 2, NCH, 2, C2])
                m.vx_wide, m.prob_wide = sf("vx_wide", [128, 2, H * HD]), sf("prob_wide", [128, 2, HG, 128])
                with ExitStack() as raw:
                    sr = lambda n, sh, dt=F32: raw.enter_context(nc.sbuf_tensor(n, sh, dt))
                    m.ctx_raw = sr("ctx_raw", [C2, B, D])
                    m.vec_rows = sr("vec_rows", [N_ROWS + E * NHC, 128])
                    m.w_raw, m.mask8 = sr("ffn_w_raw", [128, 128]), sr("mask8", [128, C2], U8)
                    m.wk_wide, m.wk_narrow, m.bk_row = sr("wk_wide", [128, H * HD]), sr("wk_narrow", [128, 128]), sr("bk_row", [1, 128])
                    m.slots = sr("slots", [128, 4, 128])
                    loads = load_block(nc, ctx, m, d)
                    narrow_attention(nc, ctx, m, "self", S, False, loads)
                    keys_block(nc, ctx, m)
                wide_attention(nc, ctx, m)
            linear_and_scan(nc, ctx, m)
            narrow_attention(nc, ctx, m, "cross", C2, True)
        m.comb, m.comb_sum = sb("comb", [128, B, ES]), sb("comb_sum", [128, B])
        m.slotsT = sb("slotsT", [128, E, B, SL])
        m.w1, m.w2, m.b2 = sb("w1", [128, 2, HID]), sb("w2", [128, 2, NHC, 128]), sb("b2", [128, E, 128])
        m.s_w1, m.s_w2, m.s_b2 = [sem("w1a"), sem("w1b")], [sem("w2a"), sem("w2b")], sem("b2")
        route(nc, ctx, m, d)
        m.eo = sb("eo", [128, E // 2, 2, 4, 2, 128])
        experts(nc, ctx, m, d)
        combine(nc, ctx, m, out)


def shape_constants():
    inv = (1.0 / np.float32(10000.0) ** (np.arange(0, DK, 2, dtype=np.float32) / np.float32(DK))).astype(np.float32)
    theta = (np.arange(S, dtype=np.float32)[:, None] * inv[None, :]).astype(np.float32)
    cos = np.repeat(np.cos(theta), 2, axis=-1).T
    sin = np.repeat(np.sin(theta), 2, axis=-1).T
    scale = np.float32(1.0) / np.sqrt(np.float32(DK))
    rope = np.empty((D, 2, 2, S), np.float32)
    for i, table in enumerate((cos, sin)):
        rope[:, i, 0] = np.tile(table, (H, 1)) * scale
        rope[:, i, 1] = np.tile(table, (H, 1))
    headmask = np.arange(D)[:, None] // DK == np.arange(H)[None, :]
    return {"ident": np.eye(128, dtype=np.float32), "rope": rope, "headmask": headmask.astype(np.float32)}


_INS = ["x", "ctx_1024", "mask_SxS2_bk1", "L0_attn_Wq", "L0_attn_Wk", "L0_attn_Wv", "L0_attn_Wo", "L0_xattn_W_q",
        "L0_xattn_W_k", "L0_xattn_W_v", "L0_xattn_W_o", "L0_ffn_weight", "L0_ffn_bias", "L1_attn_Wg", "L1_attn_bg",
        "L1_attn_Wv", "L1_attn_bv", "L1_attn_Wd", "L1_attn_bd", "L1_xattn_Wq", "L1_xattn_bq", "L1_xattn_Wk",
        "L1_xattn_bk", "L1_xattn_Wv", "L1_xattn_bv", "L1_xattn_Wo", "L1_xattn_bo", "L1_ffn_norm_gamma",
        "L1_ffn_slot_norm_gamma", "L1_ffn_slot_embeds", "L1_ffn_w1", "L1_ffn_b1", "L1_ffn_w2", "L1_ffn_b2"]


def kernel(**inputs):
    import concourse.bacc as _bacc
    from concourse.bass_utils import run_bass_kernel_spmd as _run

    nc = _bacc.Bacc("TRN2", target_bir_lowering=False, num_devices=1)
    arrays, aps = {}, {}
    consts = shape_constants()
    for name in _INS + sorted(consts):
        a = np.ascontiguousarray(consts[name] if name in consts else inputs[name])
        arrays[f"in_{name}_dram"] = a
        dtype = U8 if a.dtype == np.bool_ else mybir.dt.from_np(a.dtype)
        aps[name] = nc.dram_tensor(f"in_{name}_dram", a.shape, dtype, kind="ExternalInput").ap()
    out = nc.dram_tensor("out_0_dram", (B, S, D), F32, kind="ExternalOutput").ap()
    decoder_program(nc, namedtuple("Inputs", sorted(aps))(**aps), out)
    r = _run(nc, [arrays], core_ids=[0])
    return r.results[0]["out_0_dram"]
```
